# Optimizing a Trainium2 kernel written in Bass

```python
import numpy as np
import jax
import jax.numpy as jnp

def _softmax(x, axis=-1):
    return jax.nn.softmax(x, axis=axis)

def _gelu(x):
    return jax.nn.gelu(x, approximate=True)

def _silu(x):
    return jax.nn.silu(x)

def _sigmoid(x):
    return jax.nn.sigmoid(x)

def _layernorm(x, axis=-1, eps=1e-05):
    m = jnp.mean(x, axis=axis, keepdims=True)
    v = jnp.var(x, axis=axis, keepdims=True)
    return (x - m) / jnp.sqrt(v + eps)

def _scatter_add(tgt, idx, src, axis=0):
    return tgt.at[idx].add(src)

def _segment_sum(src, seg, n):
    return jax.ops.segment_sum(src, seg, n)
kernel_name = 'mk_gps_d1_gnn_r8_3be802'

def setup_inputs(seed: int=0):
    np.random.seed(seed)
    _w = jnp.asarray

    def _rec_inputs():
        import jax
        import jax.numpy as jnp
        _gk = jax.random.key(seed)
        x = -0.0003019 + 1 * jax.random.normal(jax.random.fold_in(_gk, 1), (1250, 1024), jnp.float32)
        _s = jax.random.randint(jax.random.fold_in(_gk, 2), (20000,), 0, 1250, jnp.int32)
        _d = jax.random.randint(jax.random.fold_in(_gk, 3), (20000,), 0, 1250, jnp.int32)
        _loop = jnp.arange(1250, dtype=jnp.int32)
        src = jnp.concatenate([_s, _d, _loop])
        dst = jnp.concatenate([_d, _s, _loop])
        _o = jnp.argsort(dst, stable=True)
        src = src[_o]
        dst = dst[_o]
        return (x, src, dst)
    x, src, dst = _rec_inputs()

    def _L0_gnn_setup():
        import jax, jax.numpy as jnp
        import numpy as np
        N = 2500
        E = 40000
        IN = 1024
        HID = 256
        H = 4
        D = HID // H
        OUT = 1024
        EPS = 1e-06
        NEG_SLOPE = 0.2
        key = jax.random.key(seed)
        ks = jax.random.split(key, 8)
        x = jax.random.normal(ks[0], (N, IN), dtype=jnp.float32)
        edge_index = jax.random.randint(ks[1], (2, E), 0, N, dtype=jnp.int64)
        s = 0.02
        return {'x': x, 'edge_index': edge_index, 'rms_w': jnp.ones((IN,), dtype=jnp.float32), 'W_down': jax.random.normal(ks[2], (IN, HID), dtype=jnp.float32) * s, 'Wl': jax.random.normal(ks[3], (HID, HID), dtype=jnp.float32) * s, 'Wr': jax.random.normal(ks[4], (HID, HID), dtype=jnp.float32) * s, 'att': jax.random.normal(ks[5], (H, D), dtype=jnp.float32) * s, 'W_up': jax.random.normal(ks[6], (HID, OUT), dtype=jnp.float32) * s}
    _L0_gnn_all = _L0_gnn_setup()
    _L0_gnn_in = {k: v for k, v in _L0_gnn_all.items() if k in ('rms_w', 'W_down', 'Wl', 'Wr', 'att', 'W_up')}
    del _L0_gnn_all

    def _L0_mix_setup():
        import jax, jax.numpy as jnp
        import numpy as np
        EPS = 1e-12

        def _l2norm(t):
            n = jnp.linalg.norm(t, axis=-1, keepdims=True)
            return t / jnp.maximum(n, EPS)
        key = jax.random.key(seed)
        kx, kq, kk, kv = jax.random.split(key, 4)
        B, N, D = (8, 512, 1024)
        s = 1.0 / np.sqrt(D)
        return {'x': jax.random.normal(kx, (B, N, D), dtype=jnp.float32), 'W_q': jax.random.normal(kq, (D, D), dtype=jnp.float32) * s, 'W_k': jax.random.normal(kk, (D, D), dtype=jnp.float32) * s, 'W_v': jax.random.normal(kv, (D, D), dtype=jnp.float32) * s}
    _L0_mix_all = _L0_mix_setup()
    _L0_mix_in = {k: v for k, v in _L0_mix_all.items() if k in ('W_q', 'W_k', 'W_v')}
    del _L0_mix_all

    def _L0_ffn_setup():
        import jax, jax.numpy as jnp
        import numpy as np
        D_MODEL = 1024
        HIDDEN = 512
        N_ROUTING = 2
        key = jax.random.key(seed)
        ks = jax.random.split(key, 10)
        s = 0.02
        x = jax.random.normal(ks[0], (4, 512, D_MODEL), dtype=jnp.float32)
        gate_w = jax.random.normal(ks[1], (N_ROUTING, D_MODEL), dtype=jnp.float32) * s
        w1 = jax.random.normal(ks[2], (N_ROUTING, D_MODEL, HIDDEN), dtype=jnp.float32) * s
        b1 = jax.random.normal(ks[3], (N_ROUTING, HIDDEN), dtype=jnp.float32) * s
        w2 = jax.random.normal(ks[4], (N_ROUTING, HIDDEN, D_MODEL), dtype=jnp.float32) * s
        b2 = jax.random.normal(ks[5], (N_ROUTING, D_MODEL), dtype=jnp.float32) * s
        sw1 = jax.random.normal(ks[6], (D_MODEL, HIDDEN), dtype=jnp.float32) * s
        sb1 = jax.random.normal(ks[7], (HIDDEN,), dtype=jnp.float32) * s
        sw2 = jax.random.normal(ks[8], (HIDDEN, D_MODEL), dtype=jnp.float32) * s
        sb2 = jax.random.normal(ks[9], (D_MODEL,), dtype=jnp.float32) * s
        return {'x': x, 'gate_w': gate_w, 'w1': w1, 'b1': b1, 'w2': w2, 'b2': b2, 'sw1': sw1, 'sb1': sb1, 'sw2': sw2, 'sb2': sb2}
    _L0_ffn_all = _L0_ffn_setup()
    _L0_ffn_in = {k: v for k, v in _L0_ffn_all.items() if k in ('gate_w', 'w1', 'b1', 'w2', 'b2', 'sw1', 'sb1', 'sw2', 'sb2')}
    del _L0_ffn_all
    return {'x': x, 'src': src, 'dst': dst, 'L0_gnn_rms_w': _L0_gnn_in['rms_w'], 'L0_gnn_W_down': _L0_gnn_in['W_down'], 'L0_gnn_Wl': _L0_gnn_in['Wl'], 'L0_gnn_Wr': _L0_gnn_in['Wr'], 'L0_gnn_att': _L0_gnn_in['att'], 'L0_gnn_W_up': _L0_gnn_in['W_up'], 'L0_mix_W_q': _L0_mix_in['W_q'], 'L0_mix_W_k': _L0_mix_in['W_k'], 'L0_mix_W_v': _L0_mix_in['W_v'], 'L0_ffn_gate_w': _L0_ffn_in['gate_w'], 'L0_ffn_w1': _L0_ffn_in['w1'], 'L0_ffn_b1': _L0_ffn_in['b1'], 'L0_ffn_w2': _L0_ffn_in['w2'], 'L0_ffn_b2': _L0_ffn_in['b2'], 'L0_ffn_sw1': _L0_ffn_in['sw1'], 'L0_ffn_sb1': _L0_ffn_in['sb1'], 'L0_ffn_sw2': _L0_ffn_in['sw2'], 'L0_ffn_sb2': _L0_ffn_in['sb2']}

def reference(x, src, dst, L0_gnn_rms_w, L0_gnn_W_down, L0_gnn_Wl, L0_gnn_Wr, L0_gnn_att, L0_gnn_W_up, L0_mix_W_q, L0_mix_W_k, L0_mix_W_v, L0_ffn_gate_w, L0_ffn_w1, L0_ffn_b1, L0_ffn_w2, L0_ffn_b2, L0_ffn_sw1, L0_ffn_sb1, L0_ffn_sw2, L0_ffn_sb2):
    import jax
    import jax.numpy as jnp

    def _L0_gnn_ref(x, edge_index, rms_w, W_down, Wl, Wr, att, W_up):
        import jax, jax.numpy as jnp
        import numpy as np
        N = 2500
        E = 40000
        IN = 1024
        HID = 256
        H = 4
        D = HID // H
        OUT = 1024
        EPS = 1e-06
        NEG_SLOPE = 0.2
        n = x.shape[0]
        ms = jnp.mean(jnp.square(x), axis=-1, keepdims=True)
        x = x * jax.lax.rsqrt(ms + EPS) * rms_w
        x = x @ W_down
        loop = jnp.arange(n, dtype=edge_index.dtype)
        src = jnp.concatenate([edge_index[0], loop])
        dst = jnp.concatenate([edge_index[1], loop])
        xl = (x @ Wl).reshape(n, H, D)
        xr = (x @ Wr).reshape(n, H, D)
        msg = xl[src] + xr[dst]
        act = jnp.where(msg > 0, msg, NEG_SLOPE * msg)
        e = jnp.einsum('ehd,hd->eh', act, att)
        m = jax.ops.segment_max(e, dst, num_segments=n)
        p = jnp.exp(e - m[dst])
        denom = jax.ops.segment_sum(p, dst, num_segments=n)
        alpha = p / (denom[dst] + 1e-16)
        out = jax.ops.segment_sum(alpha[..., None] * xl[src], dst, num_segments=n)
        out = out.reshape(n, HID)
        return out @ W_up

    def _L0_mix_ref(x, W_q, W_k, W_v):
        import jax, jax.numpy as jnp
        import numpy as np
        EPS = 1e-12

        def _l2norm(t):
            n = jnp.linalg.norm(t, axis=-1, keepdims=True)
            return t / jnp.maximum(n, EPS)
        Q = _l2norm(jnp.einsum('bnd,ed->bne', x, W_q))
        K = _l2norm(jnp.einsum('bnd,ed->bne', x, W_k))
        V = jnp.einsum('bnd,ed->bne', x, W_v)
        C = x.shape[1]
        global_feat = jnp.sum(K * V, axis=1, keepdims=True) / C
        return Q * global_feat

    def _L0_ffn_ref(x, gate_w, w1, b1, w2, b2, sw1, sb1, sw2, sb2):
        import jax, jax.numpy as jnp
        import numpy as np
        D_MODEL = 1024
        HIDDEN = 512
        N_ROUTING = 2
        B, S, D = x.shape
        xf = x.reshape(-1, D)
        gate_scores = xf @ gate_w.T
        gate_probs = jax.nn.softmax(gate_scores, axis=-1)
        top1 = jnp.argmax(gate_probs, axis=-1)
        one_hot = jax.nn.one_hot(top1, N_ROUTING, dtype=xf.dtype)
        masked = xf[None, :, :] * one_hot.T[:, :, None]
        h = jax.nn.relu(jnp.einsum('end,edh->enh', masked, w1) + b1[:, None, :])
        expert_out = jnp.einsum('enh,ehd->end', h, w2) + b2[:, None, :]
        routing_output = expert_out.sum(axis=0)
        shared = jax.nn.relu(xf @ sw1 + sb1) @ sw2 + sb2
        return (routing_output + shared).reshape(B, S, D)
    edge_index = jnp.stack([src, dst])
    xn = _layernorm(x, axis=-1)
    x = x + _L0_gnn_ref(xn, edge_index, L0_gnn_rms_w, L0_gnn_W_down, L0_gnn_Wl, L0_gnn_Wr, L0_gnn_att, L0_gnn_W_up) + _L0_mix_ref(xn[None], L0_mix_W_q, L0_mix_W_k, L0_mix_W_v)[0]
    x = x + _L0_ffn_ref(_layernorm(x, axis=-1)[None], L0_ffn_gate_w, L0_ffn_w1, L0_ffn_b1, L0_ffn_w2, L0_ffn_b2, L0_ffn_sw1, L0_ffn_sb1, L0_ffn_sw2, L0_ffn_sb2)[0]
    return x

_drawn_inputs = setup_inputs


def setup_inputs(seed=0):
    import zlib

    import numpy as np

    out = dict(_drawn_inputs(seed))
    spreads = {'L0_gnn_rms_w': (1.0, 0.6)}
    factors = {'L0_gnn_Wr': 32.047,
     'L0_gnn_att': 28.389,
     'L0_mix_W_q': 64.0,
     'L0_mix_W_k': 64.0,
     'L0_mix_W_v': 63.897,
     'L0_ffn_b1': 7.959,
     'L0_ffn_sb1': 8.0,
     'L0_ffn_sb2': 2.969}
    for name, (base, spread) in spreads.items():
        noise = np.random.default_rng([zlib.crc32(name.encode()), seed]).standard_normal(out[name].shape)
        drawn = base * np.exp(spread * noise) if base else spread * noise
        out[name] = jnp.asarray(drawn.astype(out[name].dtype))
    for name, factor in factors.items():
        out[name] = (out[name] * factor).astype(out[name].dtype)
    return out
```

```python
import numpy as np
import concourse.bass as bass
from concourse import mybir
from contextlib import ExitStack


f32, i32, bf16 = mybir.dt.float32, mybir.dt.int32, mybir.dt.bfloat16
ALU = mybir.AluOpType
ACT = mybir.ActivationFunctionType
AXX = mybir.AxisListType.X

N, D, HID, H, E = 1250, 1024, 256, 4, 41250
DH = HID // H
PR, T = 125, 10
NB, BR = 5, 250
KD = D // 128
G = 10
BLOCKS = E // G
EP = E // PR
QC = -(-(BLOCKS + N) // 128)
SLOTS = QC + T - 1
ROW = 125
ROWS = E // ROW
FH = 512
XLW, XRW = HID + H, HID + 2 * H
ACT_J = 7
RING = 4
BIG = 1.0e30
RNE = 12582912.0
NEG_SLOPE = 0.2
assert E == BLOCKS * G == PR * EP == ROWS * ROW and EP % G == 0 and QC == NB * KD + 2


class Steps:

    def __init__(self, eng, sem):
        self.eng, self.sem, self.done, self.turn = eng, sem, 0, 0

    def add(self, ins):
        ins.then_inc(self.sem, 1)
        self.done += 1

    def wait(self):
        self.eng.wait_ge(self.sem, self.turn + self.done)

    def link(self, ins):
        self.add(ins)
        self.wait()

    def enter(self, i, per):
        self.start, self.per, self.done = self.done, per, 0
        self.turn = i * per + self.start

    def leave(self, times):
        assert self.done == self.per, (self.done, self.per)
        self.done, self.turn = self.start + times * self.per, 0


def gps_layer(nc, x, src, dst, rms_w, W_down, Wl, Wr, att, W_up, W_q, W_k, W_v,
              gate_w, w1, b1, w2, b2, sw1, sb1, sw2, sb2, out):
    dram = lambda name, shape, dt=f32: nc.dram_tensor(name, shape, dt, kind="Internal").ap()
    edge_tab = dram("edge_tab", (BLOCKS, 2 * G), i32)
    xl_tab = dram("xl_tab", (N, XLW))
    xr_tab = dram("xr_tab", (N, XRW))
    xnT_d = dram("xnT_d", (NB, 128, KD * BR))
    q_d = dram("q_d", (NB, 128, KD * BR))
    o_d = dram("o_d", (QC, 128, HID))
    m_d = dram("m_d", (QC * 128, H))
    n_d = dram("n_d", (QC * 128, 1))
    f_d = dram("f_d", (QC * 128, 9))

    with ExitStack() as ctx:
        sb = lambda name, shape, dt=f32: ctx.enter_context(nc.sbuf_tensor(name, shape, dt))
        sem = lambda name: ctx.enter_context(nc.semaphore(name))

        WT = sb("WT", [128, 3 * KD * D])
        arena = sb("arena", [128, RING * G * XLW + G * HID])
        blk = sb("blk", [128, 6500])
        wraw = sb("wraw", [128, 2, D])

        wt = WT[:, :].rearrange("p (w k e) -> p w k e", w=3, k=KD)
        w1s = WT[:, 0:3 * 4096].rearrange("p (e k h) -> p e k h", e=3, k=KD)
        w2s = WT[:, 3 * 4096:6 * 4096].rearrange("p (e k d) -> p e k d", e=3, k=4)
        def third(a, n):
            return WT[:, 2 * KD * D + a:2 * KD * D + a + n]
        cmp1 = third(0, T * ROWS)[0:PR].rearrange("p (t r) -> p t r", t=T)
        row_i = third(3300, T * ROW)[0:PR].bitcast(i32).rearrange("p (t r) -> p t r", t=T)
        src_sb = third(4550, EP)[0:PR].bitcast(i32)
        dst_sb = third(4880, EP)[0:PR].bitcast(i32)
        tab_sb = third(5210, 2 * EP)[0:PR].bitcast(i32).rearrange("p (b w) -> p b w", w=2 * G)
        stepR = third(5870, 640)[0:PR].bitcast(bf16).rearrange("p (t r) -> p t r", t=T)
        hitA = third(6510, 420)[0:PR].bitcast(bf16).rearrange("p (t q) -> p t q", t=T)
        hitB = third(6930, 420)[0:PR].bitcast(bf16).rearrange("p (t q) -> p t q", t=T)
        heads = third(7350, ROWS)[:, :]
        heads_i = third(7680, ROWS)[0:1].bitcast(i32)
        slot_c = third(0, SLOTS * (T - 1))[0:1].rearrange("p (s t) -> p s t", t=T - 1)
        def second(a, n):
            return WT[:, KD * D + a:KD * D + a + n]
        wd = second(0, 2048).rearrange("p (k h) -> p k h", k=KD)
        wl = second(2048, 512).rearrange("p (k h) -> p k h", k=2)
        wr = second(2560, 512).rearrange("p (k h) -> p k h", k=2)
        xnTb = second(3072, 2000).rearrange("p (k r) -> p k r", k=KD)
        tmpX = second(5072, 2560)[0:PR].rearrange("p (t h) -> p t h", t=T)
        shiftA, shiftB, before = (second(7632 + PR * i, PR)[0:PR] for i in range(3))
        x_all = arena[0:PR, 0:T * D].rearrange("p (t d) -> p t d", t=T)
        XLs = blk[0:PR, 0:T * XLW].rearrange("p (t w) -> p t w", t=T)
        XRs = blk[0:PR, 2600:2600 + T * XRW].rearrange("p (t w) -> p t w", t=T)
        hTb = blk[:, 5240:5740].rearrange("p (k r) -> p k r", k=2)
        XL = arena[:, 0:RING * G * XLW].rearrange("p (r j w) -> p r j w", r=RING, j=G)
        msg = arena[:, RING * G * XLW:].rearrange("p (j f) -> p j f", j=G)
        XB = blk[:, 0:2000].rearrange("p (k r) -> p k r", k=KD)
        KVb = blk[:, 2000:4000].rearrange("p (k r) -> p k r", k=KD)
        Qb = blk[:, 4000:6000].rearrange("p (k r) -> p k r", k=KD)
        RH = arena[:, 0:QC * 265].rearrange("p (q w) -> p q w", q=QC)
        acc = blk[0:PR, 0:T * 265].rearrange("p (t w) -> p t w", t=T)
        RH_END = QC * 265
        def lane(a, *shape):
            n = int(np.prod(shape))
            v = arena[:, RH_END + a:RH_END + a + n]
            return v.rearrange("p (j w) -> p j w", w=shape[1]) if len(shape) == 2 else v
        ML = lane(0, QC, H)
        NL = lane(168, QC)
        PF = lane(210, QC + 1)
        FW = lane(254, QC, H)
        BW = lane(422, QC, H)
        FL = lane(590, QC, 9)
        FG = lane(968, QC, 9)
        ends = lane(1346, 4, H)
        edge_pen = lane(1362, 2, QC)
        carry = lane(1446, 3, H)
        XL2 = blk[0:PR, 2650:2650 + T * XLW].rearrange("p (t w) -> p t w", t=T)
        iota_n = blk[:, 5250:5250 + N]
        x1T = arena[:, 0:2000].rearrange("p (k r) -> p k r", k=KD)
        x2T = arena[:, 2000:4000].rearrange("p (k r) -> p k r", k=KD)
        sqT = arena[:, 4000:6000].rearrange("p (k r) -> p k r", k=KD)
        yT = sqT
        hT = arena[:, 6000:9000].rearrange("p (j r) -> p j r", j=12)
        gT = arena[:, 9000:9000 + 2 * N].rearrange("p (k r) -> p k r", k=2)
        xrow = blk[0:PR, 0:2 * D].rearrange("p (k d) -> p k d", k=2)
        qT = blk[:, 2048:4048].rearrange("p (k r) -> p k r", k=KD)
        yrow = blk[0:PR, 4096:4096 + 2 * D].rearrange("p (k d) -> p k d", k=2)

        diff = sb("diff", [128, 128])
        ident = sb("ident", [128, 128])
        ones = sb("ones", [128, 128])
        onesb = sb("onesb", [PR, 128], bf16)
        cols = sb("cols", [128, 128])
        gid = sb("gid", [128, QC])
        nid = sb("nid", [PR, T])
        att8 = sb("att8", [128, HID])
        att2 = sb("att2", [128, HID])
        rmsw = sb("rmsw", [128, KD])
        ix = sb("ix", [PR, 16, 11])
        ridx = sb("ridx", [PR, T], i32)
        bidx = sb("bidx", [128, QC + 1], i32)
        nidx = sb("nidx", [128, QC], i32)
        ngf = sb("ngf", [128, QC])
        uns = sb("uns", [128, 2, QC])
        thr = sb("thr", [1, T - 1])
        slot_t = sb("slot_t", [1, SLOTS])
        slot_i = sb("slot_i", [1, 3, SLOTS], i32)
        st = sb("st", [PR, 2, 2, 6])
        mv = sb("mv", [PR, 2, 2])
        vr = sb("vr", [PR, 3, 2, 2])
        es = sb("es", [PR, 2, T, H])
        esel = sb("esel", [PR, T, H])
        TAB = sb("TAB", [128, KD, 2 * G], i32)
        XR = sb("XR", [128, RING, XRW])
        bcol = sb("bcol", [128, KD], i32)
        ncol = sb("ncol", [128, RING], i32)
        pen = sb("pen", [128, RING, G])
        sc = sb("sc", [128, RING, G, H])
        mx = sb("mx", [128, 2, H])
        oo = sb("oo", [128, 2, HID])
        MR = sb("MR", [128, QC, H])
        DN = sb("DN", [128, QC, H])
        avg = sb("avg", [128, 128])
        eps = sb("eps", [128, 1])
        gw = sb("gw", [128, KD, 2])
        gwd = sb("gwd", [128, KD])
        b1s = sb("b1s", [128, 12])
        b2s = sb("b2s", [128, 3, KD])
        vb = sb("vb", [128, 2, BR])
        sq = sb("sq", [128, 2, 2 * BR])
        laneT = sq[:, :, :].rearrange("p a b -> p (a b)")[0:H, 0:774].rearrange("p (a l) -> p a l", a=6)
        msk = sq[:, 0, :].rearrange("p (e r) -> p e r", e=2)
        gwb = arena[:, 11500:11500 + KD * 128].rearrange("p (k m) -> p k m", k=KD)
        hot = vb[:, :, :].rearrange("p a b -> p (a b)")[:, 0:3 * PR].rearrange("p (k n) -> p k n", k=3)
        nrm = sb("nrm", [128, 2 * BR])
        gacc = sb("gacc", [128, KD])
        gpart = sb("gpart", [128, KD])

        ps = [ctx.enter_context(nc.psum_tensor(f"ps{i}", [128, 512], f32)) for i in range(8)]

        consts = sem("consts"); dv = sem("dv"); av = sem("av"); pl = sem("pl"); passed = sem("passed")
        ld_small = sem("ld_small"); ld_edges = sem("ld_edges"); ld_x = sem("ld_x"); ld_wd = sem("ld_wd")
        tab_ready = sem("tab_ready"); tab_stored = sem("tab_stored")
        heads_f = sem("heads_f"); heads_bc = sem("heads_bc"); rows_wanted = sem("rows_wanted")
        rows_here = sem("rows_here"); first_edges = sem("first_edges"); next_edges = sem("next_edges")
        unaligned = sem("unaligned"); unaligned_sums = sem("unaligned_sums"); hits = sem("hits")
        group_counts = sem("group_counts"); index_ready = sem("index_ready")
        wd_ready = sem("wd_ready"); var_ready = sem("var_ready"); std_ready = sem("std_ready")
        xn_ready = sem("xn_ready"); xT_pe = sem("xT_pe"); xT_act = sem("xT_act"); xT_dve = sem("xT_dve")
        xT_stored = sem("xT_stored"); hT_pe = sem("hT_pe"); hT_act = sem("hT_act"); lr_pe = sem("lr_pe")
        lr_dve = sem("lr_dve"); tabs_ready = sem("tabs_ready"); tabs_stored = sem("tabs_stored")
        w_ld = [sem("w_ld0"), sem("w_ld1")]
        w_pe = sem("w_pe"); w_act = sem("w_act")
        bcol_ready = sem("bcol_ready"); tab_here = [sem(f"tab_here{r}") for r in range(KD)]
        xl_here = [sem(f"xl_here{r}") for r in range(RING)]
        scores = sem("scores"); exps = sem("exps"); mul_act = sem("mul_act"); sums = sem("sums")
        o_stored = [sem("o_stored0"), sem("o_stored1")]
        xb_here = sem("xb_here"); kvq_pe = sem("kvq_pe"); sq_act = sem("sq_act")
        kv_dve = sem("kv_dve"); sq_pe = sem("sq_pe"); norm_act = sem("norm_act")
        block_dve = sem("block_dve"); q_stored = sem("q_stored")
        stats_stored = sem("stats_stored"); nodes_stored = sem("nodes_stored"); lanes_here = sem("lanes_here")
        ends_ready = sem("ends_ready"); ends_T = sem("ends_T"); carry_ready = sem("carry_ready")
        carry_back = sem("carry_back"); shift_ready = sem("shift_ready"); factor_act = sem("factor_act")
        factors_ready = sem("factors_ready"); factors_stored = sem("factors_stored")
        factors_here = sem("factors_here"); o_here = sem("o_here"); xl2_here = sem("xl2_here")
        hot_ready = sem("hot_ready"); slot_pe = sem("slot_pe"); slot_dve = sem("slot_dve")
        self_ready = sem("self_ready"); self_act = sem("self_act"); gnn_ready = sem("gnn_ready")
        gT_pe = sem("gT_pe"); gT_dve = sem("gT_dve")
        ff_w = sem("ff_w"); ff_small = sem("ff_small"); gate_ready = sem("gate_ready")
        xq_here = sem("xq_here"); x1_pe = sem("x1_pe"); x1_dve = sem("x1_dve"); mean_pe = sem("mean_pe")
        cen_dve = sem("cen_dve"); sqr_act = sem("sqr_act"); var_pe = sem("var_pe"); dev_act = sem("dev_act")
        x2_dve = sem("x2_dve"); gate_pe = sem("gate_pe"); mask_dve = sem("mask_dve"); h_pe = sem("h_pe")
        h_dve = sem("h_dve"); h_act = sem("h_act"); y_pe = sem("y_pe"); y_dve = sem("y_dve")
        yT_pe = sem("yT_pe"); yr_act = sem("yr_act"); yr_dve = sem("yr_dve"); out_stored = sem("out_stored")

        block = ctx.enter_context(nc.Block())

        def alone(eng, s, value):
            eng.wait_ge(s, value)
            eng.sem_inc(passed)

        @block.sync
        def _(sp):
            for s in (xT_stored, q_stored, out_stored, *o_stored):
                sp.sem_inc(s)
            sp.dma_start(heads_i, dst[::ROW].rearrange("(a r) -> a r", a=1), allow_slow_non_contiguous=True).then_inc(ld_edges, 16)
            sp.dma_start(src_sb, src.rearrange("(p e) -> p e", p=PR)).then_inc(ld_edges, 16)
            sp.dma_start(dst_sb, dst.rearrange("(p e) -> p e", p=PR)).then_inc(ld_edges, 16)
            sp.dma_start(x_all, x.rearrange("(t p) d -> p t d", p=PR)).then_inc(ld_x, 16)
            sp.dma_start(att8[:, :], att.rearrange("h d -> (h d)").partition_broadcast(128)).then_inc(ld_small, 16)
            sp.dma_start(rmsw[:, :], rms_w.rearrange("(k p) -> p k", p=128), allow_slow_non_contiguous=True).then_inc(ld_small, 16)
            sp.dma_start(gw[:, :, 0], gate_w[0].rearrange("(k p) -> p k", p=128), allow_slow_non_contiguous=True).then_inc(ff_small, 16)
            sp.dma_start(gw[:, :, 1], gate_w[1].rearrange("(k p) -> p k", p=128), allow_slow_non_contiguous=True).then_inc(ff_small, 16)
            for e, (a, c) in enumerate(((b1[0], b2[0]), (b1[1], b2[1]), (sb1, sb2))):
                sp.dma_start(b1s[:, 4 * e:4 * e + 4], a.rearrange("(k p) -> p k", p=128), allow_slow_non_contiguous=True).then_inc(ff_small, 16)
                sp.dma_start(b2s[:, e], c.rearrange("(k p) -> p k", p=128), allow_slow_non_contiguous=True).then_inc(ff_small, 16)
            sp.dma_start(wd, W_down.rearrange("(k p) h -> p k h", p=128)).then_inc(ld_wd, 16)
            sp.dma_start(wl, Wl.rearrange("(k p) h -> p k h", p=128)).then_inc(ld_wd, 16)
            sp.dma_start(wr, Wr.rearrange("(k p) h -> p k h", p=128)).then_inc(ld_wd, 16)
            sp.wait_ge(tab_ready, 1)
            sp.dma_start(edge_tab.rearrange("(p b) w -> p b w", p=PR), tab_sb).then_inc(tab_stored, 16)
            sp.wait_ge(index_ready, 1)
            sp.dma_start(n_d.rearrange("(q p) a -> p (q a)", p=128), ngf[:, :], allow_slow_non_contiguous=True).then_inc(nodes_stored, 16)
            with sp.Fori(0, NB) as b:
                sp.wait_ge(xT_act, 1 + 2 * b + 2)
                sp.wait_ge(xT_dve, 1 + 2 * b + 2)
                sp.dma_start(xnT_d[bass.ds(b, 1)].rearrange("a p f -> (a p) f"),
                             xnTb.rearrange("p k r -> p (k r)")).then_inc(xT_stored, 16)
            sp.wait_ge(tabs_ready, 1)
            sp.dma_start(xl_tab.rearrange("(t p) w -> p t w", p=PR), XLs).then_inc(tabs_stored, 16)
            sp.dma_start(xr_tab.rearrange("(t p) w -> p t w", p=PR), XRs).then_inc(tabs_stored, 16)
            sp.wait_ge(xT_pe, 1 + 4 * NB)
            for w, W in enumerate((W_k, W_q, W_v)):
                with sp.Fori(0, KD // 2) as i:
                    for k in range(2):
                        if w == 0:
                            alone(sp, w_pe, 1 + 2 * i)
                        else:
                            alone(sp, w_pe, 1 + w * KD + 2 * i + k - 1)
                        sp.dma_start(wraw[:, k, :], W[bass.ds((2 * i + k) * 128, 128), :]).then_inc(w_ld[k], 16)
            sp.wait_ge(tabs_stored, 32)

            def load_x(b):
                sp.dma_start(XB.rearrange("p k r -> p (k r)"),
                             xnT_d[bass.ds(b, 1)].rearrange("a p f -> (a p) f")).then_inc(xb_here, 16)

            def store_chunk(q, e):
                alone(sp, sums, RING + q + 1)
                sp.dma_start(o_d[bass.ds(q, 1)].rearrange("a p f -> (a p) f"), oo[:, e % 2, :]).then_inc(o_stored[e % 2], 16)
                sp.dma_start(m_d[bass.ds(q * 128, 128), :],
                             MR[:, bass.ds(q, 1), :].rearrange("p a h -> p (a h)")).then_inc(stats_stored, 16)

            def edge_block(b, more):
                for e in range(KD):
                    store_chunk(KD * b + e, e)
                    if e == KD - 2 and more:
                        alone(sp, kvq_pe, 1 + KD * b + KD)
                        load_x(b + 1)
                alone(sp, block_dve, 1 + b + 1)
                sp.dma_start(q_d[bass.ds(b, 1)].rearrange("a p f -> (a p) f"),
                             Qb.rearrange("p k r -> p (k r)")).then_inc(q_stored, 16)

            load_x(0)
            with sp.Fori(0, NB - 1) as b:
                edge_block(b, True)
            edge_block(NB - 1, False)
            for q in range(NB * KD, QC):
                store_chunk(q, q)
            sp.wait_ge(kvq_pe, 1 + NB * KD)
            for e, (a, c) in enumerate(((w1[0], w2[0]), (w1[1], w2[1]), (sw1, sw2))):
                sp.dma_start(w1s[:, e], a.rearrange("(k p) h -> p k h", p=128)).then_inc(ff_w, 16)
                sp.dma_start(w2s[:, e], c.rearrange("(k p) d -> p k d", p=128)).then_inc(ff_w, 16)
            sp.dma_start(wraw[:, :, :], W_up.rearrange("(k p) d -> p k d", p=128)).then_inc(ff_w, 16)
            sp.wait_ge(stats_stored, 16 * QC)
            sp.wait_ge(nodes_stored, 16)
            sp.dma_start(ML, m_d.rearrange("(l j) h -> l j h", j=QC)).then_inc(lanes_here, 16)
            sp.dma_start(NL, n_d.rearrange("(l j) a -> l (j a)", j=QC)).then_inc(lanes_here, 16)
            sp.wait_ge(o_stored[0], 1 + 16 * (QC // 2))
            sp.wait_ge(o_stored[1], 1 + 16 * (QC // 2))
            sp.dma_start(RH[:, :, 0:HID], o_d.rearrange("q p f -> p q f")).then_inc(o_here, 16)
            sp.wait_ge(q_stored, 1 + 16 * NB)
            sp.dma_start(XL2, xl_tab.rearrange("(t p) w -> p t w", p=PR)).then_inc(xl2_here, 16)
            sp.wait_ge(factors_ready, 1)
            sp.dma_start(f_d.rearrange("(l j) w -> l j w", j=QC), FL).then_inc(factors_stored, 16)
            sp.wait_ge(factors_stored, 16)
            sp.dma_start(FG, f_d.rearrange("(q p) w -> p q w", p=128)).then_inc(factors_here, 16)
            sp.wait_ge(gT_pe, NB)
            with sp.Fori(0, NB) as b:
                alone(sp, x1_dve, 1 + KD * b)
                sp.dma_start(xrow, x[bass.ds(b * BR, BR), :].rearrange("(k p) d -> p k d", p=PR)).then_inc(xq_here, 16)
                sp.dma_start(qT.rearrange("p k r -> p (k r)"),
                             q_d[bass.ds(b, 1)].rearrange("a p f -> (a p) f")).then_inc(xq_here, 16)
                alone(sp, yr_act, 1 + 2 * b + 2)
                alone(sp, yr_dve, 1 + 2 * b + 2)
                sp.dma_start(out[bass.ds(b * BR, BR), :].rearrange("(k p) d -> p k d", p=PR), yrow).then_inc(out_stored, 16)
            sp.wait_ge(out_stored, 1 + 16 * NB)


        @block.gpsimd
        def _(pool):
            g = nc.gpsimd
            at = Steps(pool, pl)
            g.memset(bidx[:, QC:], 0)
            g.memset(eps[:, :], 1e-5).then_inc(consts, 1)
            g.iota(diff[:, :], pattern=[[1, 128]], base=0, channel_multiplier=-1, allow_small_or_imprecise_dtypes=True).then_inc(consts, 1)
            g.iota(cols[:, :], pattern=[[1, 128]], base=0, channel_multiplier=0, allow_small_or_imprecise_dtypes=True).then_inc(consts, 1)
            g.iota(gid[:, :], pattern=[[128, QC]], base=0, channel_multiplier=1, allow_small_or_imprecise_dtypes=True).then_inc(consts, 1)
            g.iota(nid[:, :], pattern=[[PR, T]], base=0, channel_multiplier=1, allow_small_or_imprecise_dtypes=True).then_inc(consts, 1)
            pool.wait_ge(rows_wanted, 1)
            for t in range(T):
                g.indirect_dma_start(row_i[:, t, :], None, dst.rearrange("(r w) -> r w", w=ROW),
                                     bass.IndirectOffsetOnAxis(ridx[:, t:t + 1], 0)).then_inc(rows_here, 16)
            pool.wait_ge(index_ready, 1)
            pool.wait_ge(tab_stored, 16)
            pool.wait_ge(tabs_stored, 32)
            at.link(g.tensor_copy(bcol[:, 0:1], bidx[:, 0:1]))
            g.indirect_dma_start(TAB[:, 0, :], None, edge_tab[:, :],
                                 bass.IndirectOffsetOnAxis(bcol[:, 0:1], 0)).then_inc(tab_here[0], 16)

            def gather(q, e, uses, last=False):
                r, nxt = e % RING, (e + 1) % KD
                alone(pool, sums, RING + q + 1 - RING)
                if not last:
                    at.add(g.tensor_copy(bcol[:, nxt:nxt + 1], bidx[:, bass.ds(q + 1, 1)]))
                at.add(g.tensor_copy(ncol[:, r:r + 1], nidx[:, bass.ds(q, 1)]))
                alone(pool, pl, at.turn + at.done)
                if not last:
                    g.indirect_dma_start(TAB[:, nxt, :], None, edge_tab[:, :],
                                         bass.IndirectOffsetOnAxis(bcol[:, nxt:nxt + 1], 0)).then_inc(tab_here[nxt], 16)
                alone(pool, tab_here[e], 16 * uses)
                g.indirect_dma_start(XR[:, r, :], None, xr_tab[:, :],
                                     bass.IndirectOffsetOnAxis(ncol[:, r:r + 1], 0)).then_inc(xl_here[r], 16)
                for j in range(G):
                    g.indirect_dma_start(XL[:, r, j, :], None, xl_tab[:, :],
                                         bass.IndirectOffsetOnAxis(TAB[:, e, j:j + 1], 0)).then_inc(xl_here[r], 16)

            with pool.Fori(0, NB) as b:
                at.enter(b, 2 * KD)
                for e in range(KD):
                    gather(KD * b + e, e, b + 1)
            at.leave(NB)
            gather(NB * KD, 0, NB + 1)
            gather(NB * KD + 1, 1, NB + 1, last=True)
            pool.wait_ge(block_dve, 1 + NB)
            pool.wait_ge(q_stored, 1 + 16 * NB)
            g.iota(iota_n, pattern=[[1, N]], base=0, channel_multiplier=0, allow_small_or_imprecise_dtypes=True).then_inc(consts, 1)

        @block.scalar
        def _(act):
            for s in (xT_act, hT_act, w_act, sq_act, norm_act, yr_act):
                act.sem_inc(s)
            a = nc.scalar
            with act.Fori(0, NB) as b:
                act.wait_ge(var_ready, b + 1)
                a.activation(vr[:, 1], vr[:, 0], ACT.Sqrt).then_inc(std_ready, 1)
                alone(act, xT_stored, 1 + 16 * b)
                alone(act, hT_pe, 1 + b)
                for k in range(2):
                    act.wait_ge(xT_pe, 1 + 4 * b + 2 * k + 1)
                    a.copy(xnTb[:, 0:4, PR * k:PR * k + PR],
                           ps[2 * k][:, 0:4 * PR].rearrange("p (k r) -> p k r", k=4)).then_inc(xT_act, 1)
                alone(act, lr_pe, 1 + 2 * b)
                act.wait_ge(hT_pe, 1 + b + 1)
                a.copy(hTb, ps[4][:, 0:2 * BR].rearrange("p (k r) -> p k r", k=2)).then_inc(hT_act, 1)
            for w in range(3):
                if w == 1:
                    act.wait_ge(tabs_ready, 1)
                    act.wait_ge(xT_stored, 1 + 16 * NB)
                if w == 2:
                    act.wait_ge(index_ready, 1)
                    act.wait_ge(tab_stored, 16)
                with act.Fori(0, KD // 2) as i:
                    for k in range(2):
                        alone(act, w_pe, 1 + KD * w + 2 * i + k + 1)
                        for h in range(2):
                            last = a.copy(wt[:, w, 4 * h:4 * h + 4, bass.ds((2 * i + k) * 128, 128)],
                                          ps[2 * k + h][:, :].rearrange("p (k r) -> p k r", k=4))
                        last.then_inc(w_act, 1)

            def weigh(q, e):
                r = e % RING
                act.wait_ge(scores, q + 1)
                a.activation(sc[:, r], sc[:, r], ACT.Exp).then_inc(exps, 1)
                act.wait_ge(exps, q + 1)
                for j in range(ACT_J):
                    for h in range(H):
                        m = XL[:, r, j, h * DH:h * DH + DH]
                        last = a.mul(m, m, sc[:, r, j, h:h + 1])
                last.then_inc(mul_act, 1)

            weigh(0, 0)
            weigh(1, 1)
            with act.Fori(0, NB) as b:
                for e in range(KD):
                    u, k = KD * b + e, e % 2
                    if e == 0:
                        alone(act, block_dve, 1 + b)
                        alone(act, q_stored, 1 + 16 * b)
                    if e >= 2:
                        alone(act, kv_dve, 1 + u - 1)
                        alone(act, sq_pe, u - 1)
                    act.wait_ge(kvq_pe, 1 + u + 1)
                    a.copy(vb[:, k, :], ps[2 + k][:, 0:BR])
                    a.copy(Qb[:, e, :], ps[k][:, BR:2 * BR])
                    a.activation(sq[:, k, :], ps[k][:, 0:2 * BR], ACT.Square).then_inc(sq_act, 1)
                    if e == KD - 1:
                        act.wait_ge(sq_pe, KD * b + KD)
                        a.activation(nrm[:, :], ps[4][:, 0:2 * BR], ACT.Sqrt).then_inc(norm_act, 1)
                    weigh(u + 2, e + 2)
            act.wait_ge(shift_ready, 1)
            a.activation(FL[:, :, 0:H], FL[:, :, 0:H], ACT.Exp).then_inc(factor_act, 1)
            act.wait_ge(self_ready, 1)
            a.activation(es[:, 0], es[:, 0], ACT.Exp).then_inc(self_act, 1)
            act.wait_ge(ff_small, 16 * 8)
            with act.Fori(0, NB) as b:
                alone(act, yT_pe, 1 + 4 * b)
                act.wait_ge(cen_dve, b + 1)
                a.activation(sqT, x2T, ACT.Square).then_inc(sqr_act, 1)
                alone(act, x2_dve, 1 + b)
                act.wait_ge(var_pe, b + 1)
                a.activation(nrm[:, 0:BR], ps[3][:, 0:BR], ACT.Sqrt, bias=eps[:, :]).then_inc(dev_act, 1)
                for j in range(12):
                    if j < 8:
                        act.wait_ge(h_dve, 8 * b + j + 1)
                        a.activation(hT[:, j], hT[:, j], ACT.Relu, bias=b1s[:, j:j + 1]).then_inc(h_act, 1)
                    else:
                        act.wait_ge(h_pe, 12 * b + j + 1)
                        a.activation(hT[:, j], ps[j % 2][:, 0:BR], ACT.Relu, bias=b1s[:, j:j + 1]).then_inc(h_act, 1)
                alone(act, out_stored, 1 + 16 * b)
                for k in range(2):
                    act.wait_ge(yT_pe, 1 + 4 * b + 2 * k + 1)
                    a.copy(yrow[:, k, 0:512], ps[4 + 2 * k][0:PR, :]).then_inc(yr_act, 1)

        @block.vector
        def _(dve):
            for s in (x1_dve, block_dve, x2_dve, xT_dve, lr_dve, kv_dve, slot_dve, y_dve, mask_dve, yr_dve, *([sums] * RING)):
                dve.sem_inc(s)
            v = nc.vector
            at = Steps(dve, dv)
            bc = lambda ap, shape: ap.to_broadcast(shape)
            TT, TS, STT, RED = v.tensor_tensor, v.tensor_scalar, v.scalar_tensor_tensor, v.tensor_reduce

            v.memset(ones[:, :], 1.0)
            v.memset(onesb[:, :], 1.0)
            v.memset(avg[:, :], 1.0 / D)
            v.memset(gacc[:, :], 0.0)
            dve.wait_ge(consts, 5)
            TS(ident[:, :], diff[:, :], 0.0, None, ALU.is_equal)
            TS(shiftA, diff[0:PR, 0:PR], -1.0, None, ALU.is_equal)
            TS(shiftB, diff[0:PR, 0:PR], float(PR - 1), None, ALU.is_equal)
            at.add(TS(before, diff[0:PR, 0:PR], 1.0, None, ALU.is_ge))

            dve.wait_ge(ld_edges, 48)
            v.tensor_copy(heads[0:1], heads_i).then_inc(heads_f, 1)
            v.tensor_copy(tab_sb[:, :, 0:G], src_sb.rearrange("p (b j) -> p b j", j=G))
            v.tensor_copy(tab_sb[:, :, G:2 * G], dst_sb.rearrange("p (b j) -> p b j", j=G)).then_inc(tab_ready, 1)
            dve.wait_ge(heads_bc, 1)
            at.link(TT(cmp1, ps[7][0:PR, None, 0:ROWS].to_broadcast([PR, T, ROWS]),
                       nid[:, :, None].to_broadcast([PR, T, ROWS]), ALU.is_lt))
            at.link(RED(ix[:, 0, 0:T], cmp1, AXX, ALU.add))
            at.link(TS(ix[:, 1, 0:T], ix[:, 0, 0:T], -1.0, 0.0, ALU.add, ALU.max))
            v.tensor_copy(ridx[:, :], ix[:, 1, 0:T]).then_inc(rows_wanted, 1)
            dve.wait_ge(rows_here, 16 * T)
            at.link(TT(cmp1[:, :, 0:ROW], row_i, nid[:, :, None].to_broadcast([PR, T, ROW]), ALU.is_lt))
            v.memset(ix[:, 2, T:], float(E))
            at.link(RED(ix[:, 0, 0:T], cmp1[:, :, 0:ROW], AXX, ALU.add))
            STT(ix[:, 2, 0:T], ix[:, 1, 0:T], float(ROW), ix[:, 0, 0:T], ALU.mult, ALU.add).then_inc(first_edges, 1)
            dve.wait_ge(first_edges, 1)
            first = ix[:, 2, 0:T]

            def floor_div(to, a, d, margin, w):
                at.link(TS(ix[:, w, 0:T], a, 1.0 / d, -margin, ALU.mult, ALU.add))
                at.link(TS(to, ix[:, w, 0:T], RNE, -RNE, ALU.add, ALU.add))

            floor_div(ix[:, 4, 0:T], first, G, 0.45, 3)
            at.link(STT(ix[:, 5, 0:T], ix[:, 4, 0:T], -float(G), first, ALU.mult, ALU.add))
            at.link(TS(ix[:, 5, 0:T], ix[:, 5, 0:T], 0.5, None, ALU.is_gt))
            dve.wait_ge(next_edges, 1)
            at.link(TT(ix[:, 6, 0:T], ps[6][0:PR, 0:T], first, ALU.is_gt))
            TT(ix[:, 7, 0:T], ix[:, 5, 0:T], ix[:, 6, 0:T], ALU.mult).then_inc(unaligned, 1)
            at.link(TT(ix[:, 8, 0:T], ix[:, 4, 0:T], ix[:, 5, 0:T], ALU.add))
            dve.wait_ge(unaligned_sums, 1)
            at.add(v.memset(ix[:, 9, 0:T], 0.0))
            at.link(v.tensor_copy(ix[:, 11, 0:T], ps[5][0:PR, 16:16 + T]))
            at.link(v.tensor_tensor_scan(ix[:, 10, 0:T], ix[:, 11, 0:T], ix[:, 9, 0:T], 0.0, ALU.add, ALU.add))
            at.link(TT(ix[:, 10, 0:T], ix[:, 10, 0:T], ix[:, 11, 0:T], ALU.subtract))
            at.link(TT(ix[:, 10, 0:T], ix[:, 10, 0:T], ps[5][0:PR, 0:T], ALU.add))
            at.link(TT(ix[:, 8, 0:T], ix[:, 8, 0:T], ix[:, 10, 0:T], ALU.add))
            floor_div(ix[:, 12, 0:T], ix[:, 8, 0:T], 128, 0.498, 3)
            at.link(STT(ix[:, 13, 0:T], ix[:, 12, 0:T], -128.0, ix[:, 8, 0:T], ALU.mult, ALU.add))
            v.tensor_tensor(stepR, cols[0:PR, None, :].to_broadcast([PR, T, 128]),
                            ix[:, 13, 0:T, None].to_broadcast([PR, T, 128]), ALU.is_ge)
            TT(hitA[:, :, 0:QC], cols[0:PR, None, 0:QC].to_broadcast([PR, T, QC]),
               ix[:, 12, 0:T, None].to_broadcast([PR, T, QC]), ALU.is_equal)
            at.link(TT(hitB[:, :, 0:QC], cols[0:PR, None, 0:QC].to_broadcast([PR, T, QC]),
                       ix[:, 12, 0:T, None].to_broadcast([PR, T, QC]), ALU.is_gt))
            TT(hitA[:, :, QC:], hitA[:, :, 0:QC], ix[:, 7, 0:T, None].to_broadcast([PR, T, QC]), ALU.mult)
            TT(hitB[:, :, QC:], hitB[:, :, 0:QC], ix[:, 7, 0:T, None].to_broadcast([PR, T, QC]), ALU.mult).then_inc(hits, 1)
            at.link(TT(thr[:, :], ix[0:1, 12, 1:T], cols[0:1, 1:T], ALU.add))
            at.link(TT(slot_c, cols[0:1, 0:SLOTS, None].to_broadcast([1, SLOTS, T - 1]),
                       thr[:, None, :].to_broadcast([1, SLOTS, T - 1]), ALU.is_ge))
            at.link(RED(slot_t[:, :], slot_c, AXX, ALU.add))
            v.tensor_copy(slot_i[:, 0, :], slot_t[:, :])
            TS(slot_i[:, 2, :], slot_t[:, :], float(PR), None, ALU.mult)
            TT(slot_i[:, 1, :], cols[0:1, 0:SLOTS], slot_t[:, :], ALU.subtract)
            dve.wait_ge(group_counts, 1)
            at.link(TT(uns[:, 0], gid[:, :], ps[4][:, QC:2 * QC], ALU.subtract))
            at.link(TS(uns[:, 1], uns[:, 0], BLOCKS - 0.5, None, ALU.is_lt))
            TS(bidx[:, 0:QC], uns[:, 0], float(BLOCKS - 1), None, ALU.min)
            at.link(TT(ngf[:, :], uns[:, 1], ps[4][:, 0:QC], ALU.mult))
            at.link(TS(ngf[:, :], ngf[:, :], -1.0, None, ALU.add))
            TS(nidx[:, :], ngf[:, :], 0.0, None, ALU.max).then_inc(index_ready, 1)

            dve.wait_ge(ld_small, 32)
            TS(att2[:, :], att8[:, :], NEG_SLOPE, None, ALU.mult)
            at.link(TS(att8[:, :], att8[:, :], 1.0 - NEG_SLOPE, None, ALU.mult))
            dve.wait_ge(ld_wd, 48)
            for k in range(KD):
                last = TS(wd[:, k, :], wd[:, k, :], rmsw[:, k:k + 1], None, ALU.mult)
            last.then_inc(wd_ready, 1)
            dve.wait_ge(ld_x, 16)
            xnb = wraw[0:PR]
            with dve.Fori(0, NB) as b:
                at.enter(b, 10)
                for k in range(2):
                    for h in range(2):
                        at.add(v.bn_stats(st[:, k, h, :], x_all[:, bass.ds(2 * b + k, 1), 512 * h:512 * h + 512].rearrange("p a d -> p (a d)")))
                alone(dve, dv, at.turn + at.done)
                for k in range(2):
                    at.add(v.bn_aggr(mv[:, k, :], st[:, k].rearrange("p a s -> p (a s)")))
                at.wait()
                at.link(TS(vr[:, 0, :, 0:1], mv[:, :, 1:2], 1e-5, None, ALU.add))
                at.link(v.reciprocal(vr[:, 2, :, 0:1], vr[:, 0, :, 0:1]))
                at.link(TT(vr[:, 2, :, 1:2], mv[:, :, 1:2], vr[:, 2, :, 0:1], ALU.mult))
                TS(vr[:, 0, :, 1:2], vr[:, 2, :, 1:2], 1e-6, None, ALU.add).then_inc(var_ready, 1)
                dve.wait_ge(std_ready, b + 1)
                at.link(v.reciprocal(vr[:, 2], vr[:, 1]))
                alone(dve, xT_pe, 1 + 4 * b)
                for k in range(2):
                    TS(xnb[:, k, :], x_all[:, bass.ds(2 * b + k, 1), :].rearrange("p a d -> p (a d)"), mv[:, k, 0:1], vr[:, 2, k, 0:1],
                       ALU.subtract, ALU.mult).then_inc(xn_ready, 1)
                alone(dve, xT_stored, 1 + 16 * b)
                alone(dve, hT_pe, 1 + b)
                for k in range(2):
                    dve.wait_ge(xT_pe, 1 + 4 * b + 2 * k + 2)
                    v.tensor_copy(xnTb[:, 4:8, PR * k:PR * k + PR],
                                  ps[2 * k + 1][:, 0:4 * PR].rearrange("p (k r) -> p k r", k=4)).then_inc(xT_dve, 1)
                for k in range(2):
                    dve.wait_ge(lr_pe, 1 + 2 * b + k + 1)
                    TS(XLs[:, bass.ds(2 * b + k, 1), 0:HID].rearrange("p a d -> p (a d)"), ps[5 + k][0:PR, 0:HID], vr[:, 2, k, 1:2], None, ALU.mult)
                    TS(XRs[:, bass.ds(2 * b + k, 1), 0:HID].rearrange("p a d -> p (a d)"), ps[5 + k][0:PR, HID:], vr[:, 2, k, 1:2], None, ALU.mult).then_inc(lr_dve, 1)
            at.leave(NB)
            heads_view = lambda ap: ap.rearrange("p t (h d) -> p t h d", h=H)
            all_t = lambda ap: ap[:, None, :].to_broadcast([PR, T, HID])
            dve.wait_ge(lr_dve, 1 + 2 * NB)
            at.link(TT(tmpX, XLs[:, :, 0:HID], all_t(att2[0:PR]), ALU.mult))
            at.link(RED(XLs[:, :, HID:], heads_view(tmpX), AXX, ALU.add))
            at.link(TT(tmpX, XRs[:, :, 0:HID], all_t(att2[0:PR]), ALU.mult))
            at.link(RED(XRs[:, :, HID:HID + H], heads_view(tmpX), AXX, ALU.add))
            at.link(TT(tmpX, XRs[:, :, 0:HID], XLs[:, :, 0:HID], ALU.add))
            at.link(STT(tmpX, tmpX, 0.0, all_t(att8[0:PR]), ALU.max, ALU.mult))
            at.link(RED(es[:, 0], heads_view(tmpX), AXX, ALU.add))
            at.link(TT(es[:, 1], XLs[:, :, HID:], XRs[:, :, HID:HID + H], ALU.add))
            at.link(TT(esel[:, :, :], es[:, 0], es[:, 1], ALU.add))
            v.tensor_copy(XRs[:, :, HID + H:], esel[:, :, :]).then_inc(tabs_ready, 1)

            def score(q, e, uses):
                r = e % RING
                s = sc[:, r]
                dve.wait_ge(xl_here[r], 16 * (G + 1) * uses)
                at.add(TT(pen[:, r, :], TAB[:, e % KD, G:2 * G], ngf[:, bass.ds(q, 1)].to_broadcast([128, G]), ALU.is_equal))
                at.link(TT(msg, XL[:, r, :, 0:HID], XR[:, r, None, 0:HID].to_broadcast([128, G, HID]), ALU.add))
                at.add(TS(pen[:, r, :], pen[:, r, :], BIG, -BIG, ALU.mult, ALU.add))
                at.link(STT(msg, msg, 0.0, att8[:, None, :].to_broadcast([128, G, HID]), ALU.max, ALU.mult))
                at.link(RED(s, msg.rearrange("p j (h d) -> p j h d", h=H), AXX, ALU.add))
                at.link(TT(s, s, XL[:, r, :, HID:], ALU.add))
                at.link(TT(s, s, XR[:, r, None, HID:HID + H].to_broadcast([128, G, H]), ALU.add))
                at.link(TT(s, s, pen[:, r, :, None].to_broadcast([128, G, H]), ALU.add))
                at.link(RED(mx[:, 0], s.rearrange("p j h -> p h j"), AXX, ALU.max))
                at.add(TT(MR[:, bass.ds(q, 1), :].rearrange("p a h -> p (a h)"), mx[:, 0], XR[:, r, HID + H:], ALU.max))
                at.link(TT(mx[:, 1], mx[:, 0], XR[:, r, HID + H:], ALU.max))
                TT(s, s, mx[:, None, 1].to_broadcast([128, G, H]), ALU.subtract).then_inc(scores, 1)

            def message(q, e, stored):
                r = e % RING
                x = XL[:, r, :, 0:HID]
                y = x[:, ACT_J:].rearrange("p j (h d) -> p j h d", h=H)
                dve.wait_ge(exps, q + 1)
                at.add(TT(y, y, sc[:, r, ACT_J:, :, None].to_broadcast([128, G - ACT_J, H, DH]), ALU.mult))
                at.link(RED(DN[:, bass.ds(q, 1), :].rearrange("p a h -> p (a h)"), sc[:, r].rearrange("p j h -> p h j"),
                            AXX, ALU.add))
                dve.wait_ge(mul_act, q + 1)
                at.link(TT(x[:, 0:5], x[:, 0:5], x[:, 5:10], ALU.add))
                at.link(TT(x[:, 0:2], x[:, 0:2], x[:, 2:4], ALU.add))
                at.link(TT(x[:, 0], x[:, 0], x[:, 1], ALU.add))
                dve.wait_ge(o_stored[e % 2], 1 + 16 * stored)
                TT(oo[:, e % 2, :], x[:, 0], x[:, 4], ALU.add).then_inc(sums, 1)

            score(0, 0, 1)
            score(1, 1, 1)
            message(0, 0, 0)
            with dve.Fori(0, NB) as b:
                at.enter(b, KD * 16 + 5)
                for e in range(KD):
                    u = KD * b + e
                    score(u + 2, e + 2, 2 * b + (e + 2) // RING + 1)
                    message(u + 1, e + 1, 4 * b + (e + 1) // 2)
                    if e == 0:
                        alone(dve, block_dve, 1 + b)
                    dve.wait_ge(sq_act, 1 + u + 1)
                    TT(KVb[:, e, :], ps[e % 2][:, 0:BR], vb[:, e % 2, :], ALU.mult).then_inc(kv_dve, 1)
                dve.wait_ge(norm_act, 1 + b + 1)
                at.link(TS(nrm[:, :], nrm[:, :], 1e-12, None, ALU.max))
                at.link(v.reciprocal(nrm[:, :], nrm[:, :]))
                at.link(TT(KVb, KVb, nrm[:, None, 0:BR].to_broadcast([128, KD, BR]), ALU.mult))
                at.link(RED(gpart[:, :], KVb, AXX, ALU.add))
                at.link(TT(gacc[:, :], gacc[:, :], gpart[:, :], ALU.add))
                TT(Qb, Qb, nrm[:, None, BR:].to_broadcast([128, KD, BR]), ALU.mult).then_inc(block_dve, 1)
            at.leave(NB)
            message(NB * KD + 1, 1, 4 * NB)
            at.link(TS(gacc[:, :], gacc[:, :], 1.0 / N, None, ALU.mult))

            dve.wait_ge(block_dve, 1 + NB)
            dve.wait_ge(q_stored, 1 + 16 * NB)
            at.link(v.memset(acc, 0.0))
            dve.wait_ge(lanes_here, 32)
            v.memset(PF[:, 0:1], -BIG)
            v.memset(PF[:, QC:], -BIG)
            v.tensor_copy(ends[:, 2, :], NL[:, 0:1].to_broadcast([128, H]))
            v.tensor_copy(ends[:, 3, :], NL[:, QC - 1:QC].to_broadcast([128, H]))
            TT(edge_pen[:, 0], NL, NL[:, 0:1].to_broadcast([128, QC]), ALU.is_equal)
            TT(edge_pen[:, 1], NL, NL[:, QC - 1:QC].to_broadcast([128, QC]), ALU.is_equal)
            at.link(TT(PF[:, 1:QC], NL[:, 1:QC], NL[:, 0:QC - 1], ALU.is_equal))
            TS(edge_pen, edge_pen, BIG, -BIG, ALU.mult, ALU.add)
            at.link(TS(PF[:, 1:QC], PF[:, 1:QC], BIG, -BIG, ALU.mult, ALU.add))
            for h in range(H):
                v.tensor_tensor_scan(FW[:, :, h], PF[:, 0:QC], ML[:, :, h], -BIG, ALU.add, ALU.max)
                last = v.tensor_tensor_scan(BW[:, ::-1, h], PF[:, 1:QC + 1][:, ::-1], ML[:, ::-1, h], -BIG, ALU.add, ALU.max)
            at.link(last)
            v.tensor_copy(ends[:, 0, :], FW[:, QC - 1, :])
            v.tensor_copy(ends[:, 1, :], BW[:, 0, :]).then_inc(ends_ready, 1)
            dve.wait_ge(ends_T, 1)
            eT = ps[5][0:H, :].rearrange("p (a l) -> p a l", a=4)
            joined, single, sf, sb_ = laneT[:, 0, :], laneT[:, 1, 0:128], laneT[:, 2, :], laneT[:, 3, :]
            lastN = laneT[:, 4, 0:128]
            v.memset(joined, -BIG)
            v.memset(sf[:, 0:1], -BIG)
            v.memset(sb_[:, 128:129], -BIG)
            at.link(v.tensor_copy(lastN, eT[:, 3]))
            TT(single, lastN, eT[:, 2], ALU.is_equal)
            at.link(TT(joined[:, 1:128], lastN[:, 0:127], eT[:, 2, 1:128], ALU.is_equal))
            TS(single, single, BIG, -BIG, ALU.mult, ALU.add)
            at.link(TS(joined[:, 1:128], joined[:, 1:128], BIG, -BIG, ALU.mult, ALU.add))
            TT(laneT[:, 5, 0:128], single, joined[:, 1:129], ALU.add)
            at.link(TT(lastN, single, joined[:, 0:128], ALU.add))
            v.tensor_tensor_scan(sf[:, 1:129], lastN, eT[:, 0], -BIG, ALU.add, ALU.max)
            at.link(v.tensor_tensor_scan(sb_[:, 0:128][:, ::-1], laneT[:, 5, 0:128][:, ::-1], eT[:, 1, ::-1], -BIG, ALU.add, ALU.max))
            TT(lastN, sf[:, 0:128], joined[:, 0:128], ALU.add)
            TT(laneT[:, 5, 0:128], sb_[:, 1:129], joined[:, 1:129], ALU.add).then_inc(carry_ready, 1)
            dve.wait_ge(carry_back, 1)
            at.link(v.tensor_copy(carry.rearrange("p a h -> p (a h)"), ps[6][:, 0:3 * H]))
            wide = lambda ap: ap.to_broadcast([128, QC, H])
            at.link(TT(FW, FW, BW, ALU.max))
            for d in range(2):
                at.link(TT(BW, wide(edge_pen[:, d, :, None]), wide(carry[:, None, d, :]), ALU.add))
                at.link(TT(FW, FW, BW, ALU.max))
            TT(FL[:, :, 0:H], ML, FW, ALU.subtract).then_inc(shift_ready, 1)
            at.link(v.tensor_copy(PF[:, 0:1], carry[:, 2, 0:1]))
            at.link(TS(FL[:, :, 2 * H:], PF[:, 0:QC, None], -0.5, None, ALU.is_lt))
            TT(FL[:, :, H:2 * H], FW, wide(FL[:, :, 2 * H:]), ALU.mult)
            dve.wait_ge(factor_act, 1)
            v.memset(edge_pen[:, 0, 0:1], 0.0).then_inc(factors_ready, 1)
            dve.wait_ge(factors_here, 16)
            dve.wait_ge(o_here, 16)
            r4 = RH[:, :, 0:HID].rearrange("p q (h d) -> p q h d", h=H)
            TT(RH[:, :, HID:HID + H], DN[:, :, :], FG[:, :, 0:H], ALU.mult)
            v.tensor_copy(RH[:, :, HID + H:], FG[:, :, H:])
            at.link(TT(r4, r4, FG[:, :, 0:H, None].to_broadcast([128, QC, H, DH]), ALU.mult))
            dve.wait_ge(consts, 6)
            with dve.Fori(0, SLOTS // 3) as i:
                for k in range(3):
                    s = 3 * i + k
                    n0 = dve.value_load(slot_i[0:1, 2, bass.ds(s, 1)], min_val=0, max_val=N - PR)
                    qq = dve.value_load(slot_i[0:1, 1, bass.ds(s, 1)], min_val=0, max_val=QC - 1)
                    if k == 0:
                        alone(dve, slot_pe, 1 + 3 * i)
                    TT(hot[:, k, :], iota_n[:, bass.ds(n0, PR)], ngf[:, bass.ds(qq, 1)].to_broadcast([128, PR]),
                       ALU.is_equal).then_inc(hot_ready, 1)
                for k in range(3):
                    s = 3 * i + k
                    t0 = dve.value_load(slot_i[0:1, 0, bass.ds(s, 1)], min_val=0, max_val=T - 1)
                    at_t = acc[:, bass.ds(t0, 1), :].rearrange("p a w -> p (a w)")
                    alone(dve, slot_dve, 1 + s)
                    dve.wait_ge(slot_pe, 1 + s + 1)
                    TT(at_t, at_t, ps[k][0:PR, 0:265], ALU.add).then_inc(slot_dve, 1)
            dve.wait_ge(slot_dve, 1 + SLOTS)
            has = acc[:, :, 264:265]
            wide = lambda ap: ap.to_broadcast([PR, T, H])
            at.link(TS(es[:, 1, :, 0:1], has, -1.0, 1.0, ALU.mult, ALU.add))
            at.link(TT(es[:, 0], esel[:, :, :], wide(es[:, 1, :, 0:1]), ALU.mult))
            at.link(TT(es[:, 1], es[:, 0], acc[:, :, HID + H:HID + 2 * H], ALU.add))
            TT(es[:, 0], esel[:, :, :], es[:, 1], ALU.subtract).then_inc(self_ready, 1)
            dve.wait_ge(self_act, 1)
            dve.wait_ge(xl2_here, 16)
            x4 = XL2[:, :, 0:HID].rearrange("p t (h d) -> p t h d", h=H)
            a4 = acc[:, :, 0:HID].rearrange("p t (h d) -> p t h d", h=H)
            per_head = lambda ap: ap[:, :, :, None].to_broadcast([PR, T, H, DH])
            TT(es[:, 1], es[:, 0], acc[:, :, HID:HID + H], ALU.add)
            at.link(TT(x4, x4, per_head(es[:, 0]), ALU.mult))
            at.link(TS(es[:, 1], es[:, 1], 1e-16, None, ALU.add))
            at.link(v.reciprocal(es[:, 0], es[:, 1]))
            at.link(TT(a4, a4, x4, ALU.add))
            TT(a4, a4, per_head(es[:, 0]), ALU.mult).then_inc(gnn_ready, 1)
            for b in range(NB):
                dve.wait_ge(gT_pe, b + 1)
                v.tensor_copy(gT[:, :, b * BR:b * BR + BR], ps[3 + b % 2][:, 0:2 * BR].rearrange("p (k r) -> p k r", k=2)).then_inc(gT_dve, 1)

            dve.wait_ge(ff_small, 16 * 8)
            TT(gwd[:, :], gw[:, :, 1], gw[:, :, 0], ALU.subtract)
            TT(b2s[:, 0], b2s[:, 0], b2s[:, 1], ALU.add)
            dve.wait_ge(ld_small, 32)
            at.link(v.memset(msk[:, :, :], 0.0))
            at.link(TT(b2s[:, 0], b2s[:, 0], b2s[:, 2], ALU.add))
            v.tensor_copy(gwb[:, :, :], gwd[:, :, None].to_broadcast([128, KD, 128])).then_inc(gate_ready, 1)
            with dve.Fori(0, NB) as b:
                at.enter(b, 1)
                alone(dve, y_dve, 1 + KD * b)
                for e in range(KD):
                    dve.wait_ge(x1_pe, KD * b + e + 1)
                    STT(x1T[:, e], qT[:, e], gacc[:, e:e + 1], ps[e % 2][:, 0:BR], ALU.mult, ALU.add).then_inc(x1_dve, 1)
                dve.wait_ge(mean_pe, b + 1)
                TT(x2T, x1T, ps[2][:, None, 0:BR].to_broadcast([128, KD, BR]), ALU.subtract).then_inc(cen_dve, 1)
                dve.wait_ge(dev_act, b + 1)
                at.link(v.reciprocal(nrm[:, 0:BR], nrm[:, 0:BR]))
                TT(x2T, x2T, nrm[:, None, 0:BR].to_broadcast([128, KD, BR]), ALU.mult).then_inc(x2_dve, 1)
                dve.wait_ge(gate_pe, b + 1)
                TS(msk[:, 0, :], ps[2][:, 0:BR], 0.0, None, ALU.is_le)
                TS(msk[:, 1, :], ps[2][:, 0:BR], 0.0, None, ALU.is_gt).then_inc(mask_dve, 1)
                alone(dve, mask_dve, 1 + b + 1)
                for j in range(8):
                    dve.wait_ge(h_pe, 12 * b + j + 1)
                    TT(hT[:, j], ps[j % 2][:, 0:BR], msk[:, j // 4, :], ALU.mult).then_inc(h_dve, 1)
                for e in range(KD):
                    dve.wait_ge(y_pe, KD * b + e + 1)
                    STT(yT[:, e], ps[e % 2][:, 0:BR], b2s[:, 0, e:e + 1], x1T[:, e], ALU.add, ALU.add).then_inc(y_dve, 1)
                alone(dve, out_stored, 1 + 16 * b)
                for k in range(2):
                    dve.wait_ge(yT_pe, 1 + 4 * b + 2 * k + 2)
                    v.tensor_copy(yrow[:, k, 512:], ps[5 + 2 * k][0:PR, :]).then_inc(yr_dve, 1)

        @block.tensor
        def _(pe):
            for s in (w_pe, kvq_pe, hT_pe, lr_pe, yT_pe, xT_pe, slot_pe):
                pe.sem_inc(s)
            mm = nc.tensor.matmul

            def chain(out_ap, pairs, start=True, stop=True):
                for n, (l, r) in enumerate(pairs):
                    last = mm(out_ap, l, r, start=start and n == 0, stop=stop and n == len(pairs) - 1)
                return last

            pe.wait_ge(dv, 1)
            pe.wait_ge(heads_f, 1)
            mm(ps[7][:, 0:ROWS], ones[0:1, :], heads[0:1], start=True, stop=True).then_inc(heads_bc, 1)
            pe.wait_ge(first_edges, 1)
            chain(ps[6][0:PR, 0:T], [(shiftA, ix[:, 2, 0:T]), (shiftB, ix[:, 2, 1:T + 1])]).then_inc(next_edges, 1)
            pe.wait_ge(unaligned, 1)
            mm(ps[5][0:PR, 0:T], before, ix[:, 7, 0:T], start=True, stop=True)
            mm(ps[5][0:PR, 16:16 + T], ones[0:PR, 0:PR], ix[:, 7, 0:T], start=True, stop=True).then_inc(unaligned_sums, 1)
            pe.wait_ge(hits, 1)
            chain(ps[4][:, 0:2 * QC], [p for t in range(T) for p in
                  ((stepR[:, t, :], hitA[:, t, :]), (onesb[:, :], hitB[:, t, :]))]).then_inc(group_counts, 1)

            pe.wait_ge(wd_ready, 1)
            with pe.Fori(0, NB) as b:
                for k in range(2):
                    for h in range(2):
                        if h == 0:
                            pe.wait_ge(xn_ready, 2 * b + k + 1)
                            alone(pe, xT_act, 1 + 2 * b)
                            alone(pe, xT_dve, 1 + 2 * b)
                        for c in range(4):
                            last = nc.tensor.transpose(ps[2 * k + h][:, c * PR:c * PR + PR],
                                                       wraw[0:PR, k, (4 * h + c) * 128:(4 * h + c) * 128 + 128], ident[0:PR, 0:PR])
                        last.then_inc(xT_pe, 1)
                alone(pe, xT_act, 1 + 2 * b + 2)
                alone(pe, xT_dve, 1 + 2 * b + 2)
                alone(pe, hT_act, 1 + b)
                for h in range(2):
                    last = chain(ps[4][:, h * BR:h * BR + BR], [(wd[:, k, h * 128:h * 128 + 128], xnTb[:, k, :]) for k in range(KD)])
                last.then_inc(hT_pe, 1)
                alone(pe, hT_act, 1 + b + 1)
                alone(pe, lr_dve, 1 + 2 * b)
                for k in range(2):
                    hb = [hTb[:, c, k * PR:k * PR + PR] for c in range(2)]
                    chain(ps[5 + k][0:PR, 0:HID], [(hb[c], wl[:, c, :]) for c in range(2)])
                    chain(ps[5 + k][0:PR, HID:], [(hb[c], wr[:, c, :]) for c in range(2)]).then_inc(lr_pe, 1)

            for w in range(3):
                with pe.Fori(0, KD // 2) as i:
                    for k in range(2):
                        alone(pe, w_ld[k], 16 * (w * KD // 2 + i + 1))
                        alone(pe, w_act, 1 + KD * w + 2 * i + (k - 1 if w else 0))
                        for c in range(KD):
                            last = nc.tensor.transpose(ps[2 * k + c // 4][:, (c % 4) * 128:(c % 4) * 128 + 128],
                                                       wraw[:, k, c * 128:c * 128 + 128], ident[:, :])
                        last.then_inc(w_pe, 1)

            pe.wait_ge(w_act, 1 + 3 * KD)

            with pe.Fori(0, NB) as b:
                alone(pe, xb_here, 16 * (b + 1))
                for e in range(KD):
                    k = e % 2
                    freed = KD * b + (0 if e < 2 else e - 1)
                    alone(pe, sq_act, 1 + freed)
                    alone(pe, kv_dve, 1 + freed)
                    for w, to in ((0, ps[k][:, 0:BR]), (1, ps[k][:, BR:2 * BR]), (2, ps[2 + k][:, 0:BR])):
                        last = chain(to, [(wt[:, w, c, e * 128:e * 128 + 128], XB[:, c, :]) for c in range(KD)])
                    last.then_inc(kvq_pe, 1)
                    for s in ([e - 1] if e else []) + ([e] if e == KD - 1 else []):
                        alone(pe, sq_act, 1 + KD * b + s + 1)
                        if s == 0:
                            alone(pe, norm_act, 1 + b)
                        last = mm(ps[4][:, 0:2 * BR], ones[:, :], sq[:, s % 2, :], start=s == 0, stop=s == KD - 1)
                        last.then_inc(sq_pe, 1)

            pe.wait_ge(ends_ready, 1)
            for i in range(4):
                last = nc.tensor.transpose(ps[5][0:H, i * 128:i * 128 + 128], ends[:, i, :], ident[:, :])
            last.then_inc(ends_T, 1)
            pe.wait_ge(carry_ready, 1)
            for i, a in enumerate((4, 5, 0)):
                last = nc.tensor.transpose(ps[6][:, i * H:i * H + H], laneT[:, a, 0:128], ident[0:H, 0:H])
            last.then_inc(carry_back, 1)
            pe.wait_ge(dv, 1)
            with pe.Fori(0, SLOTS // 3) as i:
                for k in range(3):
                    s = 3 * i + k
                    qq = pe.value_load(slot_i[0:1, 1, bass.ds(s, 1)], min_val=0, max_val=QC - 1)
                    alone(pe, slot_dve, 1 + 3 * i)
                    alone(pe, hot_ready, s + 1)
                    mm(ps[k][0:PR, 0:265], hot[:, k, :], RH[:, bass.ds(qq, 1), :].rearrange("p a w -> p (a w)"), start=True, stop=True).then_inc(slot_pe, 1)
            pe.wait_ge(gnn_ready, 1)
            for b in range(NB):
                if b >= 2:
                    pe.wait_ge(gT_dve, b - 1)
                for h in range(2):
                    for k in range(2):
                        last = nc.tensor.transpose(ps[3 + b % 2][:, h * BR + k * PR:h * BR + k * PR + PR],
                                                   acc[:, 2 * b + k, h * 128:h * 128 + 128], ident[0:PR, 0:PR])
                last.then_inc(gT_pe, 1)

            pe.wait_ge(gT_dve, NB)
            pe.wait_ge(ff_w, 16 * 7)
            pe.wait_ge(gate_ready, 1)
            with pe.Fori(0, NB) as b:
                alone(pe, xq_here, 32 * (b + 1))
                alone(pe, y_dve, 1 + KD * b)
                for e in range(KD):
                    if e >= 2:
                        alone(pe, x1_dve, 1 + KD * b + e - 1)
                    to = ps[e % 2]
                    cut = slice(e * 128, e * 128 + 128)
                    mm(to[:, 0:PR], xrow[:, 0, cut], ident[0:PR, 0:PR], start=True, stop=False)
                    mm(to[:, PR:BR], xrow[:, 1, cut], ident[0:PR, 0:PR], start=False, stop=False)
                    chain(to[:, 0:BR], [(wraw[:, k, cut], gT[:, k, bass.ds(b * BR, BR)]) for k in range(2)], start=False).then_inc(x1_pe, 1)
                alone(pe, x1_dve, 1 + KD * b + KD)
                alone(pe, mask_dve, 1 + b)
                chain(ps[2][:, 0:BR], [(avg[:, :], x1T[:, k]) for k in range(KD)]).then_inc(mean_pe, 1)
                alone(pe, sqr_act, b + 1)
                chain(ps[3][:, 0:BR], [(avg[:, :], sqT[:, k]) for k in range(KD)]).then_inc(var_pe, 1)
                alone(pe, x2_dve, 1 + b + 1)
                chain(ps[2][:, 0:BR], [(gwb[:, k, :], x2T[:, k]) for k in range(KD)]).then_inc(gate_pe, 1)
                for j in range(12):
                    x, c = j // 4, (j % 4) * 128
                    if 2 <= j < 10:
                        alone(pe, h_dve, 8 * b + j - 1)
                    elif j >= 10:
                        alone(pe, h_act, 12 * b + j - 1)
                    chain(ps[j % 2][:, 0:BR], [(w1s[:, x, k, c:c + 128], x2T[:, k]) for k in range(KD)]).then_inc(h_pe, 1)
                alone(pe, h_act, 12 * b + 12)
                for e in range(KD):
                    if e >= 2:
                        alone(pe, y_dve, 1 + KD * b + e - 1)
                    chain(ps[e % 2][:, 0:BR], [(w2s[:, j // 4, j % 4, e * 128:e * 128 + 128], hT[:, j]) for j in range(12)]).then_inc(y_pe, 1)
                alone(pe, y_dve, 1 + KD * b + KD)
                alone(pe, yr_act, 1 + 2 * b)
                alone(pe, yr_dve, 1 + 2 * b)
                for k in range(2):
                    for h in range(2):
                        for c in range(4):
                            last = nc.tensor.transpose(ps[4 + 2 * k + h][0:PR, c * 128:c * 128 + 128],
                                                       yT[:, 4 * h + c, k * PR:k * PR + PR], ident[:, :])
                        last.then_inc(yT_pe, 1)


_INS = ["x", "src", "dst", "L0_gnn_rms_w", "L0_gnn_W_down", "L0_gnn_Wl", "L0_gnn_Wr", "L0_gnn_att", "L0_gnn_W_up",
        "L0_mix_W_q", "L0_mix_W_k", "L0_mix_W_v", "L0_ffn_gate_w", "L0_ffn_w1", "L0_ffn_b1", "L0_ffn_w2",
        "L0_ffn_b2", "L0_ffn_sw1", "L0_ffn_sb1", "L0_ffn_sw2", "L0_ffn_sb2"]


def kernel(**inputs):
    import numpy as _np
    import concourse.bacc as _bacc
    from concourse import mybir as _mybir
    from concourse.bass_utils import run_bass_kernel_spmd as _run

    nc = _bacc.Bacc("TRN2", target_bir_lowering=False, num_devices=1)
    arrays, args = {}, []
    for name in _INS:
        a = _np.ascontiguousarray(inputs[name])
        arrays[f"in_{name}_dram"] = a
        args.append(nc.dram_tensor(f"in_{name}_dram", a.shape, _mybir.dt.from_np(a.dtype), kind="ExternalInput").ap())
    args.append(nc.dram_tensor("out_0_dram", (1250, 1024), _mybir.dt.float32, kind="ExternalOutput").ap())
    gps_layer(nc, *args)
    r = _run(nc, [arrays], core_ids=[0])
    return r.results[0]["out_0_dram"]
```

```python
import numpy as np
import concourse.bass as bass
from concourse import mybir
from contextlib import ExitStack


f32, i32, bf16 = mybir.dt.float32, mybir.dt.int32, mybir.dt.bfloat16
ALU = mybir.AluOpType
ACT = mybir.ActivationFunctionType
AXX = mybir.AxisListType.X

N, D, HID, H, E = 1250, 1024, 256, 4, 41250
DH = HID // H
PR, T = 125, 10
NB, BR = 5, 250
KD = D // 128
G = 10
BLOCKS = E // G
EP = E // PR
QC = -(-(BLOCKS + N) // 128)
SLOTS = QC + T - 1
ROW = 125
ROWS = E // ROW
FH = 512
XLW, XRW = HID + H, HID + 2 * H
ACT_J = 9
RING = 4
BIG = 1.0e30
RNE = 12582912.0
NEG_SLOPE = 0.2
assert E == BLOCKS * G == PR * EP == ROWS * ROW and EP % G == 0 and QC == NB * KD + 2


class Steps:

    def __init__(self, eng, sem):
        self.eng, self.sem, self.done, self.turn = eng, sem, 0, 0

    def add(self, ins):
        ins.then_inc(self.sem, 1)
        self.done += 1

    def wait(self):
        self.eng.wait_ge(self.sem, self.turn + self.done)

    def link(self, ins):
        self.add(ins)
        self.wait()

    def enter(self, i, per):
        self.start, self.per, self.done = self.done, per, 0
        self.turn = i * per + self.start

    def leave(self, times):
        assert self.done == self.per, (self.done, self.per)
        self.done, self.turn = self.start + times * self.per, 0


def gps_layer(nc, x, src, dst, rms_w, W_down, Wl, Wr, att, W_up, W_q, W_k, W_v,
              gate_w, w1, b1, w2, b2, sw1, sb1, sw2, sb2, out):
    dram = lambda name, shape, dt=f32: nc.dram_tensor(name, shape, dt, kind="Internal").ap()
    edge_tab = dram("edge_tab", (BLOCKS, 2 * G), i32)
    xl_tab = dram("xl_tab", (N, XLW))
    xr_tab = dram("xr_tab", (N, XRW))
    xnT_d = dram("xnT_d", (NB, 128, KD * BR))
    q_d = dram("q_d", (NB, 128, KD * BR))
    o_d = dram("o_d", (QC, 128, HID))
    m_d = dram("m_d", (QC * 128, H))
    n_d = dram("n_d", (QC * 128, 1))
    f_d = dram("f_d", (QC * 128, 9))

    with ExitStack() as ctx:
        sb = lambda name, shape, dt=f32: ctx.enter_context(nc.sbuf_tensor(name, shape, dt))
        sem = lambda name: ctx.enter_context(nc.semaphore(name))

        WT = sb("WT", [128, 3 * KD * D])
        arena = sb("arena", [128, RING * G * XLW + G * HID])
        blk = sb("blk", [128, 6500])
        wraw = sb("wraw", [128, 2, D])

        wt = WT[:, :].rearrange("p (w k e) -> p w k e", w=3, k=KD)
        w1s = WT[:, 0:3 * 4096].rearrange("p (e k h) -> p e k h", e=3, k=KD)
        w2s = WT[:, 3 * 4096:6 * 4096].rearrange("p (e k d) -> p e k d", e=3, k=4)
        def third(a, n):
            return WT[:, 2 * KD * D + a:2 * KD * D + a + n]
        cmp1 = third(0, T * ROWS)[0:PR].rearrange("p (t r) -> p t r", t=T)
        row_i = third(3300, T * ROW)[0:PR].bitcast(i32).rearrange("p (t r) -> p t r", t=T)
        src_sb = third(4550, EP)[0:PR].bitcast(i32)
        dst_sb = third(4880, EP)[0:PR].bitcast(i32)
        tab_sb = third(5210, 2 * EP)[0:PR].bitcast(i32).rearrange("p (b w) -> p b w", w=2 * G)
        stepR = third(5870, 640)[0:PR].bitcast(bf16).rearrange("p (t r) -> p t r", t=T)
        hitA = third(6510, 420)[0:PR].bitcast(bf16).rearrange("p (t q) -> p t q", t=T)
        hitB = third(6930, 420)[0:PR].bitcast(bf16).rearrange("p (t q) -> p t q", t=T)
        heads = third(7350, ROWS)[:, :]
        heads_i = third(7680, ROWS)[0:1].bitcast(i32)
        slot_c = third(0, SLOTS * (T - 1))[0:1].rearrange("p (s t) -> p s t", t=T - 1)
        def second(a, n):
            return WT[:, KD * D + a:KD * D + a + n]
        wd = second(0, 2048).rearrange("p (k h) -> p k h", k=KD)
        wl = second(2048, 512).rearrange("p (k h) -> p k h", k=2)
        wr = second(2560, 512).rearrange("p (k h) -> p k h", k=2)
        xnTb = second(3072, 2000).rearrange("p (k r) -> p k r", k=KD)
        tmpX = second(5072, 2560)[0:PR].rearrange("p (t h) -> p t h", t=T)
        shiftA, shiftB, before = (second(7632 + PR * i, PR)[0:PR] for i in range(3))
        x_all = arena[0:PR, 0:T * D].rearrange("p (t d) -> p t d", t=T)
        XLs = blk[0:PR, 0:T * XLW].rearrange("p (t w) -> p t w", t=T)
        XRs = blk[0:PR, 2600:2600 + T * XRW].rearrange("p (t w) -> p t w", t=T)
        hTb = blk[:, 5240:5740].rearrange("p (k r) -> p k r", k=2)
        XL = arena[:, 0:RING * G * XLW].rearrange("p (r j w) -> p r j w", r=RING, j=G)
        msg = arena[:, RING * G * XLW:].rearrange("p (j f) -> p j f", j=G)
        XB = blk[:, 0:2000].rearrange("p (k r) -> p k r", k=KD)
        KVb = blk[:, 2000:4000].rearrange("p (k r) -> p k r", k=KD)
        Qb = blk[:, 4000:6000].rearrange("p (k r) -> p k r", k=KD)
        RH = arena[:, 0:QC * 265].rearrange("p (q w) -> p q w", q=QC)
        acc = blk[0:PR, 0:T * 265].rearrange("p (t w) -> p t w", t=T)
        RH_END = QC * 265
        def lane(a, *shape):
            n = int(np.prod(shape))
            v = arena[:, RH_END + a:RH_END + a + n]
            return v.rearrange("p (j w) -> p j w", w=shape[1]) if len(shape) == 2 else v
        ML = lane(0, QC, H)
        NL = lane(168, QC)
        PF = lane(210, QC + 1)
        FW = lane(254, QC, H)
        BW = lane(422, QC, H)
        FL = lane(590, QC, 9)
        FG = lane(968, QC, 9)
        ends = lane(1346, 4, H)
        edge_pen = lane(1362, 2, QC)
        carry = lane(1446, 3, H)
        XL2 = blk[0:PR, 2650:2650 + T * XLW].rearrange("p (t w) -> p t w", t=T)
        iota_n = blk[:, 5250:5250 + N]
        xrow = arena[0:PR, 0:2 * D].rearrange("p (k d) -> p k d", k=2)
        qT = arena[:, 2048:4048].rearrange("p (k r) -> p k r", k=KD)
        sqT = qT
        gT = arena[:, 4048:4048 + 2 * N].rearrange("p (k r) -> p k r", k=2)
        rows8 = lambda ap: ap.rearrange("p (k r) -> p k r", k=KD)
        x1T = [rows8(arena[:, a:a + 2000]) for a in (6548, 8548)]
        x2T = [rows8(arena[:, 10548:12548]), rows8(blk[:, 0:2000])]
        hT = blk[:, 2000:5000].rearrange("p (j r) -> p j r", j=12)

        diff = sb("diff", [128, 128])
        ident = sb("ident", [128, 128])
        ones = sb("ones", [128, 128])
        onesb = sb("onesb", [PR, 128], bf16)
        cols = sb("cols", [128, 128])
        gid = sb("gid", [128, QC])
        nid = sb("nid", [PR, T])
        att8 = sb("att8", [128, HID])
        att2 = sb("att2", [128, HID])
        rmsw = sb("rmsw", [128, KD])
        ix = sb("ix", [PR, 16, 11])
        ridx = sb("ridx", [PR, T], i32)
        bidx = sb("bidx", [128, QC + 1], i32)
        nidx = sb("nidx", [128, QC], i32)
        ngf = sb("ngf", [128, QC])
        uns = sb("uns", [128, 2, QC])
        thr = sb("thr", [1, T - 1])
        slot_t = sb("slot_t", [1, SLOTS])
        slot_i = sb("slot_i", [1, SLOTS], i32)
        st = sb("st", [PR, 2, 2, 6])
        mv = sb("mv", [PR, 2, 2])
        vr = sb("vr", [PR, 3, 2, 2])
        es = sb("es", [PR, 2, T, H])
        esel = sb("esel", [PR, T, H])
        TAB = sb("TAB", [128, KD, 2 * G], i32)
        XR = sb("XR", [128, RING, XRW])
        bcol = sb("bcol", [128, KD], i32)
        ncol = sb("ncol", [128, RING], i32)
        pen = sb("pen", [128, RING, G])
        sc = sb("sc", [128, RING, G, H])
        mx = sb("mx", [128, 2, H])
        oo = sb("oo", [128, 2, HID])
        MR = sb("MR", [128, QC, H])
        DN = sb("DN", [128, QC, H])
        avg = sb("avg", [128, 128])
        eps = sb("eps", [128, 1])
        gw = sb("gw", [128, KD, 2])
        gwd = sb("gwd", [128, KD])
        b1s = sb("b1s", [128, 12])
        b2s = sb("b2s", [128, 3, KD])
        vb = sb("vb", [128, 2, BR])
        sq = sb("sq", [128, 2, 2 * BR])
        laneT = sq[:, :, :].rearrange("p a b -> p (a b)")[0:H, 0:774].rearrange("p (a l) -> p a l", a=6)
        part = sq[:, :, :].rearrange("p a b -> p (a b)").rearrange("p (k r) -> p k r", k=4)
        msk = vb[:, :, :]
        hot = vb[:, :, :].rearrange("p a b -> p (a b)")[:, 0:3 * PR].rearrange("p (k n) -> p k n", k=3)
        nrm = sb("nrm", [128, 2 * BR])
        gacc = sb("gacc", [128, KD])
        gpart = sb("gpart", [128, KD])

        yrow = [blk[0:PR, 5000:5000 + D].rearrange("p (k d) -> p k d", k=2),
                XR[0:PR, :, :].rearrange("p a b -> p (a b)")[:, 0:D].rearrange("p (k d) -> p k d", k=2)]

        ps = [ctx.enter_context(nc.psum_tensor(f"ps{i}", [128, 512], f32)) for i in range(8)]

        consts = sem("consts"); dv = sem("dv"); av = sem("av"); pl = sem("pl"); passed = sem("passed")
        ld_small = sem("ld_small"); ld_edges = sem("ld_edges"); ld_x = sem("ld_x"); ld_wd = sem("ld_wd")
        tab_ready = sem("tab_ready"); tab_stored = sem("tab_stored")
        heads_f = sem("heads_f"); heads_bc = sem("heads_bc"); rows_wanted = sem("rows_wanted")
        rows_here = sem("rows_here"); first_edges = sem("first_edges"); next_edges = sem("next_edges")
        unaligned = sem("unaligned"); unaligned_sums = sem("unaligned_sums"); hits = sem("hits")
        group_counts = sem("group_counts"); index_ready = sem("index_ready")
        wd_ready = sem("wd_ready"); var_ready = sem("var_ready"); std_ready = sem("std_ready")
        xn_ready = sem("xn_ready"); xT_pe = sem("xT_pe"); xT_act = sem("xT_act"); xT_dve = sem("xT_dve")
        xT_stored = sem("xT_stored"); hT_pe = sem("hT_pe"); hT_act = sem("hT_act"); lr_pe = sem("lr_pe")
        lr_dve = sem("lr_dve"); tabs_ready = sem("tabs_ready"); tabs_stored = sem("tabs_stored")
        w_ld = [sem("w_ld0"), sem("w_ld1")]
        w_pe = sem("w_pe"); w_act = sem("w_act")
        bcol_ready = sem("bcol_ready"); tab_here = [sem(f"tab_here{r}") for r in range(KD)]
        xl_here = [sem(f"xl_here{r}") for r in range(RING)]
        scores = sem("scores"); exps = sem("exps"); mul_act = sem("mul_act"); sums = sem("sums")
        o_stored = [sem("o_stored0"), sem("o_stored1")]
        xb_here = sem("xb_here"); kvq_pe = sem("kvq_pe"); sq_act = sem("sq_act")
        kv_dve = sem("kv_dve"); sq_pe = sem("sq_pe"); norm_act = sem("norm_act")
        block_dve = sem("block_dve"); q_stored = sem("q_stored")
        stats_stored = sem("stats_stored"); nodes_stored = sem("nodes_stored"); lanes_here = sem("lanes_here")
        ends_ready = sem("ends_ready"); ends_T = sem("ends_T"); carry_ready = sem("carry_ready")
        carry_back = sem("carry_back"); shift_ready = sem("shift_ready"); factor_act = sem("factor_act")
        factors_ready = sem("factors_ready"); factors_stored = sem("factors_stored")
        factors_here = sem("factors_here"); o_here = sem("o_here"); xl2_here = sem("xl2_here")
        hot_ready = sem("hot_ready"); apart = sem("apart"); rh_ready = sem("rh_ready"); slot_pe = sem("slot_pe"); slot_dve = sem("slot_dve")
        self_ready = sem("self_ready"); self_act = sem("self_act"); gnn_ready = sem("gnn_ready")
        gT_pe = sem("gT_pe"); gT_dve = sem("gT_dve")
        ff_w = sem("ff_w"); ff_small = sem("ff_small"); 
        xrow_here = sem("xrow_here"); q_here = sem("q_here"); slices_dve = sem("slices_dve"); x1_pe = sem("x1_pe"); x1_dve = sem("x1_dve"); mean_pe = sem("mean_pe")
        cen_dve = sem("cen_dve"); sqr_act = sem("sqr_act"); var_pe = sem("var_pe"); dev_act = sem("dev_act")
        x2_dve = sem("x2_dve"); gate_pe = sem("gate_pe"); mask_dve = sem("mask_dve"); h_pe = sem("h_pe")
        h_dve = sem("h_dve"); h_act = sem("h_act"); y_pe = sem("y_pe"); y_dve = sem("y_dve")
        yT_pe = sem("yT_pe"); yr_act = sem("yr_act"); yr_dve = sem("yr_dve"); out_stored = [sem("out_stored0"), sem("out_stored1")]

        block = ctx.enter_context(nc.Block())

        def alone(eng, s, value):
            eng.wait_ge(s, value)
            eng.sem_inc(passed)

        def chunk_of(slot, tile):
            return nc.s_assert_within(slot - tile, 0, QC - 1, skip_runtime_bounds_check_because=
                                      "tile t takes the slots from (its first chunk) + t up to (the next tile's) + t")

        @block.sync
        def _(sp):
            for s in (xT_stored, q_stored, *o_stored, *out_stored):
                sp.sem_inc(s)
            sp.dma_start(heads_i, dst[::ROW].rearrange("(a r) -> a r", a=1), allow_slow_non_contiguous=True).then_inc(ld_edges, 16)
            sp.dma_start(src_sb, src.rearrange("(p e) -> p e", p=PR)).then_inc(ld_edges, 16)
            sp.dma_start(dst_sb, dst.rearrange("(p e) -> p e", p=PR)).then_inc(ld_edges, 16)
            sp.dma_start(x_all, x.rearrange("(t p) d -> p t d", p=PR)).then_inc(ld_x, 16)
            sp.dma_start(att8[:, :], att.rearrange("h d -> (h d)").partition_broadcast(128)).then_inc(ld_small, 16)
            sp.dma_start(rmsw[:, :], rms_w.rearrange("(k p) -> p k", p=128), allow_slow_non_contiguous=True).then_inc(ld_small, 16)
            sp.dma_start(gw[:, :, 0], gate_w[0].rearrange("(k p) -> p k", p=128), allow_slow_non_contiguous=True).then_inc(ff_small, 16)
            sp.dma_start(gw[:, :, 1], gate_w[1].rearrange("(k p) -> p k", p=128), allow_slow_non_contiguous=True).then_inc(ff_small, 16)
            for e, (a, c) in enumerate(((b1[0], b2[0]), (b1[1], b2[1]), (sb1, sb2))):
                sp.dma_start(b1s[:, 4 * e:4 * e + 4], a.rearrange("(k p) -> p k", p=128), allow_slow_non_contiguous=True).then_inc(ff_small, 16)
                sp.dma_start(b2s[:, e], c.rearrange("(k p) -> p k", p=128), allow_slow_non_contiguous=True).then_inc(ff_small, 16)
            sp.dma_start(wd, W_down.rearrange("(k p) h -> p k h", p=128)).then_inc(ld_wd, 16)
            sp.dma_start(wl, Wl.rearrange("(k p) h -> p k h", p=128)).then_inc(ld_wd, 16)
            sp.dma_start(wr, Wr.rearrange("(k p) h -> p k h", p=128)).then_inc(ld_wd, 16)
            sp.wait_ge(tab_ready, 1)
            sp.dma_start(edge_tab.rearrange("(p b) w -> p b w", p=PR), tab_sb).then_inc(tab_stored, 16)
            sp.wait_ge(index_ready, 1)
            sp.dma_start(n_d.rearrange("(q p) a -> p (q a)", p=128), ngf[:, :], allow_slow_non_contiguous=True).then_inc(nodes_stored, 16)
            with sp.Fori(0, NB) as b:
                sp.wait_ge(xT_act, 1 + 2 * b + 2)
                sp.wait_ge(xT_dve, 1 + 2 * b + 2)
                sp.dma_start(xnT_d[bass.ds(b, 1)].rearrange("a p f -> (a p) f"),
                             xnTb.rearrange("p k r -> p (k r)")).then_inc(xT_stored, 16)
            sp.wait_ge(tabs_ready, 1)
            sp.dma_start(xl_tab.rearrange("(t p) w -> p t w", p=PR), XLs).then_inc(tabs_stored, 16)
            sp.dma_start(xr_tab.rearrange("(t p) w -> p t w", p=PR), XRs).then_inc(tabs_stored, 16)
            sp.wait_ge(xT_pe, 1 + 4 * NB)
            for w, W in enumerate((W_k, W_q, W_v)):
                with sp.Fori(0, KD // 2) as i:
                    for k in range(2):
                        if w == 0:
                            alone(sp, w_pe, 1 + 2 * i)
                        else:
                            alone(sp, w_pe, 1 + w * KD + 2 * i + k - 1)
                        sp.dma_start(wraw[:, k, :], W[bass.ds((2 * i + k) * 128, 128), :]).then_inc(w_ld[k], 16)
            sp.wait_ge(tabs_stored, 32)

            def load_x(b):
                sp.dma_start(XB.rearrange("p k r -> p (k r)"),
                             xnT_d[bass.ds(b, 1)].rearrange("a p f -> (a p) f")).then_inc(xb_here, 16)

            def store_chunk(q, e):
                alone(sp, sums, RING + q + 1)
                sp.dma_start(o_d[bass.ds(q, 1)].rearrange("a p f -> (a p) f"), oo[:, e % 2, :]).then_inc(o_stored[e % 2], 16)
                sp.dma_start(m_d[bass.ds(q * 128, 128), :],
                             MR[:, bass.ds(q, 1), :].rearrange("p a h -> p (a h)")).then_inc(stats_stored, 16)

            def edge_block(b, more):
                for e in range(KD):
                    store_chunk(KD * b + e, e)
                    if e == KD - 2 and more:
                        alone(sp, kvq_pe, 1 + KD * b + KD)
                        load_x(b + 1)
                alone(sp, block_dve, 1 + b + 1)
                sp.dma_start(q_d[bass.ds(b, 1)].rearrange("a p f -> (a p) f"),
                             Qb.rearrange("p k r -> p (k r)")).then_inc(q_stored, 16)

            load_x(0)
            with sp.Fori(0, NB - 1) as b:
                edge_block(b, True)
            edge_block(NB - 1, False)
            for q in range(NB * KD, QC):
                store_chunk(q, q)
            sp.dma_start(wraw[:, :, :], W_up.rearrange("(k p) d -> p k d", p=128)).then_inc(ff_w, 16)
            sp.wait_ge(stats_stored, 16 * QC)
            sp.wait_ge(nodes_stored, 16)
            sp.dma_start(ML, m_d.rearrange("(l j) h -> l j h", j=QC)).then_inc(lanes_here, 16)
            sp.dma_start(NL, n_d.rearrange("(l j) a -> l (j a)", j=QC)).then_inc(lanes_here, 16)
            sp.wait_ge(o_stored[0], 1 + 16 * (QC // 2))
            sp.wait_ge(o_stored[1], 1 + 16 * (QC // 2))
            sp.dma_start(RH[:, :, 0:HID], o_d.rearrange("q p f -> p q f")).then_inc(o_here, 16)
            sp.wait_ge(q_stored, 1 + 16 * NB)
            sp.dma_start(XL2, xl_tab.rearrange("(t p) w -> p t w", p=PR)).then_inc(xl2_here, 16)
            sp.wait_ge(factors_ready, 1)
            sp.dma_start(f_d.rearrange("(l j) w -> l j w", j=QC), FL).then_inc(factors_stored, 16)
            sp.wait_ge(factors_stored, 16)
            sp.dma_start(FG, f_d.rearrange("(q p) w -> p q w", p=128)).then_inc(factors_here, 16)
            sp.wait_ge(kvq_pe, 1 + NB * KD)
            for e, w in enumerate((w1[0], w1[1], sw1)):
                sp.dma_start(w1s[:, e], w.rearrange("(k p) h -> p k h", p=128)).then_inc(ff_w, 16)
            for e, w in enumerate((w2[0], w2[1], sw2)):
                sp.dma_start(w2s[:, e], w.rearrange("(k p) d -> p k d", p=128)).then_inc(ff_w, 16)
            def load_rows(b):
                sp.dma_start(xrow, x[bass.ds(b * BR, BR), :].rearrange("(k p) d -> p k d", p=PR)).then_inc(xrow_here, 16)

            def load_q(b):
                sp.dma_start(qT.rearrange("p k r -> p (k r)"),
                             q_d[bass.ds(b, 1)].rearrange("a p f -> (a p) f")).then_inc(q_here, 16)

            def store_rows(b):
                for h in range(2):
                    alone(sp, yr_act, 1 + 2 * b + h + 1)
                    alone(sp, yr_dve, 1 + 2 * b + h + 1)
                    sp.dma_start(out[bass.ds(b * BR, BR), h * 512:h * 512 + 512].rearrange("(k p) d -> p k d", p=PR),
                                 yrow[h]).then_inc(out_stored[h], 16)

            sp.wait_ge(slot_dve, 3 + SLOTS)
            load_rows(0)
            load_q(0)
            with sp.Fori(0, NB - 1) as b:
                alone(sp, x1_pe, KD * b + KD)
                load_rows(b + 1)
                alone(sp, slices_dve, 3 * b + 2)
                load_q(b + 1)
                store_rows(b)
            store_rows(NB - 1)
            for h in range(2):
                sp.wait_ge(out_stored[h], 1 + 16 * NB)


        @block.gpsimd
        def _(pool):
            g = nc.gpsimd
            at = Steps(pool, pl)
            g.memset(bidx[:, QC:], 0)
            g.memset(eps[:, :], 1e-5).then_inc(consts, 1)
            g.iota(diff[:, :], pattern=[[1, 128]], base=0, channel_multiplier=-1, allow_small_or_imprecise_dtypes=True).then_inc(consts, 1)
            g.iota(cols[:, :], pattern=[[1, 128]], base=0, channel_multiplier=0, allow_small_or_imprecise_dtypes=True).then_inc(consts, 1)
            g.iota(gid[:, :], pattern=[[128, QC]], base=0, channel_multiplier=1, allow_small_or_imprecise_dtypes=True).then_inc(consts, 1)
            g.iota(nid[:, :], pattern=[[PR, T]], base=0, channel_multiplier=1, allow_small_or_imprecise_dtypes=True).then_inc(consts, 1)
            pool.wait_ge(rows_wanted, 1)
            for t in range(T):
                g.indirect_dma_start(row_i[:, t, :], None, dst.rearrange("(r w) -> r w", w=ROW),
                                     bass.IndirectOffsetOnAxis(ridx[:, t:t + 1], 0)).then_inc(rows_here, 16)
            pool.wait_ge(index_ready, 1)
            pool.wait_ge(tab_stored, 16)
            pool.wait_ge(tabs_stored, 32)
            at.link(g.tensor_copy(bcol[:, 0:1], bidx[:, 0:1]))
            g.indirect_dma_start(TAB[:, 0, :], None, edge_tab[:, :],
                                 bass.IndirectOffsetOnAxis(bcol[:, 0:1], 0)).then_inc(tab_here[0], 16)

            def gather(q, e, uses, last=False):
                r, nxt = e % RING, (e + 1) % KD
                alone(pool, sums, RING + q + 1 - RING)
                if not last:
                    at.add(g.tensor_copy(bcol[:, nxt:nxt + 1], bidx[:, bass.ds(q + 1, 1)]))
                at.add(g.tensor_copy(ncol[:, r:r + 1], nidx[:, bass.ds(q, 1)]))
                alone(pool, pl, at.turn + at.done)
                if not last:
                    g.indirect_dma_start(TAB[:, nxt, :], None, edge_tab[:, :],
                                         bass.IndirectOffsetOnAxis(bcol[:, nxt:nxt + 1], 0)).then_inc(tab_here[nxt], 16)
                alone(pool, tab_here[e], 16 * uses)
                g.indirect_dma_start(XR[:, r, :], None, xr_tab[:, :],
                                     bass.IndirectOffsetOnAxis(ncol[:, r:r + 1], 0)).then_inc(xl_here[r], 16)
                for j in range(G):
                    g.indirect_dma_start(XL[:, r, j, :], None, xl_tab[:, :],
                                         bass.IndirectOffsetOnAxis(TAB[:, e, j:j + 1], 0)).then_inc(xl_here[r], 16)

            with pool.Fori(0, NB) as b:
                at.enter(b, 2 * KD)
                for e in range(KD):
                    gather(KD * b + e, e, b + 1)
            at.leave(NB)
            gather(NB * KD, 0, NB + 1)
            gather(NB * KD + 1, 1, NB + 1, last=True)
            pool.wait_ge(block_dve, 1 + NB)
            pool.wait_ge(q_stored, 1 + 16 * NB)
            g.iota(iota_n, pattern=[[1, N]], base=0, channel_multiplier=0, allow_small_or_imprecise_dtypes=True).then_inc(consts, 1)

        @block.scalar
        def _(act):
            for s in (xT_act, hT_act, w_act, sq_act, norm_act, yr_act):
                act.sem_inc(s)
            a = nc.scalar
            with act.Fori(0, NB) as b:
                act.wait_ge(var_ready, b + 1)
                a.activation(vr[:, 1], vr[:, 0], ACT.Sqrt).then_inc(std_ready, 1)
                alone(act, xT_stored, 1 + 16 * b)
                alone(act, hT_pe, 1 + b)
                for k in range(2):
                    act.wait_ge(xT_pe, 1 + 4 * b + 2 * k + 1)
                    a.copy(xnTb[:, 0:4, PR * k:PR * k + PR],
                           ps[2 * k][:, 0:4 * PR].rearrange("p (k r) -> p k r", k=4)).then_inc(xT_act, 1)
                alone(act, lr_pe, 1 + 2 * b)
                act.wait_ge(hT_pe, 1 + b + 1)
                a.copy(hTb, ps[4][:, 0:2 * BR].rearrange("p (k r) -> p k r", k=2)).then_inc(hT_act, 1)
            for w in range(3):
                if w == 1:
                    act.wait_ge(tabs_ready, 1)
                    act.wait_ge(xT_stored, 1 + 16 * NB)
                if w == 2:
                    act.wait_ge(index_ready, 1)
                    act.wait_ge(tab_stored, 16)
                with act.Fori(0, KD // 2) as i:
                    for k in range(2):
                        alone(act, w_pe, 1 + KD * w + 2 * i + k + 1)
                        for h in range(2):
                            last = a.copy(wt[:, w, 4 * h:4 * h + 4, bass.ds((2 * i + k) * 128, 128)],
                                          ps[2 * k + h][:, :].rearrange("p (k r) -> p k r", k=4))
                        last.then_inc(w_act, 1)

            def weigh(q, e):
                r = e % RING
                act.wait_ge(scores, q + 1)
                a.activation(sc[:, r], sc[:, r], ACT.Exp).then_inc(exps, 1)
                act.wait_ge(exps, q + 1)
                for j in range(ACT_J):
                    for h in range(H):
                        m = XL[:, r, j, h * DH:h * DH + DH]
                        last = a.mul(m, m, sc[:, r, j, h:h + 1])
                last.then_inc(mul_act, 1)

            weigh(0, 0)
            weigh(1, 1)
            with act.Fori(0, NB) as b:
                for e in range(KD):
                    u, k = KD * b + e, e % 2
                    if e == 0:
                        alone(act, block_dve, 1 + b)
                        alone(act, q_stored, 1 + 16 * b)
                    if e >= 2:
                        alone(act, kv_dve, 1 + u - 1)
                        alone(act, sq_pe, u - 1)
                    act.wait_ge(kvq_pe, 1 + u + 1)
                    a.copy(vb[:, k, :], ps[2 + k][:, 0:BR])
                    a.copy(Qb[:, e, :], ps[k][:, BR:2 * BR])
                    a.activation(sq[:, k, :], ps[k][:, 0:2 * BR], ACT.Square).then_inc(sq_act, 1)
                    if e == KD - 1:
                        act.wait_ge(sq_pe, KD * b + KD)
                        a.activation(nrm[:, :], ps[4][:, 0:2 * BR], ACT.Sqrt).then_inc(norm_act, 1)
                    weigh(u + 2, e + 2)
            act.wait_ge(shift_ready, 1)
            a.activation(FL[:, :, 0:H], FL[:, :, 0:H], ACT.Exp).then_inc(factor_act, 1)
            act.wait_ge(consts, 6)
            with act.Fori(0, SLOTS // 3) as i:
                for k in range(3):
                    s = 3 * i + k
                    t0 = act.value_load(slot_i[0:1, bass.ds(s, 1)], min_val=0, max_val=T - 1)
                    alone(act, slot_pe, 3 + s - 2)
                    a.activation(hot[:, k, :], iota_n[:, bass.ds(t0 * PR, PR)], ACT.Abs, scale=-1.0,
                                 bias=ngf[:, bass.ds(chunk_of(s, t0), 1)]).then_inc(apart, 1)
                    act.wait_ge(apart, s + 1)
                    a.activation(hot[:, k, :], hot[:, k, :], ACT.Relu, scale=-1.0, bias=ones[:, 0:1]).then_inc(hot_ready, 1)
            act.wait_ge(self_ready, 1)
            a.activation(es[:, 0], es[:, 0], ACT.Exp).then_inc(self_act, 1)
            act.wait_ge(ff_small, 16 * 8)

            def squares(b, odd):
                act.wait_ge(cen_dve, b + 1)
                a.activation(sqT, x2T[odd], ACT.Square).then_inc(sqr_act, 1)

            def deviations(b, first=False):
                if not first:
                    alone(act, x2_dve, b)
                act.wait_ge(var_pe, b + 1)
                a.activation(nrm[:, 0:BR], ps[2][:, 0:BR], ACT.Sqrt, bias=eps[:, :]).then_inc(dev_act, 1)

            def feed_forward(b, odd, more):
                for j in range(12):
                    if j < 8:
                        act.wait_ge(h_dve, 8 * b + j + 1)
                        a.activation(hT[:, j], hT[:, j], ACT.Relu, bias=b1s[:, j:j + 1]).then_inc(h_act, 1)
                    else:
                        act.wait_ge(h_pe, 12 * b + j + 1)
                        a.activation(hT[:, j], ps[j % 2][:, 0:BR], ACT.Relu, bias=b1s[:, j:j + 1]).then_inc(h_act, 1)
                if more:
                    squares(b + 1, 1 - odd)
                    deviations(b + 1)
                for h in range(2):
                    alone(act, out_stored[h], 1 + 16 * b)
                    act.wait_ge(yT_pe, 4 * b + 2 * h + 1)
                    a.copy(yrow[h][:, 0, :], ps[6][0:PR, :]).then_inc(yr_act, 1)

            squares(0, 0)
            deviations(0, first=True)
            with act.Fori(0, NB // 2) as i:
                for odd in range(2):
                    feed_forward(2 * i + odd, odd, True)
            feed_forward(NB - 1, 0, False)

        @block.vector
        def _(dve):
            for s in (block_dve, xT_dve, lr_dve, kv_dve, slot_dve, slot_dve, slot_dve, y_dve, yr_dve, *([sums] * RING)):
                dve.sem_inc(s)
            v = nc.vector
            at = Steps(dve, dv)
            bc = lambda ap, shape: ap.to_broadcast(shape)
            TT, TS, STT, RED = v.tensor_tensor, v.tensor_scalar, v.scalar_tensor_tensor, v.tensor_reduce

            v.memset(ones[:, :], 1.0)
            v.memset(onesb[:, :], 1.0)
            v.memset(avg[:, :], 1.0 / D)
            v.memset(gacc[:, :], 0.0)
            dve.wait_ge(consts, 5)
            TS(ident[:, :], diff[:, :], 0.0, None, ALU.is_equal)
            TS(shiftA, diff[0:PR, 0:PR], -1.0, None, ALU.is_equal)
            TS(shiftB, diff[0:PR, 0:PR], float(PR - 1), None, ALU.is_equal)
            at.add(TS(before, diff[0:PR, 0:PR], 1.0, None, ALU.is_ge))

            dve.wait_ge(ld_edges, 48)
            v.tensor_copy(heads[0:1], heads_i).then_inc(heads_f, 1)
            v.tensor_copy(tab_sb[:, :, 0:G], src_sb.rearrange("p (b j) -> p b j", j=G))
            v.tensor_copy(tab_sb[:, :, G:2 * G], dst_sb.rearrange("p (b j) -> p b j", j=G)).then_inc(tab_ready, 1)
            dve.wait_ge(heads_bc, 1)
            at.link(TT(cmp1, ps[7][0:PR, None, 0:ROWS].to_broadcast([PR, T, ROWS]),
                       nid[:, :, None].to_broadcast([PR, T, ROWS]), ALU.is_lt))
            at.link(RED(ix[:, 0, 0:T], cmp1, AXX, ALU.add))
            at.link(TS(ix[:, 1, 0:T], ix[:, 0, 0:T], -1.0, 0.0, ALU.add, ALU.max))
            v.tensor_copy(ridx[:, :], ix[:, 1, 0:T]).then_inc(rows_wanted, 1)
            dve.wait_ge(rows_here, 16 * T)
            at.link(TT(cmp1[:, :, 0:ROW], row_i, nid[:, :, None].to_broadcast([PR, T, ROW]), ALU.is_lt))
            v.memset(ix[:, 2, T:], float(E))
            at.link(RED(ix[:, 0, 0:T], cmp1[:, :, 0:ROW], AXX, ALU.add))
            STT(ix[:, 2, 0:T], ix[:, 1, 0:T], float(ROW), ix[:, 0, 0:T], ALU.mult, ALU.add).then_inc(first_edges, 1)
            dve.wait_ge(first_edges, 1)
            first = ix[:, 2, 0:T]

            def floor_div(to, a, d, margin, w):
                at.link(TS(ix[:, w, 0:T], a, 1.0 / d, -margin, ALU.mult, ALU.add))
                at.link(TS(to, ix[:, w, 0:T], RNE, -RNE, ALU.add, ALU.add))

            floor_div(ix[:, 4, 0:T], first, G, 0.45, 3)
            at.link(STT(ix[:, 5, 0:T], ix[:, 4, 0:T], -float(G), first, ALU.mult, ALU.add))
            at.link(TS(ix[:, 5, 0:T], ix[:, 5, 0:T], 0.5, None, ALU.is_gt))
            dve.wait_ge(next_edges, 1)
            at.link(TT(ix[:, 6, 0:T], ps[6][0:PR, 0:T], first, ALU.is_gt))
            TT(ix[:, 7, 0:T], ix[:, 5, 0:T], ix[:, 6, 0:T], ALU.mult).then_inc(unaligned, 1)
            at.link(TT(ix[:, 8, 0:T], ix[:, 4, 0:T], ix[:, 5, 0:T], ALU.add))
            dve.wait_ge(unaligned_sums, 1)
            at.add(v.memset(ix[:, 9, 0:T], 0.0))
            at.link(v.tensor_copy(ix[:, 11, 0:T], ps[5][0:PR, 16:16 + T]))
            at.link(v.tensor_tensor_scan(ix[:, 10, 0:T], ix[:, 11, 0:T], ix[:, 9, 0:T], 0.0, ALU.add, ALU.add))
            at.link(TT(ix[:, 10, 0:T], ix[:, 10, 0:T], ix[:, 11, 0:T], ALU.subtract))
            at.link(TT(ix[:, 10, 0:T], ix[:, 10, 0:T], ps[5][0:PR, 0:T], ALU.add))
            at.link(TT(ix[:, 8, 0:T], ix[:, 8, 0:T], ix[:, 10, 0:T], ALU.add))
            floor_div(ix[:, 12, 0:T], ix[:, 8, 0:T], 128, 0.498, 3)
            at.link(STT(ix[:, 13, 0:T], ix[:, 12, 0:T], -128.0, ix[:, 8, 0:T], ALU.mult, ALU.add))
            v.tensor_tensor(stepR, cols[0:PR, None, :].to_broadcast([PR, T, 128]),
                            ix[:, 13, 0:T, None].to_broadcast([PR, T, 128]), ALU.is_ge)
            TT(hitA[:, :, 0:QC], cols[0:PR, None, 0:QC].to_broadcast([PR, T, QC]),
               ix[:, 12, 0:T, None].to_broadcast([PR, T, QC]), ALU.is_equal)
            at.link(TT(hitB[:, :, 0:QC], cols[0:PR, None, 0:QC].to_broadcast([PR, T, QC]),
                       ix[:, 12, 0:T, None].to_broadcast([PR, T, QC]), ALU.is_gt))
            TT(hitA[:, :, QC:], hitA[:, :, 0:QC], ix[:, 7, 0:T, None].to_broadcast([PR, T, QC]), ALU.mult)
            TT(hitB[:, :, QC:], hitB[:, :, 0:QC], ix[:, 7, 0:T, None].to_broadcast([PR, T, QC]), ALU.mult).then_inc(hits, 1)
            at.link(TT(thr[:, :], ix[0:1, 12, 1:T], cols[0:1, 1:T], ALU.add))
            at.link(TT(slot_c, cols[0:1, 0:SLOTS, None].to_broadcast([1, SLOTS, T - 1]),
                       thr[:, None, :].to_broadcast([1, SLOTS, T - 1]), ALU.is_ge))
            at.link(RED(slot_t[:, :], slot_c, AXX, ALU.add))
            v.tensor_copy(slot_i[:, :], slot_t[:, :])
            dve.wait_ge(group_counts, 1)
            at.link(TT(uns[:, 0], gid[:, :], ps[4][:, QC:2 * QC], ALU.subtract))
            at.link(TS(uns[:, 1], uns[:, 0], BLOCKS - 0.5, None, ALU.is_lt))
            TS(bidx[:, 0:QC], uns[:, 0], float(BLOCKS - 1), None, ALU.min)
            at.link(TT(ngf[:, :], uns[:, 1], ps[4][:, 0:QC], ALU.mult))
            at.link(TS(ngf[:, :], ngf[:, :], -1.0, None, ALU.add))
            TS(nidx[:, :], ngf[:, :], 0.0, None, ALU.max).then_inc(index_ready, 1)

            dve.wait_ge(ld_small, 32)
            TS(att2[:, :], att8[:, :], NEG_SLOPE, None, ALU.mult)
            at.link(TS(att8[:, :], att8[:, :], 1.0 - NEG_SLOPE, None, ALU.mult))
            dve.wait_ge(ld_wd, 48)
            for k in range(KD):
                last = TS(wd[:, k, :], wd[:, k, :], rmsw[:, k:k + 1], None, ALU.mult)
            last.then_inc(wd_ready, 1)
            dve.wait_ge(ld_x, 16)
            xnb = wraw[0:PR]
            with dve.Fori(0, NB) as b:
                at.enter(b, 10)
                for k in range(2):
                    for h in range(2):
                        at.add(v.bn_stats(st[:, k, h, :], x_all[:, bass.ds(2 * b + k, 1), 512 * h:512 * h + 512].rearrange("p a d -> p (a d)")))
                alone(dve, dv, at.turn + at.done)
                for k in range(2):
                    at.add(v.bn_aggr(mv[:, k, :], st[:, k].rearrange("p a s -> p (a s)")))
                at.wait()
                at.link(TS(vr[:, 0, :, 0:1], mv[:, :, 1:2], 1e-5, None, ALU.add))
                at.link(v.reciprocal(vr[:, 2, :, 0:1], vr[:, 0, :, 0:1]))
                at.link(TT(vr[:, 2, :, 1:2], mv[:, :, 1:2], vr[:, 2, :, 0:1], ALU.mult))
                TS(vr[:, 0, :, 1:2], vr[:, 2, :, 1:2], 1e-6, None, ALU.add).then_inc(var_ready, 1)
                dve.wait_ge(std_ready, b + 1)
                at.link(v.reciprocal(vr[:, 2], vr[:, 1]))
                alone(dve, xT_pe, 1 + 4 * b)
                for k in range(2):
                    TS(xnb[:, k, :], x_all[:, bass.ds(2 * b + k, 1), :].rearrange("p a d -> p (a d)"), mv[:, k, 0:1], vr[:, 2, k, 0:1],
                       ALU.subtract, ALU.mult).then_inc(xn_ready, 1)
                alone(dve, xT_stored, 1 + 16 * b)
                alone(dve, hT_pe, 1 + b)
                for k in range(2):
                    dve.wait_ge(xT_pe, 1 + 4 * b + 2 * k + 2)
                    v.tensor_copy(xnTb[:, 4:8, PR * k:PR * k + PR],
                                  ps[2 * k + 1][:, 0:4 * PR].rearrange("p (k r) -> p k r", k=4)).then_inc(xT_dve, 1)
                for k in range(2):
                    dve.wait_ge(lr_pe, 1 + 2 * b + k + 1)
                    TS(XLs[:, bass.ds(2 * b + k, 1), 0:HID].rearrange("p a d -> p (a d)"), ps[5 + k][0:PR, 0:HID], vr[:, 2, k, 1:2], None, ALU.mult)
                    TS(XRs[:, bass.ds(2 * b + k, 1), 0:HID].rearrange("p a d -> p (a d)"), ps[5 + k][0:PR, HID:], vr[:, 2, k, 1:2], None, ALU.mult).then_inc(lr_dve, 1)
            at.leave(NB)
            heads_view = lambda ap: ap.rearrange("p t (h d) -> p t h d", h=H)
            all_t = lambda ap: ap[:, None, :].to_broadcast([PR, T, HID])
            dve.wait_ge(lr_dve, 1 + 2 * NB)
            at.link(TT(tmpX, XLs[:, :, 0:HID], all_t(att2[0:PR]), ALU.mult))
            at.link(RED(XLs[:, :, HID:], heads_view(tmpX), AXX, ALU.add))
            at.link(TT(tmpX, XRs[:, :, 0:HID], all_t(att2[0:PR]), ALU.mult))
            at.link(RED(XRs[:, :, HID:HID + H], heads_view(tmpX), AXX, ALU.add))
            at.link(TT(tmpX, XRs[:, :, 0:HID], XLs[:, :, 0:HID], ALU.add))
            at.link(STT(tmpX, tmpX, 0.0, all_t(att8[0:PR]), ALU.max, ALU.mult))
            at.link(RED(es[:, 0], heads_view(tmpX), AXX, ALU.add))
            at.link(TT(es[:, 1], XLs[:, :, HID:], XRs[:, :, HID:HID + H], ALU.add))
            at.link(TT(esel[:, :, :], es[:, 0], es[:, 1], ALU.add))
            v.tensor_copy(XRs[:, :, HID + H:], esel[:, :, :]).then_inc(tabs_ready, 1)

            def score(q, e, uses):
                r = e % RING
                s = sc[:, r]
                dve.wait_ge(xl_here[r], 16 * (G + 1) * uses)
                at.add(TT(pen[:, r, :], TAB[:, e % KD, G:2 * G], ngf[:, bass.ds(q, 1)].to_broadcast([128, G]), ALU.is_equal))
                at.link(TT(msg, XL[:, r, :, 0:HID], XR[:, r, None, 0:HID].to_broadcast([128, G, HID]), ALU.add))
                at.add(TS(pen[:, r, :], pen[:, r, :], BIG, -BIG, ALU.mult, ALU.add))
                at.link(STT(msg, msg, 0.0, att8[:, None, :].to_broadcast([128, G, HID]), ALU.max, ALU.mult))
                at.link(RED(s, msg.rearrange("p j (h d) -> p j h d", h=H), AXX, ALU.add))
                at.link(TT(s, s, XL[:, r, :, HID:], ALU.add))
                at.link(TT(s, s, XR[:, r, None, HID:HID + H].to_broadcast([128, G, H]), ALU.add))
                at.link(TT(s, s, pen[:, r, :, None].to_broadcast([128, G, H]), ALU.add))
                at.link(RED(mx[:, 0], s.rearrange("p j h -> p h j"), AXX, ALU.max))
                at.add(TT(MR[:, bass.ds(q, 1), :].rearrange("p a h -> p (a h)"), mx[:, 0], XR[:, r, HID + H:], ALU.max))
                at.link(TT(mx[:, 1], mx[:, 0], XR[:, r, HID + H:], ALU.max))
                TT(s, s, mx[:, None, 1].to_broadcast([128, G, H]), ALU.subtract).then_inc(scores, 1)

            def message(q, e, stored):
                r = e % RING
                x = XL[:, r, :, 0:HID]
                y = x[:, ACT_J:].rearrange("p j (h d) -> p j h d", h=H)
                dve.wait_ge(exps, q + 1)
                at.add(TT(y, y, sc[:, r, ACT_J:, :, None].to_broadcast([128, G - ACT_J, H, DH]), ALU.mult))
                at.link(RED(DN[:, bass.ds(q, 1), :].rearrange("p a h -> p (a h)"), sc[:, r].rearrange("p j h -> p h j"),
                            AXX, ALU.add))
                dve.wait_ge(mul_act, q + 1)
                at.link(TT(x[:, 0:5], x[:, 0:5], x[:, 5:10], ALU.add))
                at.link(TT(x[:, 0:2], x[:, 0:2], x[:, 2:4], ALU.add))
                at.link(TT(x[:, 0], x[:, 0], x[:, 1], ALU.add))
                dve.wait_ge(o_stored[e % 2], 1 + 16 * stored)
                TT(oo[:, e % 2, :], x[:, 0], x[:, 4], ALU.add).then_inc(sums, 1)

            score(0, 0, 1)
            score(1, 1, 1)
            message(0, 0, 0)
            with dve.Fori(0, NB) as b:
                at.enter(b, KD * 16 + 5)
                for e in range(KD):
                    u = KD * b + e
                    score(u + 2, e + 2, 2 * b + (e + 2) // RING + 1)
                    message(u + 1, e + 1, 4 * b + (e + 1) // 2)
                    if e == 0:
                        alone(dve, block_dve, 1 + b)
                    dve.wait_ge(sq_act, 1 + u + 1)
                    TT(KVb[:, e, :], ps[e % 2][:, 0:BR], vb[:, e % 2, :], ALU.mult).then_inc(kv_dve, 1)
                dve.wait_ge(norm_act, 1 + b + 1)
                at.link(TS(nrm[:, :], nrm[:, :], 1e-12, None, ALU.max))
                at.link(v.reciprocal(nrm[:, :], nrm[:, :]))
                at.link(TT(KVb, KVb, nrm[:, None, 0:BR].to_broadcast([128, KD, BR]), ALU.mult))
                at.link(RED(gpart[:, :], KVb, AXX, ALU.add))
                at.link(TT(gacc[:, :], gacc[:, :], gpart[:, :], ALU.add))
                TT(Qb, Qb, nrm[:, None, BR:].to_broadcast([128, KD, BR]), ALU.mult).then_inc(block_dve, 1)
            at.leave(NB)
            message(NB * KD + 1, 1, 4 * NB)
            at.link(TS(gacc[:, :], gacc[:, :], 1.0 / N, None, ALU.mult))

            dve.wait_ge(block_dve, 1 + NB)
            dve.wait_ge(q_stored, 1 + 16 * NB)
            at.link(v.memset(acc, 0.0))
            dve.wait_ge(lanes_here, 32)
            v.memset(PF[:, 0:1], -BIG)
            v.memset(PF[:, QC:], -BIG)
            v.tensor_copy(ends[:, 2, :], NL[:, 0:1].to_broadcast([128, H]))
            v.tensor_copy(ends[:, 3, :], NL[:, QC - 1:QC].to_broadcast([128, H]))
            TT(edge_pen[:, 0], NL, NL[:, 0:1].to_broadcast([128, QC]), ALU.is_equal)
            TT(edge_pen[:, 1], NL, NL[:, QC - 1:QC].to_broadcast([128, QC]), ALU.is_equal)
            at.link(TT(PF[:, 1:QC], NL[:, 1:QC], NL[:, 0:QC - 1], ALU.is_equal))
            TS(edge_pen, edge_pen, BIG, -BIG, ALU.mult, ALU.add)
            at.link(TS(PF[:, 1:QC], PF[:, 1:QC], BIG, -BIG, ALU.mult, ALU.add))
            for h in range(H):
                v.tensor_tensor_scan(FW[:, :, h], PF[:, 0:QC], ML[:, :, h], -BIG, ALU.add, ALU.max)
                last = v.tensor_tensor_scan(BW[:, ::-1, h], PF[:, 1:QC + 1][:, ::-1], ML[:, ::-1, h], -BIG, ALU.add, ALU.max)
            at.link(last)
            v.tensor_copy(ends[:, 0, :], FW[:, QC - 1, :])
            v.tensor_copy(ends[:, 1, :], BW[:, 0, :]).then_inc(ends_ready, 1)
            dve.wait_ge(ends_T, 1)
            eT = ps[5][0:H, :].rearrange("p (a l) -> p a l", a=4)
            joined, single, sf, sb_ = laneT[:, 0, :], laneT[:, 1, 0:128], laneT[:, 2, :], laneT[:, 3, :]
            lastN = laneT[:, 4, 0:128]
            v.memset(joined, -BIG)
            v.memset(sf[:, 0:1], -BIG)
            v.memset(sb_[:, 128:129], -BIG)
            at.link(v.tensor_copy(lastN, eT[:, 3]))
            TT(single, lastN, eT[:, 2], ALU.is_equal)
            at.link(TT(joined[:, 1:128], lastN[:, 0:127], eT[:, 2, 1:128], ALU.is_equal))
            TS(single, single, BIG, -BIG, ALU.mult, ALU.add)
            at.link(TS(joined[:, 1:128], joined[:, 1:128], BIG, -BIG, ALU.mult, ALU.add))
            TT(laneT[:, 5, 0:128], single, joined[:, 1:129], ALU.add)
            at.link(TT(lastN, single, joined[:, 0:128], ALU.add))
            v.tensor_tensor_scan(sf[:, 1:129], lastN, eT[:, 0], -BIG, ALU.add, ALU.max)
            at.link(v.tensor_tensor_scan(sb_[:, 0:128][:, ::-1], laneT[:, 5, 0:128][:, ::-1], eT[:, 1, ::-1], -BIG, ALU.add, ALU.max))
            TT(lastN, sf[:, 0:128], joined[:, 0:128], ALU.add)
            TT(laneT[:, 5, 0:128], sb_[:, 1:129], joined[:, 1:129], ALU.add).then_inc(carry_ready, 1)
            dve.wait_ge(carry_back, 1)
            at.link(v.tensor_copy(carry.rearrange("p a h -> p (a h)"), ps[6][:, 0:3 * H]))
            wide = lambda ap: ap.to_broadcast([128, QC, H])
            at.link(TT(FW, FW, BW, ALU.max))
            for d in range(2):
                at.link(TT(BW, wide(edge_pen[:, d, :, None]), wide(carry[:, None, d, :]), ALU.add))
                at.link(TT(FW, FW, BW, ALU.max))
            TT(FL[:, :, 0:H], ML, FW, ALU.subtract).then_inc(shift_ready, 1)
            at.link(v.tensor_copy(PF[:, 0:1], carry[:, 2, 0:1]))
            at.link(TS(FL[:, :, 2 * H:], PF[:, 0:QC, None], -0.5, None, ALU.is_lt))
            TT(FL[:, :, H:2 * H], FW, wide(FL[:, :, 2 * H:]), ALU.mult)
            dve.wait_ge(factor_act, 1)
            v.memset(edge_pen[:, 0, 0:1], 0.0).then_inc(factors_ready, 1)
            dve.wait_ge(factors_here, 16)
            dve.wait_ge(o_here, 16)
            r4 = RH[:, :, 0:HID].rearrange("p q (h d) -> p q h d", h=H)
            TT(RH[:, :, HID:HID + H], DN[:, :, :], FG[:, :, 0:H], ALU.mult)
            v.tensor_copy(RH[:, :, HID + H:], FG[:, :, H:])
            TT(r4, r4, FG[:, :, 0:H, None].to_broadcast([128, QC, H, DH]), ALU.mult).then_inc(rh_ready, 1)
            with dve.Fori(0, SLOTS // 3) as i:
                for k in range(3):
                    s = 3 * i + k
                    t0 = dve.value_load(slot_i[0:1, bass.ds(s, 1)], min_val=0, max_val=T - 1)
                    at_t = acc[:, bass.ds(t0, 1), :].rearrange("p a w -> p (a w)")
                    alone(dve, slot_dve, 3 + s)
                    dve.wait_ge(slot_pe, 3 + s + 1)
                    TT(at_t, at_t, ps[k][0:PR, 0:265], ALU.add).then_inc(slot_dve, 1)
            dve.wait_ge(slot_dve, 3 + SLOTS)
            has = acc[:, :, 264:265]
            wide = lambda ap: ap.to_broadcast([PR, T, H])
            at.link(TS(es[:, 1, :, 0:1], has, -1.0, 1.0, ALU.mult, ALU.add))
            at.link(TT(es[:, 0], esel[:, :, :], wide(es[:, 1, :, 0:1]), ALU.mult))
            at.link(TT(es[:, 1], es[:, 0], acc[:, :, HID + H:HID + 2 * H], ALU.add))
            TT(es[:, 0], esel[:, :, :], es[:, 1], ALU.subtract).then_inc(self_ready, 1)
            dve.wait_ge(self_act, 1)
            dve.wait_ge(xl2_here, 16)
            x4 = XL2[:, :, 0:HID].rearrange("p t (h d) -> p t h d", h=H)
            a4 = acc[:, :, 0:HID].rearrange("p t (h d) -> p t h d", h=H)
            per_head = lambda ap: ap[:, :, :, None].to_broadcast([PR, T, H, DH])
            TT(es[:, 1], es[:, 0], acc[:, :, HID:HID + H], ALU.add)
            at.link(TT(x4, x4, per_head(es[:, 0]), ALU.mult))
            at.link(TS(es[:, 1], es[:, 1], 1e-16, None, ALU.add))
            at.link(v.reciprocal(es[:, 0], es[:, 1]))
            at.link(TT(a4, a4, x4, ALU.add))
            TT(a4, a4, per_head(es[:, 0]), ALU.mult).then_inc(gnn_ready, 1)
            for b in range(NB):
                dve.wait_ge(gT_pe, b + 1)
                v.tensor_copy(gT[:, :, b * BR:b * BR + BR], ps[3 + b % 2][:, 0:2 * BR].rearrange("p (k r) -> p k r", k=2)).then_inc(gT_dve, 1)

            dve.wait_ge(ff_small, 16 * 8)
            TT(gwd[:, :], gw[:, :, 1], gw[:, :, 0], ALU.subtract)
            at.link(TT(b2s[:, 0], b2s[:, 0], b2s[:, 1], ALU.add))
            at.link(TT(b2s[:, 0], b2s[:, 0], b2s[:, 2], ALU.add))

            def residual(b, odd, e):
                dve.wait_ge(x1_pe, KD * b + e + 1)
                STT(x1T[odd][:, e], qT[:, e], gacc[:, e:e + 1], ps[3 + e % 2][:, 0:BR], ALU.mult, ALU.add).then_inc(x1_dve, 1)

            def add_slices(s):
                at.link(TT(part, s[:, 0:4], s[:, 4:8], ALU.add))
                at.link(TT(part[:, 0:2], part[:, 0:2], part[:, 2:4], ALU.add))
                TT(part[:, 0], part[:, 0], part[:, 1], ALU.add).then_inc(slices_dve, 1)

            def centre(b, odd):
                dve.wait_ge(x1_dve, KD * b + KD)
                add_slices(x1T[odd])
                dve.wait_ge(mean_pe, b + 1)
                TT(x2T[odd], x1T[odd], ps[5][:, None, 0:BR].to_broadcast([128, KD, BR]), ALU.subtract).then_inc(cen_dve, 1)

            def sum_squares(b):
                dve.wait_ge(sqr_act, b + 1)
                add_slices(sqT)

            def normalise(b, odd):
                dve.wait_ge(dev_act, b + 1)
                at.link(v.reciprocal(nrm[:, 0:BR], nrm[:, 0:BR]))
                TT(x2T[odd], x2T[odd], nrm[:, None, 0:BR].to_broadcast([128, KD, BR]), ALU.mult).then_inc(x2_dve, 1)

            def gate_sums(b, odd):
                dve.wait_ge(x2_dve, b + 1)
                at.link(TS(part[:, 0], x2T[odd][:, 0], gwd[:, 0:1], None, ALU.mult))
                for k in range(1, KD):
                    ins = STT(part[:, 0], x2T[odd][:, k], gwd[:, k:k + 1], part[:, 0], ALU.mult, ALU.add)
                    if k < KD - 1:
                        at.link(ins)
                ins.then_inc(slices_dve, 1)

            def masks(b, hidden):
                if hidden is not None:
                    alone(dve, h_dve, hidden)
                dve.wait_ge(gate_pe, b + 1)
                TS(msk[:, 0, :], ps[5][:, 0:BR], 0.0, None, ALU.is_le)
                TS(msk[:, 1, :], ps[5][:, 0:BR], 0.0, None, ALU.is_gt).then_inc(mask_dve, 1)

            def feed_forward(b, odd, more):
                alone(dve, mask_dve, b + 1)
                for j in range(8):
                    dve.wait_ge(h_pe, 12 * b + j + 1)
                    TT(hT[:, j], ps[j % 2][:, 0:BR], msk[:, j // 4, :], ALU.mult).then_inc(h_dve, 1)
                    if more:
                        if j == 0:
                            alone(dve, q_here, 16 * (b + 2))
                        residual(b + 1, 1 - odd, j)
                if more:
                    centre(b + 1, 1 - odd)
                    sum_squares(b + 1)
                for e in range(KD):
                    dve.wait_ge(y_pe, KD * b + e + 1)
                    STT(x1T[odd][:, e], ps[e % 2][:, 0:BR], b2s[:, 0, e:e + 1], x1T[odd][:, e], ALU.add, ALU.add).then_inc(y_dve, 1)
                    if more and e == 0:
                        normalise(b + 1, 1 - odd)
                    if more and e == 1:
                        gate_sums(b + 1, 1 - odd)
                    if more and e == 3:
                        masks(b + 1, 8 * b + 8)
                for h in range(2):
                    alone(dve, out_stored[h], 1 + 16 * b)
                    dve.wait_ge(yT_pe, 4 * b + 2 * h + 2)
                    v.tensor_copy(yrow[h][:, 1, :], ps[7][0:PR, :]).then_inc(yr_dve, 1)

            dve.wait_ge(q_here, 16)
            for e in range(KD):
                residual(0, 0, e)
            centre(0, 0)
            sum_squares(0)
            normalise(0, 0)
            gate_sums(0, 0)
            masks(0, None)
            with dve.Fori(0, NB // 2) as i:
                at.enter(i, 2 * 12)
                for odd in range(2):
                    feed_forward(2 * i + odd, odd, True)
            at.leave(NB // 2)
            feed_forward(NB - 1, 0, False)

        @block.tensor
        def _(pe):
            for s in (w_pe, kvq_pe, hT_pe, lr_pe, xT_pe, slot_pe, slot_pe, slot_pe):
                pe.sem_inc(s)
            mm = nc.tensor.matmul

            def chain(out_ap, pairs, start=True, stop=True):
                for n, (l, r) in enumerate(pairs):
                    last = mm(out_ap, l, r, start=start and n == 0, stop=stop and n == len(pairs) - 1)
                return last

            pe.wait_ge(dv, 1)
            pe.wait_ge(heads_f, 1)
            mm(ps[7][:, 0:ROWS], ones[0:1, :], heads[0:1], start=True, stop=True).then_inc(heads_bc, 1)
            pe.wait_ge(first_edges, 1)
            chain(ps[6][0:PR, 0:T], [(shiftA, ix[:, 2, 0:T]), (shiftB, ix[:, 2, 1:T + 1])]).then_inc(next_edges, 1)
            pe.wait_ge(unaligned, 1)
            mm(ps[5][0:PR, 0:T], before, ix[:, 7, 0:T], start=True, stop=True)
            mm(ps[5][0:PR, 16:16 + T], ones[0:PR, 0:PR], ix[:, 7, 0:T], start=True, stop=True).then_inc(unaligned_sums, 1)
            pe.wait_ge(hits, 1)
            chain(ps[4][:, 0:2 * QC], [p for t in range(T) for p in
                  ((stepR[:, t, :], hitA[:, t, :]), (onesb[:, :], hitB[:, t, :]))]).then_inc(group_counts, 1)

            pe.wait_ge(wd_ready, 1)
            with pe.Fori(0, NB) as b:
                for k in range(2):
                    for h in range(2):
                        if h == 0:
                            pe.wait_ge(xn_ready, 2 * b + k + 1)
                            alone(pe, xT_act, 1 + 2 * b)
                            alone(pe, xT_dve, 1 + 2 * b)
                        for c in range(4):
                            last = nc.tensor.transpose(ps[2 * k + h][:, c * PR:c * PR + PR],
                                                       wraw[0:PR, k, (4 * h + c) * 128:(4 * h + c) * 128 + 128], ident[0:PR, 0:PR])
                        last.then_inc(xT_pe, 1)
                alone(pe, xT_act, 1 + 2 * b + 2)
                alone(pe, xT_dve, 1 + 2 * b + 2)
                alone(pe, hT_act, 1 + b)
                for h in range(2):
                    last = chain(ps[4][:, h * BR:h * BR + BR], [(wd[:, k, h * 128:h * 128 + 128], xnTb[:, k, :]) for k in range(KD)])
                last.then_inc(hT_pe, 1)
                alone(pe, hT_act, 1 + b + 1)
                alone(pe, lr_dve, 1 + 2 * b)
                for k in range(2):
                    hb = [hTb[:, c, k * PR:k * PR + PR] for c in range(2)]
                    chain(ps[5 + k][0:PR, 0:HID], [(hb[c], wl[:, c, :]) for c in range(2)])
                    chain(ps[5 + k][0:PR, HID:], [(hb[c], wr[:, c, :]) for c in range(2)]).then_inc(lr_pe, 1)

            for w in range(3):
                with pe.Fori(0, KD // 2) as i:
                    for k in range(2):
                        alone(pe, w_ld[k], 16 * (w * KD // 2 + i + 1))
                        alone(pe, w_act, 1 + KD * w + 2 * i + (k - 1 if w else 0))
                        for c in range(KD):
                            last = nc.tensor.transpose(ps[2 * k + c // 4][:, (c % 4) * 128:(c % 4) * 128 + 128],
                                                       wraw[:, k, c * 128:c * 128 + 128], ident[:, :])
                        last.then_inc(w_pe, 1)

            pe.wait_ge(w_act, 1 + 3 * KD)

            with pe.Fori(0, NB) as b:
                alone(pe, xb_here, 16 * (b + 1))
                for e in range(KD):
                    k = e % 2
                    freed = KD * b + (0 if e < 2 else e - 1)
                    alone(pe, sq_act, 1 + freed)
                    alone(pe, kv_dve, 1 + freed)
                    for w, to in ((0, ps[k][:, 0:BR]), (1, ps[k][:, BR:2 * BR]), (2, ps[2 + k][:, 0:BR])):
                        last = chain(to, [(wt[:, w, c, e * 128:e * 128 + 128], XB[:, c, :]) for c in range(KD)])
                    last.then_inc(kvq_pe, 1)
                    for s in ([e - 1] if e else []) + ([e] if e == KD - 1 else []):
                        alone(pe, sq_act, 1 + KD * b + s + 1)
                        if s == 0:
                            alone(pe, norm_act, 1 + b)
                        last = mm(ps[4][:, 0:2 * BR], ones[:, :], sq[:, s % 2, :], start=s == 0, stop=s == KD - 1)
                        last.then_inc(sq_pe, 1)

            pe.wait_ge(ends_ready, 1)
            for i in range(4):
                last = nc.tensor.transpose(ps[5][0:H, i * 128:i * 128 + 128], ends[:, i, :], ident[:, :])
            last.then_inc(ends_T, 1)
            pe.wait_ge(carry_ready, 1)
            for i, a in enumerate((4, 5, 0)):
                last = nc.tensor.transpose(ps[6][:, i * H:i * H + H], laneT[:, a, 0:128], ident[0:H, 0:H])
            last.then_inc(carry_back, 1)
            pe.wait_ge(rh_ready, 1)
            with pe.Fori(0, SLOTS // 3) as i:
                for k in range(3):
                    s = 3 * i + k
                    t0 = pe.value_load(slot_i[0:1, bass.ds(s, 1)], min_val=0, max_val=T - 1)
                    alone(pe, slot_dve, 3 + s - 2)
                    alone(pe, hot_ready, s + 1)
                    mm(ps[k][0:PR, 0:265], hot[:, k, :], RH[:, bass.ds(chunk_of(s, t0), 1), :].rearrange("p a w -> p (a w)"), start=True, stop=True).then_inc(slot_pe, 1)
            pe.wait_ge(gnn_ready, 1)
            for b in range(NB):
                if b >= 2:
                    pe.wait_ge(gT_dve, b - 1)
                for h in range(2):
                    for k in range(2):
                        last = nc.tensor.transpose(ps[3 + b % 2][:, h * BR + k * PR:h * BR + k * PR + PR],
                                                   acc[:, 2 * b + k, h * 128:h * 128 + 128], ident[0:PR, 0:PR])
                last.then_inc(gT_pe, 1)

            pe.wait_ge(gT_dve, NB)
            pe.wait_ge(ff_w, 16 * 7)

            def residual(b, e, first=False):
                if e >= 2 or not first:
                    alone(pe, x1_dve, KD * b + e - 1)
                to = ps[3 + e % 2]
                cut = slice(e * 128, e * 128 + 128)
                mm(to[:, 0:PR], xrow[:, 0, cut], ident[0:PR, 0:PR], start=True, stop=False)
                mm(to[:, PR:BR], xrow[:, 1, cut], ident[0:PR, 0:PR], start=False, stop=False)
                chain(to[:, 0:BR], [(wraw[:, k, cut], gT[:, k, bass.ds(b * BR, BR)]) for k in range(2)], start=False).then_inc(x1_pe, 1)

            def over_lanes(step, to, weights, done):
                alone(pe, slices_dve, step)
                mm(to[:, 0:BR], weights[:, :], part[:, 0], start=True, stop=True).then_inc(done, 1)

            mean = lambda b: over_lanes(3 * b + 1, ps[5], avg, mean_pe)
            variance = lambda b: over_lanes(3 * b + 2, ps[2], avg, var_pe)
            gate = lambda b: over_lanes(3 * b + 3, ps[5], ones, gate_pe)

            def feed_forward(b, odd, more):
                alone(pe, x2_dve, b + 1)
                alone(pe, y_dve, 1 + KD * b)
                for j in range(12):
                    x, c = j // 4, (j % 4) * 128
                    if 2 <= j < 10:
                        alone(pe, h_dve, 8 * b + j - 1)
                    elif j >= 10:
                        alone(pe, h_act, 12 * b + j - 1)
                    chain(ps[j % 2][:, 0:BR], [(w1s[:, x, k, c:c + 128], x2T[odd][:, k]) for k in range(KD)]).then_inc(h_pe, 1)
                    if more and j < KD:
                        if j == 0:
                            alone(pe, xrow_here, 16 * (b + 2))
                        residual(b + 1, j)
                    if more and j == 9:
                        mean(b + 1)
                for e in range(KD):
                    if e < 2:
                        alone(pe, h_act, 12 * b + 11 + e)
                    else:
                        alone(pe, y_dve, 1 + KD * b + e - 1)
                    steps = [(w2s[:, j // 4, j % 4, e * 128:e * 128 + 128], hT[:, j]) for j in range(12)]
                    if e == 0:
                        chain(ps[0][:, 0:BR], steps[:11], stop=False)
                        alone(pe, h_act, 12 * b + 12)
                        chain(ps[0][:, 0:BR], steps[11:], start=False).then_inc(y_pe, 1)
                    else:
                        chain(ps[e % 2][:, 0:BR], steps).then_inc(y_pe, 1)
                    if more and e == 0:
                        variance(b + 1)
                    if more and e == 3:
                        gate(b + 1)
                for h in range(2):
                    alone(pe, y_dve, 1 + KD * b + 4 * h + 4)
                    for k, copied in enumerate((yr_act, yr_dve)):
                        alone(pe, copied, 1 + 2 * b + h)
                        for c in range(4):
                            last = nc.tensor.transpose(ps[6 + k][0:PR, c * 128:c * 128 + 128],
                                                       x1T[odd][:, 4 * h + c, k * PR:k * PR + PR], ident[:, :])
                        last.then_inc(yT_pe, 1)

            pe.wait_ge(xrow_here, 16)
            for e in range(KD):
                residual(0, e, first=True)
            mean(0)
            variance(0)
            gate(0)
            with pe.Fori(0, NB // 2) as i:
                for odd in range(2):
                    feed_forward(2 * i + odd, odd, True)
            feed_forward(NB - 1, 0, False)


_INS = ["x", "src", "dst", "L0_gnn_rms_w", "L0_gnn_W_down", "L0_gnn_Wl", "L0_gnn_Wr", "L0_gnn_att", "L0_gnn_W_up",
        "L0_mix_W_q", "L0_mix_W_k", "L0_mix_W_v", "L0_ffn_gate_w", "L0_ffn_w1", "L0_ffn_b1", "L0_ffn_w2",
        "L0_ffn_b2", "L0_ffn_sw1", "L0_ffn_sb1", "L0_ffn_sw2", "L0_ffn_sb2"]


def kernel(**inputs):
    import numpy as _np
    import concourse.bacc as _bacc
    from concourse import mybir as _mybir
    from concourse.bass_utils import run_bass_kernel_spmd as _run

    nc = _bacc.Bacc("TRN2", target_bir_lowering=False, num_devices=1)
    arrays, args = {}, []
    for name in _INS:
        a = _np.ascontiguousarray(inputs[name])
        arrays[f"in_{name}_dram"] = a
        args.append(nc.dram_tensor(f"in_{name}_dram", a.shape, _mybir.dt.from_np(a.dtype), kind="ExternalInput").ap())
    args.append(nc.dram_tensor("out_0_dram", (1250, 1024), _mybir.dt.float32, kind="ExternalOutput").ap())
    gps_layer(nc, *args)
    r = _run(nc, [arrays], core_ids=[0])
    return r.results[0]["out_0_dram"]
```

```python
import numpy as np
import concourse.bass as bass
from concourse import mybir
from contextlib import ExitStack


f32, i32, bf16 = mybir.dt.float32, mybir.dt.int32, mybir.dt.bfloat16
ALU = mybir.AluOpType
ACT = mybir.ActivationFunctionType
AXX = mybir.AxisListType.X

N, D, HID, H, E = 1250, 1024, 256, 4, 41250
DH = HID // H
PR, T = 125, 10
NB, BR = 5, 250
KD = D // 128
G = 10
BLOCKS = E // G
EP = E // PR
QC = -(-(BLOCKS + N) // 128)
SLOTS = QC + T - 1
ROW = 125
ROWS = E // ROW
XLW, XRW = HID + H, HID + 2 * H
SUMW = HID + 2 * H + 1
RING = 4
PER_BUF = -(-G * XLW // SUMW)
BIG = 1.0e30
RNE = 12582912.0
NEG_SLOPE = 0.2
assert NB % 2 == 1 and KD // 2 == NB - 1
assert E == BLOCKS * G == PR * EP == ROWS * ROW and EP % G == 0 and QC == NB * KD + 2


class Steps:

    def __init__(self, eng, sem):
        self.eng, self.sem, self.done, self.turn = eng, sem, 0, 0

    def add(self, ins):
        ins.then_inc(self.sem, 1)
        self.done += 1

    def wait(self):
        self.eng.wait_ge(self.sem, self.turn + self.done)

    def link(self, ins):
        self.add(ins)
        self.wait()

    def enter(self, i, per):
        self.start, self.per, self.done = self.done, per, 0
        self.turn = i * per + self.start

    def leave(self, times):
        assert self.done == self.per, (self.done, self.per)
        self.done, self.turn = self.start + times * self.per, 0


def gps_layer(nc, x, src, dst, rms_w, W_down, Wl, Wr, att, W_up, W_q, W_k, W_v,
              gate_w, w1, b1, w2, b2, sw1, sb1, sw2, sb2, out):
    dram = lambda name, shape, dt=f32: nc.dram_tensor(name, shape, dt, kind="Internal").ap()
    edge_tab = dram("edge_tab", (BLOCKS, 2 * G), i32)
    xl_tab = dram("xl_tab", (N, XLW))
    xr_tab = dram("xr_tab", (N, XRW))
    xnT_d = dram("xnT_d", (NB, 128, KD * BR))
    q_d = dram("q_d", (NB, 128, KD * BR + BR))
    o_d = dram("o_d", (QC, 128, HID))
    m_d = dram("m_d", (QC * 128, H))
    n_d = dram("n_d", (QC * 128, 1))
    f_d = dram("f_d", (QC * 128, 9))

    with ExitStack() as ctx:
        sb = lambda name, shape, dt=f32: ctx.enter_context(nc.sbuf_tensor(name, shape, dt))
        sem = lambda name: ctx.enter_context(nc.semaphore(name))

        WT = sb("WT", [128, 3 * KD * D])
        arena = sb("arena", [128, RING * G * XLW + G * HID])
        blk = sb("blk", [128, 6500])
        wraw = sb("wraw", [128, 2, D])

        wt = WT[:, :].rearrange("p (w k e) -> p w k e", w=3, k=KD)
        w1s = WT[:, 0:3 * 4096].rearrange("p (e k h) -> p e k h", e=3, k=KD)
        w2s = WT[:, 3 * 4096:6 * 4096].rearrange("p (e k d) -> p e k d", e=3, k=4)
        def third(a, n):
            return WT[:, 2 * KD * D + a:2 * KD * D + a + n]
        wd = third(0, 2048).rearrange("p (k h) -> p k h", k=KD)
        wl = third(2048, 512).rearrange("p (k h) -> p k h", k=2)
        wr = third(2560, 512).rearrange("p (k h) -> p k h", k=2)
        xnTb = third(3072, 2000).rearrange("p (k r) -> p k r", k=KD)
        tmpX = third(5072, 512)[0:PR].rearrange("p (t h) -> p t h", t=2)
        shiftA, shiftB, before = (third(7632 + PR * i, PR)[0:PR] for i in range(3))
        x_all = arena[0:PR, 0:T * D].rearrange("p (t d) -> p t d", t=T)
        raw = arena[:, T * D:(T + 2) * D].rearrange("p (k e) -> p k e", k=2)
        cmp1 = blk[0:PR, 0:T * ROWS].rearrange("p (t r) -> p t r", t=T)
        row_i = blk[0:PR, 3300:3300 + T * ROW].bitcast(i32).rearrange("p (t r) -> p t r", t=T)
        tab_sb = blk[0:PR, 4550:4550 + 2 * EP].bitcast(i32).rearrange("p (b w) -> p b w", w=2 * G)
        stepR = blk[0:PR, 5740:6380].bitcast(bf16).rearrange("p (t r) -> p t r", t=T)
        XLs = blk[0:PR, 0:T * XLW].rearrange("p (t w) -> p t w", t=T)
        XRs = blk[0:PR, 2600:2600 + T * XRW].rearrange("p (t w) -> p t w", t=T)
        hTb = blk[:, 5240:5740].rearrange("p (k r) -> p k r", k=2)
        XL = arena[:, 0:RING * G * XLW].rearrange("p (r j w) -> p r j w", r=RING, j=G)
        msg = arena[:, RING * G * XLW:].rearrange("p (j f) -> p j f", j=G)
        XB = blk[:, 0:2000].rearrange("p (k r) -> p k r", k=KD)
        KVb = blk[:, 2000:4000].rearrange("p (k r) -> p k r", k=KD)
        QN = blk[:, 4000:6000 + BR]
        Qb = QN[:, 0:2000].rearrange("p (k r) -> p k r", k=KD)
        RH = arena[:, 0:QC * SUMW].rearrange("p (q w) -> p q w", q=QC)
        acc = blk[0:PR, 0:T * SUMW].rearrange("p (t w) -> p t w", t=T)
        RH_END = QC * SUMW
        def lane(a, *shape):
            n = int(np.prod(shape))
            v = arena[:, RH_END + a:RH_END + a + n]
            return v.rearrange("p (j w) -> p j w", w=shape[1]) if len(shape) == 2 else v
        ML = lane(0, QC, H)
        NL = lane(168, QC)
        PF = lane(210, QC + 1)
        FW = lane(254, QC, H)
        BW = lane(422, QC, H)
        FL = lane(590, QC, 9)
        FG = lane(968, QC, 9)
        ends = lane(1346, 4, H)
        edge_pen = lane(1362, 2, QC)
        carry = lane(1446, 3, H)
        XL2 = blk[0:PR, T * SUMW:T * (SUMW + XLW)].rearrange("p (t w) -> p t w", t=T)
        iota_n = blk[:, 5250:5250 + N]
        xrow = arena[0:PR, 0:2 * D].rearrange("p (k d) -> p k d", k=2)
        qn = arena[:, 2048:4048 + BR]
        qT, q_norm = qn[:, 0:2000].rearrange("p (k r) -> p k r", k=KD), qn[:, 2000:]
        sqT = qT
        gT = arena[:, 4298:4298 + 2 * N].rearrange("p (k r) -> p k r", k=2)
        rows8 = lambda ap: ap.rearrange("p (k r) -> p k r", k=KD)
        x1T = [rows8(arena[:, a:a + 2000]) for a in (6798, 8798)]
        x2T = [rows8(arena[:, 10798:12798]), rows8(blk[:, 0:2000])]
        hT = blk[:, 2000:5000].rearrange("p (j r) -> p j r", j=12)

        diff = sb("diff", [128, 128])
        ident = sb("ident", [128, 128])
        ones = sb("ones", [128, 128])
        onesb = sb("onesb", [PR, 128], bf16)
        cols = sb("cols", [128, 128])
        gid = sb("gid", [128, QC])
        nid = sb("nid", [PR, T])
        att8 = sb("att8", [128, HID])
        att2 = sb("att2", [128, HID])
        rmsw = sb("rmsw", [128, KD])
        ix = sb("ix", [PR, 16, 11])
        ridx = sb("ridx", [PR, T], i32)
        bidx = sb("bidx", [128, QC + 1], i32)
        nidx = sb("nidx", [128, QC], i32)
        ngf = sb("ngf", [128, QC])
        uns = sb("uns", [128, 2, QC])
        thr = sb("thr", [1, T - 1])
        slot_t = sb("slot_t", [1, SLOTS])
        slot_i = sb("slot_i", [1, SLOTS], i32)
        st = sb("st", [PR, 2, 2, 6])
        mv = sb("mv", [PR, 2, 2])
        vr = sb("vr", [PR, 3, 2, 2])
        rms = sb("rms", [PR, NB, 2])
        lin = sb("lin", [PR, 5, 2, H])
        es = sb("es", [PR, 2, T, H])
        esel = sb("esel", [PR, T, H])
        TAB = sb("TAB", [128, QC, 2 * G], i32)
        idx = sb("idx", [128, RING, G], i32)
        XR = sb("XR", [128, RING, XRW])
        bcol = sb("bcol", [128, 6], i32)
        tab_rows = sb("tab_rows", [128, 6, 2 * G], i32)
        ncol = sb("ncol", [128, RING], i32)
        pen = sb("pen", [128, RING, G])
        sc = sb("sc", [128, RING, G, H])
        mx = sb("mx", [128, H])
        oo = sb("oo", [128, 2, HID])
        MR = sb("MR", [128, QC, H])
        DN = sb("DN", [128, QC, H])
        avg = sb("avg", [128, 128])
        eps = sb("eps", [128, 1])
        gw = sb("gw", [128, KD, 2])
        gwd = sb("gwd", [128, KD])
        b1s = sb("b1s", [128, 12])
        b2s = sb("b2s", [128, 3, KD])
        vb = sb("vb", [128, 2, BR])
        sq = sb("sq", [128, 2, 2 * BR])
        laneT = sq[:, :, :].rearrange("p a b -> p (a b)")[0:H, 0:774].rearrange("p (a l) -> p a l", a=6)
        part = sq[:, :, :].rearrange("p a b -> p (a b)").rearrange("p (k r) -> p k r", k=4)
        msk = vb[:, :, :]
        hot = vb[:, :, :].rearrange("p a b -> p (a b)")[:, 0:3 * PR].rearrange("p (k n) -> p k n", k=3)
        nrm = sb("nrm", [128, ROWS])
        gacc = sb("gacc", [128, KD])
        gpart = sb("gpart", [128, KD])

        flat = lambda t: t.rearrange("p a b -> p (a b)")
        src_sb = flat(oo[0:PR, :, :])[:, 0:EP].bitcast(i32)
        dst_sb = flat(vb[0:PR, :, :])[:, 0:EP].bitcast(i32)
        heads = nrm[:, 0:ROWS]
        heads_i = flat(sq[0:1, :, :])[:, 0:ROWS].bitcast(i32)
        slot_c = flat(sq[0:1, :, :])[:, ROWS:ROWS + SLOTS * (T - 1)].rearrange("p (s t) -> p s t", t=T - 1)
        hitA, hitB = (flat(XR[0:PR, :, :])[:, 420 * i:420 * i + 420].bitcast(bf16).rearrange("p (t q) -> p t q", t=T)
                      for i in range(2))
        yrow = [blk[0:PR, 5000:5000 + D].rearrange("p (k d) -> p k d", k=2),
                XR[0:PR, :, :].rearrange("p a b -> p (a b)")[:, 0:D].rearrange("p (k d) -> p k d", k=2)]

        ps = [ctx.enter_context(nc.psum_tensor(f"ps{i}", [128, 512], f32)) for i in range(8)]

        consts = sem("consts"); dv = sem("dv"); pl = sem("pl"); passed = sem("passed")
        ld_small = sem("ld_small"); ld_edges = sem("ld_edges"); ld_x = sem("ld_x"); ld_wd = sem("ld_wd")
        tab_ready = sem("tab_ready"); tab_stored = sem("tab_stored")
        heads_f = sem("heads_f"); heads_bc = sem("heads_bc"); rows_wanted = sem("rows_wanted")
        rows_here = sem("rows_here"); first_edges = sem("first_edges"); next_edges = sem("next_edges")
        unaligned = sem("unaligned"); unaligned_sums = sem("unaligned_sums"); hits = sem("hits")
        group_counts = sem("group_counts"); index_ready = sem("index_ready")
        wd_ready = sem("wd_ready"); var_ready = sem("var_ready"); std_ready = sem("std_ready")
        xn_ready = sem("xn_ready"); xT_pe = sem("xT_pe"); xT_act = sem("xT_act"); xT_dve = sem("xT_dve")
        xT_stored = sem("xT_stored"); hT_pe = sem("hT_pe"); hT_act = sem("hT_act"); lr_pe = sem("lr_pe")
        lr_act = sem("lr_act"); tabs_ready = sem("tabs_ready"); tabs_stored = sem("tabs_stored")
        w_ld = [sem("w_ld0"), sem("w_ld1")]
        wv_ld = [sem("wv_ld0"), sem("wv_ld1")]; half_pe = sem("half_pe"); half_act = sem("half_act")
        w_pe = sem("w_pe"); w_act = sem("w_act")
        tab_here = [sem(f"tab_here{k}") for k in range(6)]; edges_ready = sem("edges_ready")
        xl_here = [sem(f"xl_here{r}") for r in range(RING)]
        scores = sem("scores"); exps = sem("exps"); mul_act = sem("mul_act"); part_sums = sem("part_sums"); sums = sem("sums"); o_ready = sem("o_ready")
        o_stored = [sem("o_stored0"), sem("o_stored1")]
        xb_here = sem("xb_here"); kvq_pe = sem("kvq_pe"); sq_act = sem("sq_act")
        kv_dve = sem("kv_dve"); sq_pe = sem("sq_pe"); norm_act = sem("norm_act")
        block_dve = sem("block_dve"); q_stored = sem("q_stored")
        stats_stored = sem("stats_stored"); nodes_stored = sem("nodes_stored"); lanes_here = sem("lanes_here")
        ends_ready = sem("ends_ready"); ends_T = sem("ends_T"); carry_ready = sem("carry_ready")
        carry_back = sem("carry_back"); shift_ready = sem("shift_ready"); factor_act = sem("factor_act")
        factors_ready = sem("factors_ready"); factors_stored = sem("factors_stored")
        factors_here = sem("factors_here"); o_here = sem("o_here"); xl2_here = sem("xl2_here")
        hot_ready = sem("hot_ready"); apart = sem("apart"); rh_ready = sem("rh_ready"); slot_pe = sem("slot_pe"); acc_zero = sem("acc_zero"); slot_dve = sem("slot_dve")
        self_ready = sem("self_ready"); self_act = sem("self_act"); gnn_ready = sem("gnn_ready")
        gT_pe = sem("gT_pe"); gT_dve = sem("gT_dve")
        ff_w = sem("ff_w"); ff_small = sem("ff_small")
        xrow_here = sem("xrow_here"); q_here = sem("q_here"); slices_dve = sem("slices_dve"); x1_pe = sem("x1_pe"); x1_dve = sem("x1_dve"); mean_pe = sem("mean_pe")
        cen_dve = sem("cen_dve"); sqr_act = sem("sqr_act"); var_pe = sem("var_pe"); dev_act = sem("dev_act")
        x2_dve = sem("x2_dve"); gate_pe = sem("gate_pe"); mask_dve = sem("mask_dve"); h_pe = sem("h_pe")
        h_dve = sem("h_dve"); h_act = sem("h_act"); y_pe = sem("y_pe"); y_dve = sem("y_dve")
        yT_pe = sem("yT_pe"); yr_act = sem("yr_act"); yr_dve = sem("yr_dve"); out_stored = [sem("out_stored0"), sem("out_stored1")]

        block = ctx.enter_context(nc.Block())

        def alone(eng, s, value):
            eng.wait_ge(s, value)
            eng.sem_inc(passed)

        def chunk_of(slot, tile):
            return nc.s_assert_within(slot - tile, 0, QC - 1, skip_runtime_bounds_check_because=
                                      "tile t takes the slots from (its first chunk) + t up to (the next tile's) + t")

        @block.sync
        def _(sp):
            for s in (q_stored, *o_stored, *out_stored):
                sp.sem_inc(s)
            sp.dma_start(heads_i, dst[::ROW].rearrange("(a r) -> a r", a=1), allow_slow_non_contiguous=True).then_inc(ld_edges, 16)
            sp.dma_start(src_sb, src.rearrange("(p e) -> p e", p=PR)).then_inc(ld_edges, 16)
            sp.dma_start(dst_sb, dst.rearrange("(p e) -> p e", p=PR)).then_inc(ld_edges, 16)

            def load_w(r, W, to, done):
                sp.dma_start(to, W[bass.ds(r * 128, 128), :]).then_inc(done, 16)

            def load_rows_of_x(b):
                if b:
                    sp.wait_ge(ld_x, 16 * b)
                sp.dma_start(x_all[:, bass.ds(2 * b, 2), :], x[bass.ds(b * BR, BR), :].rearrange("(t p) d -> p t d", p=PR)).then_inc(ld_x, 16)

            for k in range(2):
                load_w(k, W_k, raw[:, k, :], w_ld[k])
            load_rows_of_x(0)
            sp.dma_start(att8[:, :], att.rearrange("h d -> (h d)").partition_broadcast(128)).then_inc(ld_small, 16)
            sp.dma_start(rmsw[:, :], rms_w.rearrange("(k p) -> p k", p=128), allow_slow_non_contiguous=True).then_inc(ld_small, 16)
            sp.wait_ge(tab_ready, 1)
            sp.dma_start(edge_tab.rearrange("(p b) w -> p b w", p=PR), tab_sb).then_inc(tab_stored, 16)
            sp.dma_start(wd, W_down.rearrange("(k p) h -> p k h", p=128)).then_inc(ld_wd, 16)
            sp.dma_start(wl, Wl.rearrange("(k p) h -> p k h", p=128)).then_inc(ld_wd, 16)
            sp.dma_start(wr, Wr.rearrange("(k p) h -> p k h", p=128)).then_inc(ld_wd, 16)
            with sp.Fori(1, KD // 2) as i:
                for k in range(2):
                    alone(sp, w_pe, 2 * i + k - 1)
                    load_w(2 * i + k, W_k, raw[:, k, :], w_ld[k])
            load_rows_of_x(1)
            for k in range(2):
                sp.wait_ge(w_pe, KD - 1 + k)
                load_w(k, W_q, raw[:, k, :], w_ld[k])
            load_rows_of_x(2)
            sp.dma_start(gw[:, :, 0], gate_w[0].rearrange("(k p) -> p k", p=128), allow_slow_non_contiguous=True).then_inc(ff_small, 16)
            sp.dma_start(gw[:, :, 1], gate_w[1].rearrange("(k p) -> p k", p=128), allow_slow_non_contiguous=True).then_inc(ff_small, 16)
            for e, (a, c) in enumerate(((b1[0], b2[0]), (b1[1], b2[1]), (sb1, sb2))):
                sp.dma_start(b1s[:, 4 * e:4 * e + 4], a.rearrange("(k p) -> p k", p=128), allow_slow_non_contiguous=True).then_inc(ff_small, 16)
                sp.dma_start(b2s[:, e], c.rearrange("(k p) -> p k", p=128), allow_slow_non_contiguous=True).then_inc(ff_small, 16)
            sp.wait_ge(index_ready, 1)
            sp.dma_start(n_d.rearrange("(q p) a -> p (q a)", p=128), ngf[:, :], allow_slow_non_contiguous=True).then_inc(nodes_stored, 16)

            def row_block(b, more_x=False, more_w=False):
                sp.wait_ge(xT_act, 2 * b + 2)
                sp.wait_ge(xT_dve, 2 * b + 2)
                sp.dma_start(xnT_d[bass.ds(b, 1)].rearrange("a p f -> (a p) f"),
                             xnTb.rearrange("p k r -> p (k r)")).then_inc(xT_stored, 16)
                if more_x:
                    load_rows_of_x(b + 3)
                if more_w:
                    for k in range(2):
                        alone(sp, half_pe, 4 * b + 2 * k + 2)
                        load_w(2 * b + 2 + k, W_q, raw[:, k, :], w_ld[k])

            def store_tables(b):
                alone(sp, tabs_ready, b + 1)
                rows = bass.ds(b * BR, BR)
                sp.dma_start(xl_tab[rows, :].rearrange("(t p) w -> p t w", p=PR), XLs[:, bass.ds(2 * b, 2), :]).then_inc(tabs_stored, 16)
                sp.dma_start(xr_tab[rows, :].rearrange("(t p) w -> p t w", p=PR), XRs[:, bass.ds(2 * b, 2), :]).then_inc(tabs_stored, 16)

            row_block(0, True, True)
            row_block(1, True, True)
            store_tables(0)
            row_block(2, False, True)
            store_tables(1)
            row_block(3)
            store_tables(2)
            sp.wait_ge(xT_pe, 4 * NB)
            for k in range(2):
                load_w(k, W_v, wraw[:, k, :], wv_ld[k])
            row_block(4)
            store_tables(3)
            store_tables(4)
            with sp.Fori(1, KD // 2) as i:
                for k in range(2):
                    alone(sp, w_pe, KD + 2 * i + k - 1)
                    load_w(2 * i + k, W_v, wraw[:, k, :], wv_ld[k])
            sp.wait_ge(xT_stored, 16 * NB)
            sp.wait_ge(tabs_stored, 32 * NB)

            def load_x(b):
                sp.dma_start(XB.rearrange("p k r -> p (k r)"),
                             xnT_d[bass.ds(b, 1)].rearrange("a p f -> (a p) f")).then_inc(xb_here, 16)

            def store_maxima(q):
                alone(sp, scores, q + 1)
                sp.dma_start(m_d[bass.ds(q * 128, 128), :],
                             MR[:, bass.ds(q, 1), :].rearrange("p a h -> p (a h)")).then_inc(stats_stored, 16)

            def store_sums(q, e):
                alone(sp, o_ready, 2 + q + 1)
                sp.dma_start(o_d[bass.ds(q, 1)].rearrange("a p f -> (a p) f"), oo[:, e % 2, :]).then_inc(o_stored[e % 2], 16)

            def edge_block(b, more):
                for e in range(KD):
                    store_sums(KD * b + e, e)
                    store_maxima(KD * b + e + 2)
                    if e == KD - 2 and more:
                        alone(sp, kvq_pe, 1 + KD * b + KD)
                        load_x(b + 1)
                alone(sp, norm_act, 1 + b + 1)
                sp.dma_start(q_d[bass.ds(b, 1)].rearrange("a p f -> (a p) f"), QN).then_inc(q_stored, 16)

            load_x(0)
            store_maxima(0)
            store_maxima(1)
            with sp.Fori(0, NB - 1) as b:
                edge_block(b, True)
            edge_block(NB - 1, False)
            sp.wait_ge(stats_stored, 16 * QC)
            sp.wait_ge(nodes_stored, 16)
            sp.dma_start(ML, m_d.rearrange("(l j) h -> l j h", j=QC)).then_inc(lanes_here, 16)
            sp.dma_start(NL, n_d.rearrange("(l j) a -> l (j a)", j=QC)).then_inc(lanes_here, 16)
            def load_sums(a, z):
                sp.dma_start(RH[:, a:z, 0:HID], o_d[a:z].rearrange("q p f -> p q f")).then_inc(o_here, 16)

            sp.wait_ge(o_stored[0], 1 + 16 * (QC // 2 - 1))
            sp.wait_ge(o_stored[1], 1 + 16 * (QC // 2 - 1))
            load_sums(2 * PER_BUF, QC - 2)
            store_sums(QC - 2, 0)
            load_sums(0, PER_BUF - 1)
            store_sums(QC - 1, 1)
            sp.wait_ge(o_stored[0], 1 + 16 * (QC // 2))
            sp.wait_ge(o_stored[1], 1 + 16 * (QC // 2))
            load_sums(PER_BUF - 1, 2 * PER_BUF)
            load_sums(QC - 2, QC)
            sp.wait_ge(q_stored, 1 + 16 * NB)
            sp.dma_start(XL2, xl_tab.rearrange("(t p) w -> p t w", p=PR)).then_inc(xl2_here, 16)
            sp.wait_ge(factors_ready, 1)
            sp.dma_start(f_d.rearrange("(l j) w -> l j w", j=QC), FL).then_inc(factors_stored, 16)
            sp.wait_ge(factors_stored, 16)
            sp.dma_start(FG, f_d.rearrange("(q p) w -> p q w", p=128)).then_inc(factors_here, 16)
            sp.dma_start(wraw[:, :, :], W_up.rearrange("(k p) d -> p k d", p=128)).then_inc(ff_w, 16)
            sp.wait_ge(kvq_pe, 1 + NB * KD)
            for e, w in enumerate((w1[0], w1[1], sw1)):
                sp.dma_start(w1s[:, e], w.rearrange("(k p) h -> p k h", p=128)).then_inc(ff_w, 16)
            for e, w in enumerate((w2[0], w2[1], sw2)):
                sp.dma_start(w2s[:, e], w.rearrange("(k p) d -> p k d", p=128)).then_inc(ff_w, 16)
            def load_rows(b):
                sp.dma_start(xrow, x[bass.ds(b * BR, BR), :].rearrange("(k p) d -> p k d", p=PR)).then_inc(xrow_here, 16)

            def load_q(b):
                sp.dma_start(qn, q_d[bass.ds(b, 1)].rearrange("a p f -> (a p) f")).then_inc(q_here, 16)

            def store_rows(b):
                for h in range(2):
                    alone(sp, yr_act, 1 + 2 * b + h + 1)
                    alone(sp, yr_dve, 1 + 2 * b + h + 1)
                    sp.dma_start(out[bass.ds(b * BR, BR), h * 512:h * 512 + 512].rearrange("(k p) d -> p k d", p=PR),
                                 yrow[h]).then_inc(out_stored[h], 16)

            sp.wait_ge(slot_dve, 3 + SLOTS)
            load_rows(0)
            load_q(0)

            def load_next(b):
                alone(sp, x1_pe, KD * b + KD)
                load_rows(b + 1)
                alone(sp, slices_dve, 3 * b + 2)
                load_q(b + 1)

            load_next(0)
            with sp.Fori(0, NB - 2) as b:
                load_next(b + 1)
                store_rows(b)
            store_rows(NB - 2)
            store_rows(NB - 1)
            for h in range(2):
                sp.wait_ge(out_stored[h], 1 + 16 * NB)


        @block.gpsimd
        def _(pool):
            g = nc.gpsimd
            at = Steps(pool, pl)
            g.memset(eps[:, :], 1e-5).then_inc(consts, 1)
            g.iota(diff[:, :], pattern=[[1, 128]], base=0, channel_multiplier=-1, allow_small_or_imprecise_dtypes=True).then_inc(consts, 1)
            g.iota(cols[:, :], pattern=[[1, 128]], base=0, channel_multiplier=0, allow_small_or_imprecise_dtypes=True).then_inc(consts, 1)
            g.iota(gid[:, :], pattern=[[128, QC]], base=0, channel_multiplier=1, allow_small_or_imprecise_dtypes=True).then_inc(consts, 1)
            g.iota(nid[:, :], pattern=[[PR, T]], base=0, channel_multiplier=1, allow_small_or_imprecise_dtypes=True).then_inc(consts, 1)
            pool.wait_ge(rows_wanted, 1)
            for t in range(T):
                g.indirect_dma_start(row_i[:, t, :], None, dst.rearrange("(r w) -> r w", w=ROW),
                                     bass.IndirectOffsetOnAxis(ridx[:, t:t + 1], 0)).then_inc(rows_here, 16)
            pool.wait_ge(index_ready, 1)
            pool.wait_ge(tab_stored, 16)
            with pool.Fori(0, QC // 6) as i:
                at.enter(i, 2 * 6)
                for k in range(6):
                    at.add(g.tensor_copy(bcol[:, k:k + 1], bidx[:, bass.ds(6 * i + k, 1)]))
                alone(pool, pl, at.turn + at.done)
                for k in range(6):
                    g.indirect_dma_start(tab_rows[:, k, :], None, edge_tab[:, :],
                                         bass.IndirectOffsetOnAxis(bcol[:, k:k + 1], 0)).then_inc(tab_here[k], 16)
                for k in range(6):
                    alone(pool, tab_here[k], 16 * (i + 1))
                    at.add(g.tensor_copy(TAB[:, bass.ds(6 * i + k, 1), :].rearrange("p a w -> p (a w)"), tab_rows[:, k, :]))
            at.leave(QC // 6)
            at.wait()
            pool.sem_inc(edges_ready)
            pool.wait_ge(tabs_stored, 32 * NB)

            def gather(q, e):
                r = e % RING
                alone(pool, sums, q + 1)
                at.add(g.tensor_copy(idx[:, r, :], TAB[:, bass.ds(q, 1), 0:G].rearrange("p a w -> p (a w)")))
                at.add(g.tensor_copy(ncol[:, r:r + 1], nidx[:, bass.ds(q, 1)]))
                alone(pool, pl, at.turn + at.done)
                g.indirect_dma_start(XR[:, r, :], None, xr_tab[:, :],
                                     bass.IndirectOffsetOnAxis(ncol[:, r:r + 1], 0)).then_inc(xl_here[r], 16)
                for j in range(G):
                    g.indirect_dma_start(XL[:, r, j, :], None, xl_tab[:, :],
                                         bass.IndirectOffsetOnAxis(idx[:, r, j:j + 1], 0)).then_inc(xl_here[r], 16)

            with pool.Fori(0, NB) as b:
                at.enter(b, 2 * KD)
                for e in range(KD):
                    gather(KD * b + e, e)
            at.leave(NB)
            gather(NB * KD, 0)
            gather(NB * KD + 1, 1)
            pool.wait_ge(block_dve, 1 + NB)
            pool.wait_ge(q_stored, 1 + 16 * NB)
            g.memset(acc, 0.0).then_inc(acc_zero, 1)
            g.iota(iota_n, pattern=[[1, N]], base=0, channel_multiplier=0, allow_small_or_imprecise_dtypes=True).then_inc(consts, 1)

        @block.scalar
        def _(act):
            for s in (half_act, lr_act, hT_act, w_act, sq_act, norm_act, yr_act, o_ready, o_ready):
                act.sem_inc(s)
            a = nc.scalar

            def transposed_rows(w, i, done):
                for k in range(2):
                    alone(act, w_pe, done + 2 * i + k + 1)
                    for h in range(2):
                        last = a.copy(wt[:, w, 4 * h:4 * h + 4, bass.ds((2 * i + k) * 128, 128)],
                                      ps[2 * k + h][:, :].rearrange("p (k r) -> p k r", k=4))
                    last.then_inc(w_act, 1)

            def half_row(b, c):
                k, h = c // 2, c % 2
                alone(act, half_pe, 4 * b + c + 1)
                a.copy(wt[:, 1, 4 * h:4 * h + 4, bass.ds((2 * b + k) * 128, 128)],
                       ps[7][:, :].rearrange("p (k r) -> p k r", k=4)).then_inc(half_act, 1)

            def deviation(b):
                act.wait_ge(var_ready, b + 1)
                a.activation(vr[:, 1], vr[:, 0], ACT.Sqrt).then_inc(std_ready, 1)

            def copy_rows(b, first=False):
                if not first:
                    alone(act, xT_stored, 16 * b)
                    alone(act, hT_pe, b)
                for k in range(2):
                    act.wait_ge(xT_pe, 4 * b + 2 * k + 1)
                    a.copy(xnTb[:, 0:4, PR * k:PR * k + PR],
                           ps[2 * k][:, 0:4 * PR].rearrange("p (k r) -> p k r", k=4)).then_inc(xT_act, 1)

            def copy_hidden(b):
                alone(act, lr_pe, 1 + 2 * b)
                act.wait_ge(hT_pe, b + 1)
                a.copy(hTb, ps[4][:, 0:2 * BR].rearrange("p (k r) -> p k r", k=2)).then_inc(hT_act, 1)

            def scale_rows(b):
                for k in range(2):
                    alone(act, lr_pe, 1 + 2 * b + k + 1)
                    for to, cut in ((XLs, slice(0, HID)), (XRs, slice(HID, 2 * HID))):
                        last = a.mul(to[:, bass.ds(2 * b + k, 1), 0:HID].rearrange("p a d -> p (a d)"),
                                     ps[5 + k][0:PR, cut], rms[:, bass.ds(b, 1), k])
                    last.then_inc(lr_act, 1)

            with act.Fori(0, 2) as i:
                transposed_rows(0, i, 0)
            deviation(0)
            with act.Fori(2, KD // 2) as i:
                transposed_rows(0, i, 0)
            copy_rows(0, first=True)
            act.wait_ge(tab_stored, 16)
            deviation(1)

            def row_block(b, ahead):
                half_row(b, 0)
                copy_hidden(b)
                half_row(b, 1)
                copy_rows(b + 1)
                half_row(b, 2)
                scale_rows(b)
                half_row(b, 3)
                if ahead:
                    deviation(b + 2)

            with act.Fori(0, NB - 2) as b:
                row_block(b, True)
            row_block(NB - 2, False)
            copy_hidden(NB - 1)
            scale_rows(NB - 1)
            act.wait_ge(tabs_ready, NB)
            act.wait_ge(xT_stored, 16 * NB)
            with act.Fori(0, KD // 2) as i:
                transposed_rows(2, i, KD)

            def weigh(q, e):
                r = e % RING
                act.wait_ge(scores, q + 1)
                a.activation(sc[:, r], sc[:, r], ACT.Exp).then_inc(exps, 1)
                act.wait_ge(exps, q + 1)
                for j in range(G):
                    for h in range(H):
                        m = XL[:, r, j, h * DH:h * DH + DH]
                        last = a.mul(m, m, sc[:, r, j, h:h + 1])
                last.then_inc(mul_act, 1)

            def take_sum(q, e, stored):
                alone(act, o_stored[e % 2], 1 + 16 * stored)
                act.wait_ge(sums, RING + q + 1)
                a.copy(oo[:, e % 2, :], ps[5 + e % 2][:, 0:HID]).then_inc(o_ready, 1)

            weigh(0, 0)
            weigh(1, 1)
            with act.Fori(0, NB) as b:
                for e in range(KD):
                    u, k = KD * b + e, e % 2
                    take_sum(u, e, 4 * b + e // 2)
                    if e == 0:
                        alone(act, block_dve, 1 + b)
                        alone(act, q_stored, 1 + 16 * b)
                    if e >= 2:
                        alone(act, kv_dve, 1 + u - 1)
                        alone(act, sq_pe, u - 1)
                    act.wait_ge(kvq_pe, 1 + u + 1)
                    a.copy(vb[:, k, :], ps[2 + k][:, 0:BR])
                    a.copy(Qb[:, e, :], ps[k][:, BR:2 * BR])
                    a.activation(sq[:, k, :], ps[k][:, 0:2 * BR], ACT.Square).then_inc(sq_act, 1)
                    if e == KD - 1:
                        act.wait_ge(sq_pe, KD * b + KD)
                        a.activation(nrm[:, 0:BR], ps[4][:, 0:BR], ACT.Sqrt)
                        a.activation(QN[:, 2000:], ps[4][:, BR:2 * BR], ACT.Sqrt).then_inc(norm_act, 1)
                    weigh(u + 2, e + 2)
            take_sum(NB * KD, 0, 4 * NB)
            take_sum(NB * KD + 1, 1, 4 * NB)
            act.wait_ge(shift_ready, 1)
            a.activation(FL[:, :, 0:H], FL[:, :, 0:H], ACT.Exp).then_inc(factor_act, 1)
            act.wait_ge(consts, 6)
            with act.Fori(0, SLOTS // 3) as i:
                for k in range(3):
                    s = 3 * i + k
                    t0 = act.value_load(slot_i[0:1, bass.ds(s, 1)], min_val=0, max_val=T - 1)
                    alone(act, slot_pe, 3 + s - 2)
                    a.activation(hot[:, k, :], iota_n[:, bass.ds(t0 * PR, PR)], ACT.Abs, scale=-1.0,
                                 bias=ngf[:, bass.ds(chunk_of(s, t0), 1)]).then_inc(apart, 1)
                    act.wait_ge(apart, s + 1)
                    a.activation(hot[:, k, :], hot[:, k, :], ACT.Relu, scale=-1.0, bias=ones[:, 0:1]).then_inc(hot_ready, 1)
            act.wait_ge(self_ready, 1)
            a.activation(es[:, 0], es[:, 0], ACT.Exp).then_inc(self_act, 1)
            act.wait_ge(ff_small, 16 * 8)

            def squares(b, odd):
                act.wait_ge(cen_dve, b + 1)
                a.activation(sqT, x2T[odd], ACT.Square).then_inc(sqr_act, 1)

            def deviations(b, first=False):
                if not first:
                    alone(act, x2_dve, b)
                act.wait_ge(var_pe, b + 1)
                a.activation(nrm[:, 0:BR], ps[2][:, 0:BR], ACT.Sqrt, bias=eps[:, :]).then_inc(dev_act, 1)

            def feed_forward(b, odd, more):
                for j in range(12):
                    if j < 8:
                        act.wait_ge(h_dve, 8 * b + j + 1)
                        a.activation(hT[:, j], hT[:, j], ACT.Relu, bias=b1s[:, j:j + 1]).then_inc(h_act, 1)
                    else:
                        act.wait_ge(h_pe, 12 * b + j + 1)
                        a.activation(hT[:, j], ps[j % 2][:, 0:BR], ACT.Relu, bias=b1s[:, j:j + 1]).then_inc(h_act, 1)
                if more:
                    squares(b + 1, 1 - odd)
                    deviations(b + 1)
                for h in range(2):
                    alone(act, out_stored[h], 1 + 16 * b)
                    act.wait_ge(yT_pe, 4 * b + 2 * h + 1)
                    a.copy(yrow[h][:, 0, :], ps[6][0:PR, :]).then_inc(yr_act, 1)

            squares(0, 0)
            deviations(0, first=True)
            with act.Fori(0, NB // 2) as i:
                for odd in range(2):
                    feed_forward(2 * i + odd, odd, True)
            feed_forward(NB - 1, 0, False)

        @block.vector
        def _(dve):
            for s in (block_dve, kv_dve, slot_dve, slot_dve, slot_dve, y_dve, yr_dve):
                dve.sem_inc(s)
            v = nc.vector
            at = Steps(dve, dv)
            TT, TS, STT, RED = v.tensor_tensor, v.tensor_scalar, v.scalar_tensor_tensor, v.tensor_reduce

            v.memset(ones[:, :], 1.0)
            v.memset(onesb[:, :], 1.0)
            v.memset(avg[:, :], 1.0 / D)
            v.memset(gacc[:, :], 0.0)
            dve.wait_ge(consts, 5)
            TS(ident[:, :], diff[:, :], 0.0, None, ALU.is_equal)
            TS(shiftA, diff[0:PR, 0:PR], -1.0, None, ALU.is_equal)
            TS(shiftB, diff[0:PR, 0:PR], float(PR - 1), None, ALU.is_equal)
            at.add(TS(before, diff[0:PR, 0:PR], 1.0, None, ALU.is_ge))

            dve.wait_ge(ld_edges, 48)
            v.tensor_copy(heads[0:1], heads_i).then_inc(heads_f, 1)
            v.tensor_copy(tab_sb[:, :, 0:G], src_sb.rearrange("p (b j) -> p b j", j=G))
            v.tensor_copy(tab_sb[:, :, G:2 * G], dst_sb.rearrange("p (b j) -> p b j", j=G)).then_inc(tab_ready, 1)
            dve.wait_ge(heads_bc, 1)
            at.link(TT(cmp1, ps[7][0:PR, None, 0:ROWS].to_broadcast([PR, T, ROWS]),
                       nid[:, :, None].to_broadcast([PR, T, ROWS]), ALU.is_lt))
            at.link(RED(ix[:, 0, 0:T], cmp1, AXX, ALU.add))
            at.link(TS(ix[:, 1, 0:T], ix[:, 0, 0:T], -1.0, 0.0, ALU.add, ALU.max))
            v.tensor_copy(ridx[:, :], ix[:, 1, 0:T]).then_inc(rows_wanted, 1)

            dve.wait_ge(ld_small, 32)
            TS(att2[:, :], att8[:, :], NEG_SLOPE, None, ALU.mult)
            at.link(TS(att8[:, :], att8[:, :], 1.0 - NEG_SLOPE, None, ALU.mult))
            xnb = wraw[0:PR]
            row = lambda ap: ap.rearrange("p a d -> p (a d)")

            def normalise_rows(b):
                dve.wait_ge(ld_x, 16 * (b + 1))
                for k in range(2):
                    for h in range(2):
                        at.add(v.bn_stats(st[:, k, h, :], row(x_all[:, bass.ds(2 * b + k, 1), 512 * h:512 * h + 512])))
                alone(dve, dv, at.turn + at.done)
                for k in range(2):
                    at.add(v.bn_aggr(mv[:, k, :], st[:, k].rearrange("p a s -> p (a s)")))
                at.wait()
                at.link(TS(vr[:, 0, :, 0:1], mv[:, :, 1:2], 1e-5, None, ALU.add))
                at.link(v.reciprocal(vr[:, 2, :, 0:1], vr[:, 0, :, 0:1]))
                at.link(TT(vr[:, 2, :, 1:2], mv[:, :, 1:2], vr[:, 2, :, 0:1], ALU.mult))
                TS(vr[:, 0, :, 1:2], vr[:, 2, :, 1:2], 1e-6, None, ALU.add).then_inc(var_ready, 1)
                dve.wait_ge(std_ready, b + 1)
                at.link(v.reciprocal(vr[:, 2], vr[:, 1]))
                at.add(TS(rms[:, bass.ds(b, 1), :], vr[:, 2, None, :, 1], 1.0, None, ALU.mult))
                for k in range(2):
                    TS(xnb[:, k, :], row(x_all[:, bass.ds(2 * b + k, 1), :]), mv[:, k, 0:1], vr[:, 2, k, 0:1],
                       ALU.subtract, ALU.mult).then_inc(xn_ready, 1)

            def copy_rows(b):
                for k in range(2):
                    dve.wait_ge(xT_pe, 4 * b + 2 * k + 2)
                    v.tensor_copy(xnTb[:, 4:8, PR * k:PR * k + PR],
                                  ps[2 * k + 1][:, 0:4 * PR].rearrange("p (k r) -> p k r", k=4)).then_inc(xT_dve, 1)

            heads_view = lambda ap: ap.rearrange("p t (h d) -> p t h d", h=H)
            all_t = lambda ap: ap[:, None, :].to_broadcast([PR, 2, HID])

            def tables(b):
                xl, xr = (t[:, bass.ds(2 * b, 2), :] for t in (XLs, XRs))
                alone(dve, lr_act, 1 + 2 * b + 2)
                at.link(TT(tmpX, xl[:, :, 0:HID], all_t(att2[0:PR]), ALU.mult))
                at.link(RED(lin[:, 0], heads_view(tmpX), AXX, ALU.add))
                at.link(TT(tmpX, xr[:, :, 0:HID], all_t(att2[0:PR]), ALU.mult))
                at.link(RED(lin[:, 1], heads_view(tmpX), AXX, ALU.add))
                at.link(TT(tmpX, xr[:, :, 0:HID], xl[:, :, 0:HID], ALU.add))
                at.link(STT(tmpX, tmpX, 0.0, all_t(att8[0:PR]), ALU.max, ALU.mult))
                at.link(RED(lin[:, 2], heads_view(tmpX), AXX, ALU.add))
                at.link(TT(lin[:, 3], lin[:, 0], lin[:, 1], ALU.add))
                at.add(TT(lin[:, 4], lin[:, 2], lin[:, 3], ALU.add))
                alone(dve, dv, at.turn + at.done)
                v.tensor_copy(xl[:, :, HID:], lin[:, 0])
                v.tensor_copy(xr[:, :, HID:HID + H], lin[:, 1])
                v.tensor_copy(esel[:, bass.ds(2 * b, 2), :], lin[:, 4])
                v.tensor_copy(xr[:, :, HID + H:], lin[:, 4]).then_inc(tabs_ready, 1)

            normalise_rows(0)
            dve.wait_ge(ld_wd, 48)
            for k in range(KD):
                last = TS(wd[:, k, :], wd[:, k, :], rmsw[:, k:k + 1], None, ALU.mult)
            last.then_inc(wd_ready, 1)

            dve.wait_ge(rows_here, 16 * T)
            at.link(TT(cmp1[:, :, 0:ROW], row_i, nid[:, :, None].to_broadcast([PR, T, ROW]), ALU.is_lt))
            v.memset(ix[:, 2, T:], float(E))
            at.link(RED(ix[:, 0, 0:T], cmp1[:, :, 0:ROW], AXX, ALU.add))
            STT(ix[:, 2, 0:T], ix[:, 1, 0:T], float(ROW), ix[:, 0, 0:T], ALU.mult, ALU.add).then_inc(first_edges, 1)
            dve.wait_ge(first_edges, 1)
            first = ix[:, 2, 0:T]

            def floor_div(to, a, d, margin, w):
                at.link(TS(ix[:, w, 0:T], a, 1.0 / d, -margin, ALU.mult, ALU.add))
                at.link(TS(to, ix[:, w, 0:T], RNE, -RNE, ALU.add, ALU.add))

            floor_div(ix[:, 4, 0:T], first, G, 0.45, 3)
            at.link(STT(ix[:, 5, 0:T], ix[:, 4, 0:T], -float(G), first, ALU.mult, ALU.add))
            at.link(TS(ix[:, 5, 0:T], ix[:, 5, 0:T], 0.5, None, ALU.is_gt))
            dve.wait_ge(next_edges, 1)
            at.link(TT(ix[:, 6, 0:T], ps[6][0:PR, 0:T], first, ALU.is_gt))
            TT(ix[:, 7, 0:T], ix[:, 5, 0:T], ix[:, 6, 0:T], ALU.mult).then_inc(unaligned, 1)
            at.link(TT(ix[:, 8, 0:T], ix[:, 4, 0:T], ix[:, 5, 0:T], ALU.add))
            dve.wait_ge(unaligned_sums, 1)
            at.add(v.memset(ix[:, 9, 0:T], 0.0))
            at.link(v.tensor_copy(ix[:, 11, 0:T], ps[5][0:PR, 16:16 + T]))
            at.link(v.tensor_tensor_scan(ix[:, 10, 0:T], ix[:, 11, 0:T], ix[:, 9, 0:T], 0.0, ALU.add, ALU.add))
            at.link(TT(ix[:, 10, 0:T], ix[:, 10, 0:T], ix[:, 11, 0:T], ALU.subtract))
            at.link(TT(ix[:, 10, 0:T], ix[:, 10, 0:T], ps[5][0:PR, 0:T], ALU.add))
            at.link(TT(ix[:, 8, 0:T], ix[:, 8, 0:T], ix[:, 10, 0:T], ALU.add))
            floor_div(ix[:, 12, 0:T], ix[:, 8, 0:T], 128, 0.498, 3)
            at.link(STT(ix[:, 13, 0:T], ix[:, 12, 0:T], -128.0, ix[:, 8, 0:T], ALU.mult, ALU.add))
            v.tensor_tensor(stepR, cols[0:PR, None, :].to_broadcast([PR, T, 128]),
                            ix[:, 13, 0:T, None].to_broadcast([PR, T, 128]), ALU.is_ge)
            TT(hitA[:, :, 0:QC], cols[0:PR, None, 0:QC].to_broadcast([PR, T, QC]),
               ix[:, 12, 0:T, None].to_broadcast([PR, T, QC]), ALU.is_equal)
            at.link(TT(hitB[:, :, 0:QC], cols[0:PR, None, 0:QC].to_broadcast([PR, T, QC]),
                       ix[:, 12, 0:T, None].to_broadcast([PR, T, QC]), ALU.is_gt))
            TT(hitA[:, :, QC:], hitA[:, :, 0:QC], ix[:, 7, 0:T, None].to_broadcast([PR, T, QC]), ALU.mult)
            TT(hitB[:, :, QC:], hitB[:, :, 0:QC], ix[:, 7, 0:T, None].to_broadcast([PR, T, QC]), ALU.mult).then_inc(hits, 1)
            at.link(TT(thr[:, :], ix[0:1, 12, 1:T], cols[0:1, 1:T], ALU.add))
            at.link(TT(slot_c, cols[0:1, 0:SLOTS, None].to_broadcast([1, SLOTS, T - 1]),
                       thr[:, None, :].to_broadcast([1, SLOTS, T - 1]), ALU.is_ge))
            at.link(RED(slot_t[:, :], slot_c, AXX, ALU.add))
            v.tensor_copy(slot_i[:, :], slot_t[:, :])
            dve.wait_ge(group_counts, 1)
            at.link(TT(uns[:, 0], gid[:, :], ps[4][:, QC:2 * QC], ALU.subtract))
            at.link(TS(uns[:, 1], uns[:, 0], BLOCKS - 0.5, None, ALU.is_lt))
            TS(bidx[:, 0:QC], uns[:, 0], float(BLOCKS - 1), None, ALU.min)
            at.link(TT(ngf[:, :], uns[:, 1], ps[4][:, 0:QC], ALU.mult))
            at.link(TS(ngf[:, :], ngf[:, :], -1.0, None, ALU.add))
            TS(nidx[:, :], ngf[:, :], 0.0, None, ALU.max).then_inc(index_ready, 1)

            copy_rows(0)
            dve.wait_ge(tab_stored, 16)
            normalise_rows(1)

            def next_rows(b):
                alone(dve, xT_stored, 16 * b + 16)
                alone(dve, hT_pe, b + 1)
                copy_rows(b + 1)

            with dve.Fori(0, NB - 2) as b:
                at.enter(b, 20)
                next_rows(b)
                normalise_rows(b + 2)
                tables(b)
            at.leave(NB - 2)
            next_rows(NB - 2)
            tables(NB - 2)
            tables(NB - 1)

            def score(q, e, uses):
                r = e % RING
                s = sc[:, r]
                dve.wait_ge(xl_here[r], 16 * (G + 1) * uses)
                at.add(TT(pen[:, r, :], TAB[:, bass.ds(q, 1), G:2 * G].rearrange("p a w -> p (a w)"), ngf[:, bass.ds(q, 1)].to_broadcast([128, G]), ALU.not_equal))
                at.link(TT(msg, XL[:, r, :, 0:HID], XR[:, r, None, 0:HID].to_broadcast([128, G, HID]), ALU.add))
                at.link(STT(msg, msg, 0.0, att8[:, None, :].to_broadcast([128, G, HID]), ALU.max, ALU.mult))
                at.link(RED(s, msg.rearrange("p j (h d) -> p j h d", h=H), AXX, ALU.add))
                at.link(TT(s, s, XL[:, r, :, HID:], ALU.add))
                at.link(TT(s, s, XR[:, r, None, HID:HID + H].to_broadcast([128, G, H]), ALU.add))
                at.link(STT(s, pen[:, r, :, None].to_broadcast([128, G, H]), -BIG, s, ALU.mult, ALU.add))
                at.link(RED(mx[:, :], s.rearrange("p j h -> p h j"), AXX, ALU.max))
                at.link(TT(MR[:, bass.ds(q, 1), :].rearrange("p a h -> p (a h)"), mx[:, :], XR[:, r, HID + H:], ALU.max))
                TT(s, s, MR[:, bass.ds(q, 1), :].to_broadcast([128, G, H]), ALU.subtract).then_inc(scores, 1)

            def message(q, e):
                r = e % RING
                x = XL[:, r, :, 0:HID]
                dve.wait_ge(exps, q + 1)
                at.add(RED(DN[:, bass.ds(q, 1), :].rearrange("p a h -> p (a h)"), sc[:, r].rearrange("p j h -> p h j"),
                            AXX, ALU.add))
                dve.wait_ge(mul_act, q + 1)
                at.link(TT(x[:, 0:5], x[:, 0:5], x[:, 5:10], ALU.add))
                TT(x[:, 0:2], x[:, 0:2], x[:, 2:4], ALU.add).then_inc(part_sums, 1)

            dve.wait_ge(edges_ready, 1)
            score(0, 0, 1)
            score(1, 1, 1)
            message(0, 0)
            with dve.Fori(0, NB) as b:
                at.enter(b, KD * 11 + 3)
                for e in range(KD):
                    u = KD * b + e
                    score(u + 2, e + 2, 2 * b + (e + 2) // RING + 1)
                    message(u + 1, e + 1)
                    if e == 0:
                        alone(dve, block_dve, 1 + b)
                    dve.wait_ge(sq_act, 1 + u + 1)
                    TT(KVb[:, e, :], ps[e % 2][:, 0:BR], vb[:, e % 2, :], ALU.mult).then_inc(kv_dve, 1)
                dve.wait_ge(norm_act, 1 + b + 1)
                at.link(TS(nrm[:, 0:BR], nrm[:, 0:BR], 1e-12, None, ALU.max))
                at.link(v.reciprocal(nrm[:, 0:BR], nrm[:, 0:BR]))
                for e in range(KD):
                    last = STT(KVb[:, e, :], KVb[:, e, :], 1.0, nrm[:, 0:BR], ALU.mult, ALU.mult, accum_out=gpart[:, e:e + 1])
                at.link(last)
                TT(gacc[:, :], gacc[:, :], gpart[:, :], ALU.add).then_inc(block_dve, 1)
            at.leave(NB)
            message(NB * KD + 1, 1)
            at.link(TS(gacc[:, :], gacc[:, :], 1.0 / N, None, ALU.mult))

            dve.wait_ge(lanes_here, 32)
            v.memset(PF[:, 0:1], -BIG)
            v.memset(PF[:, QC:], -BIG)
            v.tensor_copy(ends[:, 2, :], NL[:, 0:1].to_broadcast([128, H]))
            v.tensor_copy(ends[:, 3, :], NL[:, QC - 1:QC].to_broadcast([128, H]))
            TT(edge_pen[:, 0], NL, NL[:, 0:1].to_broadcast([128, QC]), ALU.is_equal)
            TT(edge_pen[:, 1], NL, NL[:, QC - 1:QC].to_broadcast([128, QC]), ALU.is_equal)
            at.link(TT(PF[:, 1:QC], NL[:, 1:QC], NL[:, 0:QC - 1], ALU.is_equal))
            TS(edge_pen, edge_pen, BIG, -BIG, ALU.mult, ALU.add)
            at.link(TS(PF[:, 1:QC], PF[:, 1:QC], BIG, -BIG, ALU.mult, ALU.add))
            for h in range(H):
                v.tensor_tensor_scan(FW[:, :, h], PF[:, 0:QC], ML[:, :, h], -BIG, ALU.add, ALU.max)
                last = v.tensor_tensor_scan(BW[:, ::-1, h], PF[:, 1:QC + 1][:, ::-1], ML[:, ::-1, h], -BIG, ALU.add, ALU.max)
            at.link(last)
            v.tensor_copy(ends[:, 0, :], FW[:, QC - 1, :])
            v.tensor_copy(ends[:, 1, :], BW[:, 0, :]).then_inc(ends_ready, 1)
            dve.wait_ge(ends_T, 1)
            eT = ps[3][0:H, :].rearrange("p (a l) -> p a l", a=4)
            joined, single, sf, sb_ = laneT[:, 0, :], laneT[:, 1, 0:128], laneT[:, 2, :], laneT[:, 3, :]
            lastN = laneT[:, 4, 0:128]
            v.memset(joined, -BIG)
            v.memset(sf[:, 0:1], -BIG)
            v.memset(sb_[:, 128:129], -BIG)
            at.link(v.tensor_copy(lastN, eT[:, 3]))
            TT(single, lastN, eT[:, 2], ALU.is_equal)
            at.link(TT(joined[:, 1:128], lastN[:, 0:127], eT[:, 2, 1:128], ALU.is_equal))
            TS(single, single, BIG, -BIG, ALU.mult, ALU.add)
            at.link(TS(joined[:, 1:128], joined[:, 1:128], BIG, -BIG, ALU.mult, ALU.add))
            TT(laneT[:, 5, 0:128], single, joined[:, 1:129], ALU.add)
            at.link(TT(lastN, single, joined[:, 0:128], ALU.add))
            v.tensor_tensor_scan(sf[:, 1:129], lastN, eT[:, 0], -BIG, ALU.add, ALU.max)
            at.link(v.tensor_tensor_scan(sb_[:, 0:128][:, ::-1], laneT[:, 5, 0:128][:, ::-1], eT[:, 1, ::-1], -BIG, ALU.add, ALU.max))
            TT(lastN, sf[:, 0:128], joined[:, 0:128], ALU.add)
            TT(laneT[:, 5, 0:128], sb_[:, 1:129], joined[:, 1:129], ALU.add).then_inc(carry_ready, 1)
            dve.wait_ge(carry_back, 1)
            at.link(v.tensor_copy(carry.rearrange("p a h -> p (a h)"), ps[4][:, 0:3 * H]))
            wide = lambda ap: ap.to_broadcast([128, QC, H])
            at.link(TT(FW, FW, BW, ALU.max))
            for d in range(2):
                at.link(TT(BW, wide(edge_pen[:, d, :, None]), wide(carry[:, None, d, :]), ALU.add))
                at.link(TT(FW, FW, BW, ALU.max))
            TT(FL[:, :, 0:H], ML, FW, ALU.subtract).then_inc(shift_ready, 1)
            at.link(v.tensor_copy(PF[:, 0:1], carry[:, 2, 0:1]))
            at.link(TS(FL[:, :, 2 * H:], PF[:, 0:QC, None], -0.5, None, ALU.is_lt))
            TT(FL[:, :, H:2 * H], FW, wide(FL[:, :, 2 * H:]), ALU.mult)
            dve.wait_ge(factor_act, 1)
            v.memset(edge_pen[:, 0, 0:1], 0.0).then_inc(factors_ready, 1)
            dve.wait_ge(factors_here, 16)
            dve.wait_ge(o_here, 16 * 4)
            r4 = RH[:, :, 0:HID].rearrange("p q (h d) -> p q h d", h=H)
            TT(RH[:, :, HID:HID + H], DN[:, :, :], FG[:, :, 0:H], ALU.mult)
            v.tensor_copy(RH[:, :, HID + H:], FG[:, :, H:])

            def scale_sums(q, n):
                w = bass.ds(q, n)
                TT(r4[:, w], r4[:, w], FG[:, w, 0:H, None].to_broadcast([128, n, H, DH]), ALU.mult).then_inc(rh_ready, 1)

            def add_slots(i, ahead):
                if ahead:
                    scale_sums(3 * i + 6, 3)
                for k in range(3):
                    s = 3 * i + k
                    t0 = dve.value_load(slot_i[0:1, bass.ds(s, 1)], min_val=0, max_val=T - 1)
                    at_t = acc[:, bass.ds(t0, 1), :].rearrange("p a w -> p (a w)")
                    alone(dve, slot_dve, 3 + s)
                    dve.wait_ge(slot_pe, 3 + s + 1)
                    TT(at_t, at_t, ps[k][0:PR, 0:SUMW], ALU.add).then_inc(slot_dve, 1)

            scale_sums(0, 6)
            dve.wait_ge(acc_zero, 1)
            with dve.Fori(0, QC // 3 - 2) as i:
                add_slots(i, True)
            with dve.Fori(QC // 3 - 2, SLOTS // 3) as i:
                add_slots(i, False)
            dve.wait_ge(slot_dve, 3 + SLOTS)
            has = acc[:, :, SUMW - 1:SUMW]
            wide = lambda ap: ap.to_broadcast([PR, T, H])
            at.link(TS(es[:, 1, :, 0:1], has, -1.0, 1.0, ALU.mult, ALU.add))
            at.link(TT(es[:, 0], esel[:, :, :], wide(es[:, 1, :, 0:1]), ALU.mult))
            at.link(TT(es[:, 1], es[:, 0], acc[:, :, HID + H:HID + 2 * H], ALU.add))
            TT(es[:, 0], esel[:, :, :], es[:, 1], ALU.subtract).then_inc(self_ready, 1)
            dve.wait_ge(self_act, 1)
            dve.wait_ge(xl2_here, 16)
            x4 = XL2[:, :, 0:HID].rearrange("p t (h d) -> p t h d", h=H)
            a4 = acc[:, :, 0:HID].rearrange("p t (h d) -> p t h d", h=H)
            per_head = lambda ap: ap[:, :, :, None].to_broadcast([PR, T, H, DH])
            TT(es[:, 1], es[:, 0], acc[:, :, HID:HID + H], ALU.add)
            at.link(TT(x4, x4, per_head(es[:, 0]), ALU.mult))
            at.link(TS(es[:, 1], es[:, 1], 1e-16, None, ALU.add))
            at.link(v.reciprocal(es[:, 0], es[:, 1]))
            at.link(TT(a4, a4, x4, ALU.add))
            for b in range(NB):
                two = slice(2 * b, 2 * b + 2)
                TT(a4[:, two], a4[:, two], es[:, 0, two, :, None].to_broadcast([PR, 2, H, DH]), ALU.mult).then_inc(gnn_ready, 1)
            for b in range(NB):
                dve.wait_ge(gT_pe, b + 1)
                v.tensor_copy(gT[:, :, b * BR:b * BR + BR], ps[3 + b % 2][:, 0:2 * BR].rearrange("p (k r) -> p k r", k=2)).then_inc(gT_dve, 1)

            dve.wait_ge(ff_small, 16 * 8)
            TT(gwd[:, :], gw[:, :, 1], gw[:, :, 0], ALU.subtract)
            at.link(TT(b2s[:, 0], b2s[:, 0], b2s[:, 1], ALU.add))
            at.link(TT(b2s[:, 0], b2s[:, 0], b2s[:, 2], ALU.add))

            def normalise_q(b, half):
                if half == 0:
                    alone(dve, q_here, 16 * (b + 1))
                    at.link(TS(q_norm, q_norm, 1e-12, None, ALU.max))
                    at.link(v.reciprocal(q_norm, q_norm))
                q = qT[:, 4 * half:4 * half + 4]
                at.link(TT(q, q, q_norm[:, None, :].to_broadcast([128, 4, BR]), ALU.mult))

            def residual(b, odd, e):
                dve.wait_ge(x1_pe, KD * b + e + 1)
                STT(x1T[odd][:, e], qT[:, e], gacc[:, e:e + 1], ps[3 + e % 2][:, 0:BR], ALU.mult, ALU.add).then_inc(x1_dve, 1)

            def add_slices(s):
                at.link(TT(part, s[:, 0:4], s[:, 4:8], ALU.add))
                at.link(TT(part[:, 0:2], part[:, 0:2], part[:, 2:4], ALU.add))
                TT(part[:, 0], part[:, 0], part[:, 1], ALU.add).then_inc(slices_dve, 1)

            def centre(b, odd):
                dve.wait_ge(x1_dve, KD * b + KD)
                add_slices(x1T[odd])
                dve.wait_ge(mean_pe, b + 1)
                TT(x2T[odd], x1T[odd], ps[5][:, None, 0:BR].to_broadcast([128, KD, BR]), ALU.subtract).then_inc(cen_dve, 1)

            def sum_squares(b):
                dve.wait_ge(sqr_act, b + 1)
                add_slices(sqT)

            def normalise(b, odd):
                dve.wait_ge(dev_act, b + 1)
                at.link(v.reciprocal(nrm[:, 0:BR], nrm[:, 0:BR]))
                TT(x2T[odd], x2T[odd], nrm[:, None, 0:BR].to_broadcast([128, KD, BR]), ALU.mult).then_inc(x2_dve, 1)

            def gate_sums(b, odd):
                dve.wait_ge(x2_dve, b + 1)
                at.link(TS(part[:, 0], x2T[odd][:, 0], gwd[:, 0:1], None, ALU.mult))
                for k in range(1, KD):
                    ins = STT(part[:, 0], x2T[odd][:, k], gwd[:, k:k + 1], part[:, 0], ALU.mult, ALU.add)
                    if k < KD - 1:
                        at.link(ins)
                ins.then_inc(slices_dve, 1)

            def masks(b, hidden):
                if hidden is not None:
                    alone(dve, h_dve, hidden)
                dve.wait_ge(gate_pe, b + 1)
                TS(msk[:, 0, :], ps[5][:, 0:BR], 0.0, None, ALU.is_le)
                TS(msk[:, 1, :], ps[5][:, 0:BR], 0.0, None, ALU.is_gt).then_inc(mask_dve, 1)

            def feed_forward(b, odd, more):
                alone(dve, mask_dve, b + 1)
                for j in range(8):
                    if more and j % 4 == 0:
                        normalise_q(b + 1, j // 4)
                    dve.wait_ge(h_pe, 12 * b + j + 1)
                    TT(hT[:, j], ps[j % 2][:, 0:BR], msk[:, j // 4, :], ALU.mult).then_inc(h_dve, 1)
                    if more:
                        residual(b + 1, 1 - odd, j)
                if more:
                    centre(b + 1, 1 - odd)
                    sum_squares(b + 1)
                for e in range(KD):
                    dve.wait_ge(y_pe, KD * b + e + 1)
                    STT(x1T[odd][:, e], ps[e % 2][:, 0:BR], b2s[:, 0, e:e + 1], x1T[odd][:, e], ALU.add, ALU.add).then_inc(y_dve, 1)
                    if more and e == 0:
                        normalise(b + 1, 1 - odd)
                    if more and e == 1:
                        gate_sums(b + 1, 1 - odd)
                    if more and e == 3:
                        masks(b + 1, 8 * b + 8)
                for h in range(2):
                    alone(dve, out_stored[h], 1 + 16 * b)
                    dve.wait_ge(yT_pe, 4 * b + 2 * h + 2)
                    v.tensor_copy(yrow[h][:, 1, :], ps[7][0:PR, :]).then_inc(yr_dve, 1)

            normalise_q(0, 0)
            normalise_q(0, 1)
            for e in range(KD):
                residual(0, 0, e)
            centre(0, 0)
            sum_squares(0)
            normalise(0, 0)
            gate_sums(0, 0)
            masks(0, None)
            with dve.Fori(0, NB // 2) as i:
                at.enter(i, 2 * 16)
                for odd in range(2):
                    feed_forward(2 * i + odd, odd, True)
            at.leave(NB // 2)
            feed_forward(NB - 1, 0, False)

        @block.tensor
        def _(pe):
            for s in (kvq_pe, lr_pe, slot_pe, slot_pe, slot_pe, *([sums] * RING)):
                pe.sem_inc(s)
            mm = nc.tensor.matmul

            def chain(out_ap, pairs, start=True, stop=True):
                for n, (l, r) in enumerate(pairs):
                    last = mm(out_ap, l, r, start=start and n == 0, stop=stop and n == len(pairs) - 1)
                return last

            pe.wait_ge(dv, 1)
            pe.wait_ge(heads_f, 1)
            mm(ps[7][:, 0:ROWS], ones[0:1, :], heads[0:1], start=True, stop=True).then_inc(heads_bc, 1)
            def transpose_row(k, src):
                for c in range(KD):
                    last = nc.tensor.transpose(ps[2 * k + c // 4][:, (c % 4) * 128:(c % 4) * 128 + 128],
                                               src[:, k, c * 128:c * 128 + 128], ident[:, :])
                last.then_inc(w_pe, 1)

            def transpose_half(b, c):
                k, h = c // 2, c % 2
                if h == 0:
                    alone(pe, w_ld[k], 16 * (KD // 2 + b + 1))
                alone(pe, half_act, 1 + 4 * b + c)
                for n in range(4):
                    last = nc.tensor.transpose(ps[7][:, n * 128:n * 128 + 128],
                                               raw[:, k, (4 * h + n) * 128:(4 * h + n) * 128 + 128], ident[:, :])
                last.then_inc(half_pe, 1)

            def transpose_rows(b, first=False):
                for k in range(2):
                    for h in range(2):
                        if h == 0:
                            pe.wait_ge(xn_ready, 2 * b + k + 1)
                            if not first:
                                alone(pe, xT_act, 2 * b)
                                alone(pe, xT_dve, 2 * b)
                        for c in range(4):
                            last = nc.tensor.transpose(ps[2 * k + h][:, c * PR:c * PR + PR],
                                                       wraw[0:PR, k, (4 * h + c) * 128:(4 * h + c) * 128 + 128], ident[0:PR, 0:PR])
                        last.then_inc(xT_pe, 1)

            def hidden(b, h):
                if h == 0:
                    alone(pe, xT_act, 2 * b + 2)
                    alone(pe, xT_dve, 2 * b + 2)
                    alone(pe, hT_act, 1 + b)
                last = chain(ps[4][:, h * BR:h * BR + BR], [(wd[:, k, h * 128:h * 128 + 128], xnTb[:, k, :]) for k in range(KD)])
                if h == 1:
                    last.then_inc(hT_pe, 1)

            def left_right(b):
                alone(pe, hT_act, 1 + b + 1)
                alone(pe, lr_act, 1 + 2 * b)
                for k in range(2):
                    hb = [hTb[:, c, k * PR:k * PR + PR] for c in range(2)]
                    chain(ps[5 + k][0:PR, 0:HID], [(hb[c], wl[:, c, :]) for c in range(2)])
                    chain(ps[5 + k][0:PR, HID:], [(hb[c], wr[:, c, :]) for c in range(2)]).then_inc(lr_pe, 1)

            with pe.Fori(0, KD // 2) as i:
                for k in range(2):
                    alone(pe, w_ld[k], 16 * (i + 1))
                    alone(pe, w_act, 1 + 2 * i)
                    transpose_row(k, raw)
            pe.wait_ge(w_act, 1 + KD)
            transpose_rows(0, first=True)

            pe.wait_ge(first_edges, 1)
            chain(ps[6][0:PR, 0:T], [(shiftA, ix[:, 2, 0:T]), (shiftB, ix[:, 2, 1:T + 1])]).then_inc(next_edges, 1)
            pe.wait_ge(unaligned, 1)
            mm(ps[5][0:PR, 0:T], before, ix[:, 7, 0:T], start=True, stop=True)
            mm(ps[5][0:PR, 16:16 + T], ones[0:PR, 0:PR], ix[:, 7, 0:T], start=True, stop=True).then_inc(unaligned_sums, 1)
            pe.wait_ge(hits, 1)
            chain(ps[4][:, 0:2 * QC], [p for t in range(T) for p in
                  ((stepR[:, t, :], hitA[:, t, :]), (onesb[:, :], hitB[:, t, :]))]).then_inc(group_counts, 1)

            pe.wait_ge(wd_ready, 1)
            pe.wait_ge(index_ready, 1)
            with pe.Fori(0, NB - 1) as b:
                hidden(b, 0)
                transpose_half(b, 0)
                hidden(b, 1)
                transpose_half(b, 1)
                transpose_rows(b + 1)
                transpose_half(b, 2)
                left_right(b)
                transpose_half(b, 3)
            hidden(NB - 1, 0)
            hidden(NB - 1, 1)
            left_right(NB - 1)

            with pe.Fori(0, KD // 2) as i:
                for k in range(2):
                    alone(pe, wv_ld[k], 16 * (i + 1))
                    alone(pe, w_act, 1 + KD + 2 * i + k - 1)
                    transpose_row(k, wraw)

            pe.wait_ge(w_act, 1 + 2 * KD)
            pe.wait_ge(half_act, 1 + 2 * KD)

            def sum_messages(q, e):
                alone(pe, o_ready, 2 + q - 1)
                alone(pe, part_sums, q + 1)
                chain(ps[5 + e % 2][:, 0:HID], [(ident[:, :], XL[:, e % RING, j, 0:HID]) for j in (0, 1, 4)]).then_inc(sums, 1)

            with pe.Fori(0, NB) as b:
                alone(pe, xb_here, 16 * (b + 1))
                for e in range(KD):
                    k = e % 2
                    freed = KD * b + (0 if e < 2 else e - 1)
                    alone(pe, sq_act, 1 + freed)
                    alone(pe, kv_dve, 1 + freed)
                    for w, to in ((0, ps[k][:, 0:BR]), (1, ps[k][:, BR:2 * BR]), (2, ps[2 + k][:, 0:BR])):
                        last = chain(to, [(wt[:, w, c, e * 128:e * 128 + 128], XB[:, c, :]) for c in range(KD)])
                        if w == 0:
                            sum_messages(KD * b + e, e)
                    last.then_inc(kvq_pe, 1)
                    for s in ([e - 1] if e else []) + ([e] if e == KD - 1 else []):
                        alone(pe, sq_act, 1 + KD * b + s + 1)
                        if s == 0:
                            alone(pe, norm_act, 1 + b)
                        last = mm(ps[4][:, 0:2 * BR], ones[:, :], sq[:, s % 2, :], start=s == 0, stop=s == KD - 1)
                        last.then_inc(sq_pe, 1)

            sum_messages(NB * KD, 0)
            sum_messages(NB * KD + 1, 1)

            pe.wait_ge(norm_act, 1 + NB)
            pe.wait_ge(ends_ready, 1)
            for i in range(4):
                last = nc.tensor.transpose(ps[3][0:H, i * 128:i * 128 + 128], ends[:, i, :], ident[:, :])
            last.then_inc(ends_T, 1)
            pe.wait_ge(carry_ready, 1)
            for i, a in enumerate((4, 5, 0)):
                last = nc.tensor.transpose(ps[4][:, i * H:i * H + H], laneT[:, a, 0:128], ident[0:H, 0:H])
            last.then_inc(carry_back, 1)
            def slots(i, scaled):
                alone(pe, rh_ready, scaled)
                for k in range(3):
                    s = 3 * i + k
                    t0 = pe.value_load(slot_i[0:1, bass.ds(s, 1)], min_val=0, max_val=T - 1)
                    alone(pe, slot_dve, 3 + s - 2)
                    alone(pe, hot_ready, s + 1)
                    mm(ps[k][0:PR, 0:SUMW], hot[:, k, :], RH[:, bass.ds(chunk_of(s, t0), 1), :].rearrange("p a w -> p (a w)"), start=True, stop=True).then_inc(slot_pe, 1)

            with pe.Fori(0, QC // 3 - 2) as i:
                slots(i, i + 1)
            with pe.Fori(QC // 3 - 2, SLOTS // 3) as i:
                slots(i, QC // 3 - 1)
            for b in range(NB):
                pe.wait_ge(gnn_ready, b + 1)
                if b >= 2:
                    pe.wait_ge(gT_dve, b - 1)
                for h in range(2):
                    for k in range(2):
                        last = nc.tensor.transpose(ps[3 + b % 2][:, h * BR + k * PR:h * BR + k * PR + PR],
                                                   acc[:, 2 * b + k, h * 128:h * 128 + 128], ident[0:PR, 0:PR])
                last.then_inc(gT_pe, 1)

            pe.wait_ge(gT_dve, NB)
            pe.wait_ge(ff_w, 16 * 7)

            def residual(b, e, first=False):
                if e >= 2 or not first:
                    alone(pe, x1_dve, KD * b + e - 1)
                to = ps[3 + e % 2]
                cut = slice(e * 128, e * 128 + 128)
                mm(to[:, 0:PR], xrow[:, 0, cut], ident[0:PR, 0:PR], start=True, stop=False)
                mm(to[:, PR:BR], xrow[:, 1, cut], ident[0:PR, 0:PR], start=False, stop=False)
                chain(to[:, 0:BR], [(wraw[:, k, cut], gT[:, k, bass.ds(b * BR, BR)]) for k in range(2)], start=False).then_inc(x1_pe, 1)

            def over_lanes(step, to, weights, done):
                alone(pe, slices_dve, step)
                mm(to[:, 0:BR], weights[:, :], part[:, 0], start=True, stop=True).then_inc(done, 1)

            mean = lambda b: over_lanes(3 * b + 1, ps[5], avg, mean_pe)
            variance = lambda b: over_lanes(3 * b + 2, ps[2], avg, var_pe)
            gate = lambda b: over_lanes(3 * b + 3, ps[5], ones, gate_pe)

            def feed_forward(b, odd, more):
                alone(pe, x2_dve, b + 1)
                alone(pe, y_dve, 1 + KD * b)
                for j in range(12):
                    x, c = j // 4, (j % 4) * 128
                    if 2 <= j < 10:
                        alone(pe, h_dve, 8 * b + j - 1)
                    elif j >= 10:
                        alone(pe, h_act, 12 * b + j - 1)
                    chain(ps[j % 2][:, 0:BR], [(w1s[:, x, k, c:c + 128], x2T[odd][:, k]) for k in range(KD)]).then_inc(h_pe, 1)
                    if more and j < KD:
                        if j == 0:
                            alone(pe, xrow_here, 16 * (b + 2))
                        residual(b + 1, j)
                    if more and j == 9:
                        mean(b + 1)
                for e in range(KD):
                    if e < 2:
                        alone(pe, h_act, 12 * b + 11 + e)
                    else:
                        alone(pe, y_dve, 1 + KD * b + e - 1)
                    steps = [(w2s[:, j // 4, j % 4, e * 128:e * 128 + 128], hT[:, j]) for j in range(12)]
                    if e == 0:
                        chain(ps[0][:, 0:BR], steps[:11], stop=False)
                        alone(pe, h_act, 12 * b + 12)
                        chain(ps[0][:, 0:BR], steps[11:], start=False).then_inc(y_pe, 1)
                    else:
                        chain(ps[e % 2][:, 0:BR], steps).then_inc(y_pe, 1)
                    if more and e == 0:
                        variance(b + 1)
                    if more and e == 3:
                        gate(b + 1)
                for h in range(2):
                    alone(pe, y_dve, 1 + KD * b + 4 * h + 4)
                    for k, copied in enumerate((yr_act, yr_dve)):
                        alone(pe, copied, 1 + 2 * b + h)
                        for c in range(4):
                            last = nc.tensor.transpose(ps[6 + k][0:PR, c * 128:c * 128 + 128],
                                                       x1T[odd][:, 4 * h + c, k * PR:k * PR + PR], ident[:, :])
                        last.then_inc(yT_pe, 1)

            pe.wait_ge(xrow_here, 16)
            for e in range(KD):
                residual(0, e, first=True)
            mean(0)
            variance(0)
            gate(0)
            with pe.Fori(0, NB // 2) as i:
                for odd in range(2):
                    feed_forward(2 * i + odd, odd, True)
            feed_forward(NB - 1, 0, False)


_INS = ["x", "src", "dst", "L0_gnn_rms_w", "L0_gnn_W_down", "L0_gnn_Wl", "L0_gnn_Wr", "L0_gnn_att", "L0_gnn_W_up",
        "L0_mix_W_q", "L0_mix_W_k", "L0_mix_W_v", "L0_ffn_gate_w", "L0_ffn_w1", "L0_ffn_b1", "L0_ffn_w2",
        "L0_ffn_b2", "L0_ffn_sw1", "L0_ffn_sb1", "L0_ffn_sw2", "L0_ffn_sb2"]


def kernel(**inputs):
    import numpy as _np
    import concourse.bacc as _bacc
    from concourse import mybir as _mybir
    from concourse.bass_utils import run_bass_kernel_spmd as _run

    nc = _bacc.Bacc("TRN2", target_bir_lowering=False, num_devices=1)
    arrays, args = {}, []
    for name in _INS:
        a = _np.ascontiguousarray(inputs[name])
        arrays[f"in_{name}_dram"] = a
        args.append(nc.dram_tensor(f"in_{name}_dram", a.shape, _mybir.dt.from_np(a.dtype), kind="ExternalInput").ap())
    args.append(nc.dram_tensor("out_0_dram", (1250, 1024), _mybir.dt.float32, kind="ExternalOutput").ap())
    gps_layer(nc, *args)
    r = _run(nc, [arrays], core_ids=[0])
    return r.results[0]["out_0_dram"]
```
